# Optimizing a Trainium2 kernel written in Bass

```python
import numpy as np
import jax
import jax.numpy as jnp

def _softmax(x, axis=-1):
    return jax.nn.softmax(x, axis=axis)

def _gelu(x):
    return jax.nn.gelu(x, approximate=True)

def _silu(x):
    return jax.nn.silu(x)

def _sigmoid(x):
    return jax.nn.sigmoid(x)

def _layernorm(x, axis=-1, eps=1e-05):
    m = jnp.mean(x, axis=axis, keepdims=True)
    v = jnp.var(x, axis=axis, keepdims=True)
    return (x - m) / jnp.sqrt(v + eps)

def _scatter_add(tgt, idx, src, axis=0):
    return tgt.at[idx].add(src)

def _segment_sum(src, seg, n):
    return jax.ops.segment_sum(src, seg, n)
kernel_name = 'mk_gnn_preln_d2_gnn_r8_2670fd'

def setup_inputs(seed: int=0):
    np.random.seed(seed)
    _w = jnp.asarray

    def _rec_inputs():
        import jax
        import jax.numpy as jnp
        _gk = jax.random.key(seed)
        x = -0.0005121 + 1.001 * jax.random.normal(jax.random.fold_in(_gk, 1), (12500, 32), jnp.float32)
        src = jax.random.randint(jax.random.fold_in(_gk, 2), (400000,), 0, 12500, jnp.int32)
        dst = jax.random.randint(jax.random.fold_in(_gk, 3), (400000,), 0, 12500, jnp.int32)
        _o = jnp.argsort(dst, stable=True)
        src = src[_o]
        dst = dst[_o]
        edge_type_86 = jax.random.randint(jax.random.fold_in(_gk, 13), (400000,), 0, 86, jnp.int32)
        edge_weight = jax.random.uniform(jax.random.fold_in(_gk, 14), (400000,), jnp.float32, 0.0, 1)
        return (x, src, dst, edge_type_86, edge_weight)
    x, src, dst, edge_type_86, edge_weight = _rec_inputs()

    def _L0_gnn_setup():
        import jax, jax.numpy as jnp
        import numpy as np
        N_NODES = 12500
        N_EDGES = 200000
        N_FEAT = 32
        key = jax.random.key(seed)
        k1, k2, k3, k4 = jax.random.split(key, 4)
        u = jax.random.normal(k1, (N_NODES, N_FEAT), dtype=jnp.float32)
        weights = jax.random.uniform(k2, (N_EDGES,), dtype=jnp.float32)
        row = jax.random.randint(k3, (N_EDGES,), 0, N_NODES)
        col = jax.random.randint(k4, (N_EDGES,), 0, N_NODES)
        edge_index = jnp.stack([row, col]).astype(jnp.int64)
        return {'u': u, 'weights': weights, 'edge_index': edge_index}
    _L0_gnn_all = _L0_gnn_setup()
    _L0_gnn_in = {k: v for k, v in _L0_gnn_all.items() if k in ()}
    del _L0_gnn_all

    def _L1_gnn_setup():
        import jax, jax.numpy as jnp
        import numpy as np
        N_NODES = 6250
        N_EDGES = 100000
        INP_DIM = 32
        OUT_DIM = 32
        ATTN_DIM = 32
        NUM_RELS = 86
        NUM_BASES = 16
        GAMMA = 0.0
        key = jax.random.key(seed)
        ks = jax.random.split(key, 12)
        return {'h': jax.random.normal(ks[0], (N_NODES, INP_DIM), jnp.float32), 'weight': jax.random.normal(ks[1], (NUM_BASES, INP_DIM, OUT_DIM), jnp.float32), 'w_comp': jax.random.normal(ks[2], (NUM_RELS, NUM_BASES), jnp.float32), 'self_loop_weight': jax.random.normal(ks[3], (INP_DIM, OUT_DIM), jnp.float32), 'A1_w': jax.random.normal(ks[4], (ATTN_DIM, INP_DIM), jnp.float32), 'A1_b': jax.random.normal(ks[5], (ATTN_DIM,), jnp.float32), 'A2_w': jax.random.normal(ks[6], (ATTN_DIM, INP_DIM), jnp.float32), 'A2_b': jax.random.normal(ks[7], (ATTN_DIM,), jnp.float32), 'rel_emb': jax.random.normal(ks[8], (NUM_RELS, ATTN_DIM), jnp.float32), 'src': jax.random.randint(ks[9], (N_EDGES,), 0, N_NODES, jnp.int32), 'dst': jax.random.randint(ks[10], (N_EDGES,), 0, N_NODES, jnp.int32), 'etype': jax.random.randint(ks[11], (N_EDGES,), 0, NUM_RELS, jnp.int32)}
    _L1_gnn_all = _L1_gnn_setup()
    _L1_gnn_in = {k: v for k, v in _L1_gnn_all.items() if k in ('weight', 'w_comp', 'self_loop_weight', 'A1_w', 'A1_b', 'A2_w', 'A2_b', 'rel_emb')}
    del _L1_gnn_all
    return {'x': x, 'src': src, 'dst': dst, 'edge_type_86': edge_type_86, 'edge_weight': edge_weight, 'L1_gnn_weight': _L1_gnn_in['weight'], 'L1_gnn_w_comp': _L1_gnn_in['w_comp'], 'L1_gnn_self_loop_weight': _L1_gnn_in['self_loop_weight'], 'L1_gnn_A1_w': _L1_gnn_in['A1_w'], 'L1_gnn_A1_b': _L1_gnn_in['A1_b'], 'L1_gnn_A2_w': _L1_gnn_in['A2_w'], 'L1_gnn_A2_b': _L1_gnn_in['A2_b'], 'L1_gnn_rel_emb': _L1_gnn_in['rel_emb']}

def reference(x, src, dst, edge_type_86, edge_weight, L1_gnn_weight, L1_gnn_w_comp, L1_gnn_self_loop_weight, L1_gnn_A1_w, L1_gnn_A1_b, L1_gnn_A2_w, L1_gnn_A2_b, L1_gnn_rel_emb):
    import jax
    import jax.numpy as jnp

    def _L0_gnn_ref(u, weights, edge_index):
        import jax, jax.numpy as jnp
        import numpy as np
        N_NODES = 12500
        N_EDGES = 200000
        N_FEAT = 32
        row, col = (edge_index[0], edge_index[1])
        diff = u[col] - u[row]
        weighted_diff = weights[:, None] * diff
        laplacian = jax.ops.segment_sum(weighted_diff, row, num_segments=u.shape[0])
        return laplacian

    def _L1_gnn_ref(h, weight, w_comp, self_loop_weight, A1_w, A1_b, A2_w, A2_b, rel_emb, src, dst, etype):
        import jax, jax.numpy as jnp
        import numpy as np
        N_NODES = 6250
        N_EDGES = 100000
        INP_DIM = 32
        OUT_DIM = 32
        ATTN_DIM = 32
        NUM_RELS = 86
        NUM_BASES = 16
        GAMMA = 0.0
        E = src.shape[0]
        N = h.shape[0]
        x = h[src]
        y = h[dst]
        c = w_comp[etype]
        xb = jnp.einsum('ei,bio->ebo', x, weight)
        msg = jnp.einsum('eb,ebo->eo', c, xb)
        x_hat = x @ A1_w.T + A1_b
        y_hat = y @ A2_w.T + A2_b + rel_emb[etype]
        scale = jnp.sqrt(jnp.asarray(INP_DIM, h.dtype))
        a = jnp.tanh(jax.nn.relu(jnp.sum(x_hat * y_hat, axis=-1) / scale))
        a = jnp.where(a > GAMMA, a, jnp.zeros_like(a))
        nei = jax.ops.segment_sum(a[:, None] * msg, dst, num_segments=N)
        last_e = jax.ops.segment_max(jnp.arange(E, dtype=jnp.int32), dst, num_segments=N)
        last_e = jnp.clip(last_e, 0, E - 1)
        curr = h[src[last_e]] @ self_loop_weight
        in_deg = jax.ops.segment_sum(jnp.ones((E,), h.dtype), dst, num_segments=N)
        h_new = jnp.where((in_deg > 0)[:, None], nei + curr, jnp.zeros_like(nei))
        return jax.nn.relu(h_new)
    edge_index = jnp.stack([src, dst])
    h = jnp.maximum(_layernorm(x, axis=-1), 0.0)
    x = x + _L0_gnn_ref(h, edge_weight, edge_index)
    h = jnp.maximum(_layernorm(x, axis=-1), 0.0)
    x = x + _L1_gnn_ref(h, L1_gnn_weight, L1_gnn_w_comp, L1_gnn_self_loop_weight, L1_gnn_A1_w, L1_gnn_A1_b, L1_gnn_A2_w, L1_gnn_A2_b, L1_gnn_rel_emb, src, dst, edge_type_86)
    return x

_drawn_inputs = setup_inputs


def setup_inputs(seed=0):
    import zlib

    import numpy as np

    out = dict(_drawn_inputs(seed))
    spreads = {}
    factors = {}
    for name, (base, spread) in spreads.items():
        noise = np.random.default_rng([zlib.crc32(name.encode()), seed]).standard_normal(out[name].shape)
        drawn = base * np.exp(spread * noise) if base else spread * noise
        out[name] = jnp.asarray(drawn.astype(out[name].dtype))
    for name, factor in factors.items():
        out[name] = (out[name] * factor).astype(out[name].dtype)
    return out
```

```python
from contextlib import ExitStack

import concourse.bass as bass
from concourse import mybir

ALU = mybir.AluOpType
ACT = mybir.ActivationFunctionType
AX_X = mybir.AxisListType.X
F32 = mybir.dt.float32
I32 = mybir.dt.int32
U32 = mybir.dt.uint32

P = 128
TS = 25
GT = 5
NG = TS // GT
SE = TS * P
EPS = 1e-5
ONE = 1
FIRST = 16


class Steps:

    def __init__(self, eng, sem, turn=None, per_turn=0, start=0):
        self.eng, self.sem, self.turn, self.per_turn, self.start, self.n = eng, sem, turn, per_turn, start, 0

    def value(self):
        v = self.start + self.n
        return v if self.turn is None else self.turn * self.per_turn + v

    def done(self, ins):
        ins.then_inc(self.sem, 1)
        self.n += 1
        self.eng.wait_ge(self.sem, self.value())


def gnn_kernel(nc, x, src, dst, edge_type_86, edge_weight, L1_gnn_weight, L1_gnn_w_comp,
               L1_gnn_self_loop_weight, L1_gnn_A1_w, L1_gnn_A1_b, L1_gnn_A2_w, L1_gnn_A2_b,
               L1_gnn_rel_emb, out):
    N, F = x.shape
    E = src.shape[0]
    R, B = L1_gnn_w_comp.shape
    S = E // SE
    J = -(-N // P)
    NP = J * P
    NT = NP + P
    M1 = F + 1
    H = R // 2
    TR = 2 * M1 + F
    RC = 14
    CHUNKS = [(r, min(RC, R - r)) for r in range(0, R, RC)]
    assert S * SE == E and F == 32 and R <= P and 2 * H == R and RC % 2 == 0 and RC * M1 <= 512 and J % 2 == 0 and J % 7 == 0
    tail = N - (P - 1) * J
    SPLIT = ((0, 112), (112, 127))

    h0_dram = nc.dram_tensor("h0", (NT, F), F32).ap()
    yh_dram = nc.dram_tensor("yh", (NT, F), F32).ap()
    self_dram = nc.dram_tensor("self_rows", (NP, F), F32).ap()
    table = nc.dram_tensor("relation_table", (NP * H, TR), F32).ap()
    lap_sums = [nc.dram_tensor(f"lap_sums{c}", (NT, F + 1), F32).ap() for c in range(GT)]
    nei_sums = [nc.dram_tensor(f"nei_sums{c}", (NT, F), F32).ap() for c in range(GT)]
    last_rows = [nc.dram_tensor(f"last_rows{c}", (NT, 2), F32).ap() for c in range(GT)]

    src_rows = src.rearrange("(t p) -> t p", p=P)
    dst_rows = dst.rearrange("(t p) -> t p", p=P)
    et_rows = edge_type_86.rearrange("(t p) -> t p", p=P)
    w_rows = edge_weight.rearrange("(t p) -> t p", p=P)

    with ExitStack() as ctx:
        def sb(name, shape, dt=F32):
            return ctx.enter_context(nc.sbuf_tensor(name, shape, dt))

        def sem(name):
            return ctx.enter_context(nc.semaphore(name))

        banks = [ctx.enter_context(nc.psum_tensor(f"bank{b}", [P, 512], F32)) for b in range(8)]
        cols_ps, sum_ps = banks[0], banks[1:3]
        row_ps = [b[:, 0:P] for b in banks[3:5]]
        chunk_ps = banks[0:len(CHUNKS)]
        turn_ps, node_ps = banks[6], banks[7]
        A_CHUNKS, V_CHUNKS = (len(CHUNKS) + 1) // 2, len(CHUNKS) // 2

        ident = sb("ident", [P, P])
        tri = sb("tri", [P, P])
        rowsel = sb("rowsel", [P, TS, P])
        trash = sb("trash", [P, 1])
        part = sb("part", [P, 1])
        zeros = sb("zeros", [P, 99 * 33])
        xn = sb("xn", [P, J, F])
        hn = sb("hn", [P, J, F])
        sq = sb("sq", [P, J, F])
        stat = sb("stat", [P, 4, J])
        last_in = sb("last_in", [P, GT, J, 2])
        cidx = sb("cidx", [P, J], U32)
        relT = sb("relT", [F, R])
        wcT = sb("wcT", [B, R])
        rel_sb = sb("rel_sb", [R, F])
        wc_sb = sb("wc_sb", [R, B])
        w_sb = sb("w_sb", [B, F, F])
        a1 = sb("a1", [F, F + 1])
        a2 = sb("a2", [F, F + 1])
        TW = sb("TW", [F + 1, R, M1])
        NW = sb("NW", [F + 1, 3 * F])
        hs = sb("hs", [P, 2, F])
        hT = sb("hT", [F + 1, 2, P])
        tb = [sb(f"tb{b}", [P, H, TR]) for b in range(2)]
        nrow = sb("nrow", [P, 2, 3 * F])
        acc_flat, part_flat = (tb[b][:].rearrange("p r c -> p (r c)")[:, 0:J * M1] for b in range(2))
        acc = acc_flat.rearrange("p (j f) -> p j f", j=J)
        yhn = sb("yhn", [P, J, F])
        sfn = sb("sfn", [P, J, F])
        raw = sb("raw", [P, P], I32)
        rawf = sb("rawf", [P, P])
        cols = sb("cols", [P, P])
        idx_a = sb("idx_a", [P, TS], U32)
        idx_b = sb("idx_b", [P, TS], U32)
        idx_s = sb("idx_s", [P, TS], U32)
        shifted = sb("shifted", [P, TS])
        picked = sb("picked", [P, TS])
        cnt = sb("cnt", [P, TS])
        eq = sb("eq", [P, TS, P])
        rows_a = sb("rows_a", [P, TS, TR])
        rows_b = sb("rows_b", [P, TS, F])
        val = sb("val", [P, TS, F + 1])
        prod = sb("prod", [P, TS, F + 2])
        et_i = sb("et_i", [P, TS], I32)
        odd = sb("odd", [P, TS, 2])
        weight2 = sb("weight2", [P, TS, 2])
        val2 = sb("val2", [P, TS, 2, F])
        score = sb("score", [P, 4, TS])
        sums = sb("sums", [P, TS, F + 1])
        eno = sb("eno", [P, TS])
        lastrow = sb("lastrow", [P, TS, 2])
        cidx_s = sb("cidx_s", [P, 7], U32)
        cg = sb("cg", [P, 7, F])

        s_const = sem("const_ready")
        s_x = sem("x_loaded")
        s_w = sem("weights_loaded")
        s_zero = sem("tables_zeroed")
        s_zt = sem("zeros_ready")
        s_wt = sem("weight_transposed")
        s_wtc = sem("weight_copied")
        s_wp = sem("weight_products")
        s_wready = sem("table_weights_ready")
        s_v = sem("dve_steps")
        s_var = sem("variance_ready")
        s_std = sem("deviation_ready")
        s_h0 = sem("h0_ready")
        s_h0d = sem("h0_stored")
        s_rawld = [sem(f"edges_loaded{n}") for n in (0, 1)]
        s_cast = [sem(f"edges_cast{n}") for n in (0, 1)]
        s_cols = [sem(f"columns_turned{n}") for n in (0, 1)]
        s_stage = [sem(f"columns_staged{n}") for n in (0, 1)]
        s_row = [sem(f"rows_spread{n}") for n in (0, 1)]
        s_eq = [sem(f"equal_ready{n}") for n in (0, 1)]
        s_val = [sem(f"values_ready{n}") for n in (0, 1)]
        s_sum = [sem(f"sums_ready{n}") for n in (0, 1)]
        s_out = [sem(f"sums_copied{n}") for n in (0, 1)]
        s_sidx = [sem(f"scatter_index_ready{n}") for n in (0, 1)]
        s_got = [[sem(f"gathered{n}_{g}") for g in range(NG)] for n in (0, 1)]
        s_put = [[sem(f"scattered{n}_{c}") for c in range(GT)] for n in (0, 1)]
        s_lastput = [sem(f"last_scattered{c}") for c in range(GT)]
        s_dve = [sem(f"dve_edge_steps{n}") for n in (0, 1)]
        s_score = sem("score_ready")
        s_att = sem("attention_ready")
        s_gate = sem("pool_gate")
        s_agate = sem("act_gate")
        s_sgate = sem("sp_gate")
        s_part = sem("partial_sums_loaded")
        s_partused = sem("partial_sums_used")
        s_h1 = sem("h1_ready")
        s_xh = sem("source_rows_copied")
        s_hs = sem("node_rows_staged")
        s_hst = sem("node_rows_turned")
        s_hT = sem("node_rows_copied")
        s_np = sem("node_products")
        s_npc = sem("node_products_copied")
        s_tp = sem("table_products")
        s_ca = sem("chunks_free_act")
        s_cv = sem("chunks_free_dve")
        s_tst = [sem(f"table_stored{b}") for b in range(2)]
        s_nst = sem("node_tables_stored")
        s_ci = sem("self_index_ready")
        s_cg = sem("self_gathered")
        s_cgc = sem("self_copied")
        s_tail = sem("dve_tail_steps")
        s_res = sem("result_ready")
        s_fin = sem("result_stored")

        block = ctx.enter_context(nc.Block())
        NW_DMAS = 9

        def node_parts(t):
            for a, b in SPLIT:
                yield slice(a, b), J, t[a * J:b * J, :].rearrange("(p j) f -> p j f", j=J)
            yield slice(P - 1, P), tail, t[(P - 1) * J:N, :].rearrange("(p j) f -> p j f", j=tail)

        def count_from_one(eng, *sems):
            for s in sems:
                eng.sem_inc(s, ONE)

        def whole(t):
            return t.rearrange("(p j) f -> p (j f)", p=P)

        @block.sync
        def _(sp):
            with nc.allow_non_contiguous_dma(reason="small weights"):
                sp.wait_ge(s_zt, 2)
                for parts, n, dram in node_parts(x):
                    sp.dma_start(xn[parts, 0:n, :], dram).then_inc(s_x, 16)
                sp.dma_start(rel_sb[:], L1_gnn_rel_emb).then_inc(s_w, 16)
                sp.dma_start(wc_sb[:], L1_gnn_w_comp).then_inc(s_w, 16)
                sp.dma_start(w_sb[:], L1_gnn_weight).then_inc(s_w, 16)
                sp.dma_start(a1[:, 0:F], L1_gnn_A1_w).then_inc(s_w, 16)
                sp.dma_start(a1[:, F:F + 1], L1_gnn_A1_b.rearrange("(a b) -> a b", b=1)).then_inc(s_w, 16)
                sp.dma_start(a2[:, 0:F], L1_gnn_A2_w).then_inc(s_w, 16)
                sp.dma_start(a2[:, F:F + 1], L1_gnn_A2_b.rearrange("(a b) -> a b", b=1)).then_inc(s_w, 16)
                sp.dma_start(NW[0:F, 2 * F:3 * F], L1_gnn_self_loop_weight).then_inc(s_w, 16)
                sp.dma_start(NW[F:F + 1, 2 * F:3 * F], zeros[0:1, 0:F]).then_inc(s_w, 16)
                sp.dma_start(h0_dram[NP:NT, :], zeros[:, 0:F]).then_inc(s_tst[0], 16)
                sp.dma_start(yh_dram[NP:NT, :], zeros[:, 0:F]).then_inc(s_tst[1], 16)
                sp.wait_ge(s_h0, 1)
                sp.dma_start(whole(h0_dram[0:NP, :]), hn[:].rearrange("p j f -> p (j f)")).then_inc(s_h0d, 16)

                def edge_rows(n, i):
                    sp.wait_ge(s_row[n], i * TS + ONE)
                    sp.sem_inc(s_sgate, 1)
                    sp.wait_ge(s_cast[n], i + ONE)
                    sp.sem_inc(s_sgate, 1)
                    rows = bass.ds(i * TS, TS)
                    sp.dma_start(raw[0:TS, :], src_rows[rows, :]).then_inc(s_rawld[n], 16)
                    sp.dma_start(raw[32:32 + TS, :], dst_rows[rows, :]).then_inc(s_rawld[n], 16)
                    if n == 0:
                        sp.dma_start(rawf[64:64 + TS, :], w_rows[rows, :]).then_inc(s_rawld[n], 16)
                    else:
                        sp.dma_start(raw[64:64 + TS, :], et_rows[rows, :]).then_inc(s_rawld[n], 16)

                sp.wait_ge(s_agate, 2)
                with sp.Fori(0, S) as i:
                    edge_rows(0, i)

                for c in range(GT):
                    for d in range(GT):
                        if c == 0:
                            sp.wait_ge(s_put[0][d], 16 * S * NG + FIRST)
                    if c:
                        sp.wait_ge(s_partused, c)
                    sp.dma_start(part_flat, whole(lap_sums[c][0:NP, :])).then_inc(s_part, 16)

                tv = table.rearrange("(p j h) c -> p j (h c)", p=P, j=J)
                with sp.Fori(0, J // 2) as i:
                    for b in range(2):
                        sp.wait_ge(s_ca, i * (2 * A_CHUNKS) + (b + 2) * A_CHUNKS)
                        sp.sem_inc(s_sgate, 1)
                        sp.wait_ge(s_cv, i * (2 * V_CHUNKS) + (b + 2) * V_CHUNKS)
                        sp.sem_inc(s_sgate, 1)
                        sp.dma_start(tv[:, bass.ds(i * 2 + b, 1), :].rearrange("p j c -> p (j c)"),
                                     tb[b][:].rearrange("p r c -> p (r c)")).then_inc(s_tst[b], 16)
                sp.wait_ge(s_npc, J + ONE)
                sp.dma_start(whole(yh_dram[0:NP, :]), yhn[:].rearrange("p j f -> p (j f)")).then_inc(s_nst, 16)
                sp.dma_start(whole(self_dram), sfn[:].rearrange("p j f -> p (j f)")).then_inc(s_nst, 16)

                with sp.Fori(0, S) as i:
                    edge_rows(1, i)

                for c in range(GT):
                    if c == 0:
                        for d in range(GT):
                            sp.wait_ge(s_put[1][d], 16 * S * NG + FIRST)
                            sp.wait_ge(s_lastput[d], 16 * S * NG + FIRST)
                        for d in range(GT):
                            sp.dma_start(last_in[:, d, :, :].rearrange("p j f -> p (j f)"),
                                         whole(last_rows[d][0:NP, :])).then_inc(s_part, 16)
                    sp.wait_ge(s_partused, GT + c)
                    sp.dma_start(part_flat[:, 0:J * F],
                                 whole(nei_sums[c][0:NP, :])).then_inc(s_part, 16)

                sp.wait_ge(s_res, 1)
                for parts, n, dram in node_parts(out):
                    sp.dma_start(dram, xn[parts, 0:n, :]).then_inc(s_fin, 16)
                sp.wait_ge(s_fin, 16 * 3)

        @block.gpsimd
        def _(pool):
            nc.gpsimd.memset(zeros[:], 0.0).then_inc(s_zt, 1)
            nc.gpsimd.memset(xn[:], 0.0).then_inc(s_zt, 1)
            pool.wait_ge(s_zt, 2)
            for c in range(GT):
                pool.dma_start(whole(lap_sums[c]), zeros[:, 0:99 * 33]).then_inc(s_put[0][c], 16)
                pool.dma_start(whole(nei_sums[c]), zeros[:, 0:99 * F]).then_inc(s_put[1][c], 16)
                pool.dma_start(whole(last_rows[c]), zeros[:, 0:99 * 2]).then_inc(s_lastput[c], 16)
            nc.gpsimd.memset(ident[:], 0.0).then_inc(s_const, 1)
            nc.gpsimd.memset(tri[:], 1.0).then_inc(s_const, 1)
            nc.gpsimd.iota(part[:], pattern=[[0, 1]], base=0, channel_multiplier=1,
                           allow_small_or_imprecise_dtypes=True).then_inc(s_const, 1)
            nc.gpsimd.iota(trash[:], pattern=[[0, 1]], base=NP, channel_multiplier=1,
                           allow_small_or_imprecise_dtypes=True).then_inc(s_const, 1)
            nc.gpsimd.iota(eno[:], pattern=[[P, TS]], base=1, channel_multiplier=1,
                           allow_small_or_imprecise_dtypes=True).then_inc(s_const, 1)
            pool.wait_ge(s_const, 5)
            nc.gpsimd.affine_select(out=ident[:], in_=ident[:], compare_op=ALU.not_equal, fill=1.0, base=0,
                                    pattern=[[-1, P]], channel_multiplier=1).then_inc(s_const, 1)
            nc.gpsimd.affine_select(out=tri[:], in_=tri[:], compare_op=ALU.is_ge, fill=0.0, base=0,
                                    pattern=[[1, P]], channel_multiplier=-1).then_inc(s_const, 1)

            pool.wait_ge(s_h0d, 16)
            pool.wait_ge(s_tst[0], FIRST)
            pool.wait_ge(s_tst[1], FIRST)
            pool.sem_inc(s_gate, 1)

            def gather(n, i, g):
                for t in range(g * GT, (g + 1) * GT):
                    if n == 0:
                        nc.gpsimd.indirect_dma_start(
                            rows_b[:, t, :], None, h0_dram,
                            bass.IndirectOffsetOnAxis(ap=idx_a[:, t:t + 1], axis=0)).then_inc(s_got[n][g], 16)
                    else:
                        nc.gpsimd.indirect_dma_start(
                            rows_a[:, t, :], None, table,
                            bass.IndirectOffsetOnAxis(ap=idx_a[:, t:t + 1], axis=0)).then_inc(s_got[n][g], 16)
                        nc.gpsimd.indirect_dma_start(
                            rows_b[:, t, :], None, yh_dram,
                            bass.IndirectOffsetOnAxis(ap=idx_b[:, t:t + 1], axis=0)).then_inc(s_got[n][g], 16)

            def scatter(n, i, g):
                pool.wait_ge(s_out[n], i * NG + (g + 1) + ONE)
                pool.wait_ge(s_sidx[n], i * NG + (g + 1))
                for c in range(GT):
                    pool.wait_ge(s_put[n][c], i * (16 * NG) + 16 * g + FIRST)
                    if n:
                        pool.wait_ge(s_lastput[c], i * (16 * NG) + 16 * g + FIRST)
                pool.sem_inc(s_gate, 1)
                for c in range(GT):
                    t = g * GT + c
                    to = bass.IndirectOffsetOnAxis(ap=idx_s[:, t:t + 1], axis=0)
                    if n == 0:
                        nc.gpsimd.indirect_dma_start(lap_sums[c], to, sums[:, t, :], None,
                                                     compute_op=ALU.add).then_inc(s_put[n][c], 16)
                    else:
                        nc.gpsimd.indirect_dma_start(nei_sums[c], to, sums[:, t, 0:F], None,
                                                     compute_op=ALU.add).then_inc(s_put[n][c], 16)
                        nc.gpsimd.indirect_dma_start(last_rows[c], to, lastrow[:, t, :],
                                                     None).then_inc(s_lastput[c], 16)

            def edge_turn(n, i):
                pool.wait_ge(s_stage[n], i + 1 + ONE)
                pool.sem_inc(s_gate, 1)
                gather(n, i, 0)
                for g in range(NG):
                    if g + 1 < NG:
                        gather(n, i, g + 1)
                    scatter(n, i, g)

            with pool.Fori(0, S) as i:
                edge_turn(0, i)
            for b in range(2):
                pool.wait_ge(s_tst[b], 16 * (J // 2) + FIRST)
            pool.wait_ge(s_nst, 32)
            pool.sem_inc(s_gate, 1)
            with pool.Fori(0, S) as i:
                edge_turn(1, i)

            with pool.Fori(0, J // 7) as i:
                pool.wait_ge(s_ci, i + 1)
                pool.sem_inc(s_gate, 1)
                for t in range(7):
                    nc.gpsimd.indirect_dma_start(
                        cg[:, t, :], None, self_dram,
                        bass.IndirectOffsetOnAxis(ap=cidx_s[:, t:t + 1], axis=0)).then_inc(s_cg, 16)

        @block.scalar
        def _(act):
            count_from_one(act, *s_cast, *s_out, s_hT, s_npc)

            def deviation(n):
                act.wait_ge(s_var, n + 1)
                nc.scalar.activation(stat[:, 2, :], stat[:, 1, :], ACT.Sqrt).then_inc(s_std, 1)

            def edge_turn(n, i):
                act.wait_ge(s_rawld[n], i * 48 + 48)
                act.sem_inc(s_agate, 1)
                rows = 64 if n == 0 else 96
                nc.scalar.copy(rawf[0:rows, :], raw[0:rows, :]).then_inc(s_cast[n], 1)
                for g in range(NG):
                    a, b = g * GT, (g + 1) * GT
                    if n == 1:
                        act.wait_ge(s_score, i * NG + (g + 1))
                        act.sem_inc(s_agate, 1)
                        nc.scalar.activation(score[:, 2, a:b], score[:, 1, a:b], ACT.Tanh,
                                             scale=float(F) ** -0.5).then_inc(s_att, 1)
                    act.wait_ge(s_sum[n], i * TS + (g + 1) * GT)
                    act.sem_inc(s_agate, 1)
                    o = (g // 2) * GT * M1
                    width = M1 if n == 0 else F
                    nc.scalar.copy(sums[:, a:b, 0:width], sum_ps[g % 2][:, o:o + GT * M1].rearrange(
                        "p (t f) -> p t f", f=M1)[:, :, 0:width]).then_inc(s_out[n], 1)

            act.wait_ge(s_zt, 2)
            nc.scalar.copy(raw[:], zeros[:, 0:P]).then_inc(s_agate, 1)
            nc.scalar.copy(rawf[:], zeros[:, 0:P]).then_inc(s_agate, 1)
            deviation(0)
            act.wait_ge(s_agate, 2)
            with act.Fori(0, S) as i:
                edge_turn(0, i)
            deviation(1)
            act.wait_ge(s_wready, 1)
            act.sem_inc(s_ca, A_CHUNKS)
            with act.Fori(0, J // 2) as i:
                for b in range(2):
                    j = i * 2 + b
                    act.wait_ge(s_hst, j + 1 + ONE)
                    act.sem_inc(s_agate, 1)
                    nc.scalar.copy(hT[0:F, b, :], turn_ps[0:F, 0:P]).then_inc(s_hT, 1)
                    act.wait_ge(s_xh, j + 1 + ONE)
                    act.sem_inc(s_agate, 1)
                    nc.scalar.copy(yhn[:, bass.ds(j, 1), :].rearrange("p j f -> p (j f)"),
                                   nrow[:, b, F:2 * F]).then_inc(s_agate, 1)
                    nc.scalar.copy(sfn[:, bass.ds(j, 1), :].rearrange("p j f -> p (j f)"),
                                   nrow[:, b, 2 * F:3 * F]).then_inc(s_npc, 1)
                    act.wait_ge(s_tst[b], i * 16 + FIRST)
                    for q, (r, n) in enumerate(CHUNKS):
                        if q % 2:
                            continue
                        act.wait_ge(s_tp, i * (2 * len(CHUNKS)) + (b * len(CHUNKS) + q + 1))
                        act.sem_inc(s_agate, 1)
                        ins = nc.scalar.copy(tb[b][:, r // 2:(r + n) // 2, 0:2 * M1],
                                             chunk_ps[q][:, 0:n * M1].rearrange("p (h c) -> p h c", c=2 * M1))
                        ins.then_inc(s_ca, 1)
            with act.Fori(0, S) as i:
                edge_turn(1, i)

        @block.tensor
        def _(pe):
            count_from_one(pe, *s_row, s_hst)
            pe.wait_ge(s_const, 7)
            pe.wait_ge(s_w, 16 * NW_DMAS)
            nc.tensor.transpose(banks[0][0:F, 0:R], rel_sb[:], ident[0:R, 0:R])
            nc.tensor.transpose(banks[1][0:B, 0:R], wc_sb[:], ident[0:R, 0:R])
            nc.tensor.matmul(banks[2][0:F + 1, 0:F], a1[:], ident[0:F, 0:F], start=True, stop=True)
            nc.tensor.matmul(banks[3][0:F + 1, 0:F], a2[:], ident[0:F, 0:F], start=True, stop=True).then_inc(s_wt, 1)
            pe.wait_ge(s_wtc, 1)
            for q in range(7):
                k = 5 if q < 6 else 2
                if q >= 1:
                    pe.wait_ge(s_wtc, q + 1)
                for m in range(k):
                    o = q * 5 + m
                    ins = nc.tensor.matmul(banks[q % 2][0:F, m * R:(m + 1) * R], w_sb[:, :, o], wcT[:],
                                           start=True, stop=True)
                ins.then_inc(s_wp, 1)
            nc.tensor.matmul(banks[2][0:F + 1, 0:R], a1[:], relT[:], start=True, stop=True).then_inc(s_wp, 1)

            def edge_turn(n, i):
                pe.wait_ge(s_cast[n], i + 1 + ONE)
                pe.wait_ge(s_rawld[n], i * 48 + 48)
                pe.wait_ge(s_stage[n], i + ONE)
                nc.tensor.transpose(cols_ps[:, 0:P], rawf[:], ident[:]).then_inc(s_cols[n], 1)
                key = 0 if n == 0 else 32
                width = M1 if n == 0 else F
                for t in range(TS):
                    pe.wait_ge(s_eq[n], i * TS + max(t - 1, 0) + ONE)
                    nc.tensor.matmul(row_ps[t % 2], rowsel[key:key + 32, t, :], rawf[key:key + 32, :],
                                     start=True, stop=True).then_inc(s_row[n], 1)
                    if t >= GT - 1 and t % GT == GT - 1:
                        g = t // GT
                        pe.wait_ge(s_eq[n], i * TS + (t + 1) + ONE)
                        pe.wait_ge(s_val[n], i * NG + (g + 1))
                        pe.wait_ge(s_out[n], i * NG + max(g - 1, 0) + ONE)
                        for c in range(GT):
                            o = (g // 2) * GT * M1 + c * M1
                            k = g * GT + c
                            if n == 0:
                                ins = nc.tensor.matmul(sum_ps[g % 2][:, o:o + M1], eq[:, k, :], val[:, k, :],
                                                       start=True, stop=True)
                            else:
                                for h in range(2):
                                    ins = nc.tensor.matmul(sum_ps[g % 2][:, o:o + F], eq[:, k, :], val2[:, k, h, :],
                                                           start=h == 0, stop=h == 1)
                            ins.then_inc(s_sum[n], 1)

            pe.wait_ge(s_const, 8)
            with pe.Fori(0, S) as i:
                edge_turn(0, i)

            pe.wait_ge(s_wready, 1)
            with pe.Fori(0, J // 2) as i:
                for b in range(2):
                    j = i * 2 + b
                    pe.wait_ge(s_hs, j + 1)
                    pe.wait_ge(s_hT, j + ONE)
                    pe.wait_ge(s_ca, i * (2 * A_CHUNKS) + (b + 1) * A_CHUNKS)
                    nc.tensor.transpose(turn_ps[0:F, 0:P], hs[:, b, :], ident[:]).then_inc(s_hst, 1)
                    pe.wait_ge(s_hT, j + 1 + ONE)
                    pe.wait_ge(s_xh, j + ONE)
                    nc.tensor.matmul(node_ps[:, 0:3 * F], hT[:, b, :], NW[:], start=True, stop=True).then_inc(s_np, 1)
                    for q, (r, n) in enumerate(CHUNKS):
                        if q % 2 == 0:
                            pe.wait_ge(s_ca, i * (2 * A_CHUNKS) + (b * A_CHUNKS + q // 2 + 1))
                        else:
                            pe.wait_ge(s_cv, i * (2 * V_CHUNKS) + (b * V_CHUNKS + q // 2 + 1))
                        nc.tensor.matmul(chunk_ps[q][:, 0:n * M1], hT[:, b, :],
                                         TW[:, r:r + n, :].rearrange("p r c -> p (r c)"),
                                         start=True, stop=True).then_inc(s_tp, 1)
            with pe.Fori(0, S) as i:
                edge_turn(1, i)

        @block.vector
        def _(dve):
            count_from_one(dve, *s_stage, *s_eq, s_xh)
            steps = Steps(dve, s_v)

            def bc(a):
                return a.unsqueeze(2).broadcast_to([P, J, F])

            def layer_norm(n):
                steps.done(nc.vector.tensor_reduce(stat[:, 0, :], xn[:], AX_X, ALU.add))
                steps.done(nc.vector.tensor_scalar(stat[:, 1, :], stat[:, 0, :], 1.0 / F, None, ALU.mult))
                steps.done(nc.vector.tensor_tensor(hn[:], xn[:], bc(stat[:, 1, :]), ALU.subtract))
                steps.done(nc.vector.tensor_tensor(sq[:], hn[:], hn[:], ALU.mult))
                steps.done(nc.vector.tensor_reduce(stat[:, 0, :], sq[:], AX_X, ALU.add))
                nc.vector.tensor_scalar(stat[:, 1, :], stat[:, 0, :], 1.0 / F, EPS, ALU.mult, ALU.add).then_inc(s_var, 1)
                dve.wait_ge(s_std, n + 1)
                steps.done(nc.vector.reciprocal(stat[:, 3, :], stat[:, 2, :]))
                steps.done(nc.vector.tensor_tensor(hn[:], hn[:], bc(stat[:, 3, :]), ALU.mult))
                nc.vector.tensor_scalar(hn[:], hn[:], 0.0, None, ALU.max).then_inc(s_h1 if n else s_h0, 1)

            dve.wait_ge(s_x, 48)
            layer_norm(0)

            dve.wait_ge(s_wt, 1)
            nc.vector.tensor_copy(NW[:, 0:F], banks[2][0:F + 1, 0:F]).then_inc(s_v, 1)
            nc.vector.tensor_copy(NW[:, F:2 * F], banks[3][0:F + 1, 0:F]).then_inc(s_v, 1)
            nc.vector.tensor_copy(relT[:], banks[0][0:F, 0:R]).then_inc(s_v, 1)
            steps.n += 3
            nc.vector.tensor_copy(wcT[:], banks[1][0:B, 0:R]).then_inc(s_v, 1)
            steps.n += 1
            nc.vector.memset(TW[F:F + 1, :, 0:F], 0.0).then_inc(s_v, 1)
            steps.n += 1
            dve.wait_ge(s_v, steps.value())
            nc.vector.memset(hT[F:F + 1, :, :], 1.0).then_inc(s_wtc, 1)
            for q in range(7):
                k = 5 if q < 6 else 2
                dve.wait_ge(s_wp, q + 1)
                nc.vector.tensor_copy(TW[0:F, :, q * 5:q * 5 + k],
                                      banks[q % 2][0:F, 0:k * R].rearrange("p (o r) -> p r o", o=k)).then_inc(s_wtc, 1)
            dve.wait_ge(s_wp, 8)
            dve.wait_ge(s_wtc, 8)
            nc.vector.tensor_copy(TW[:, :, F:F + 1], banks[2][0:F + 1, 0:R].unsqueeze(2)).then_inc(s_wready, 1)
            dve.wait_ge(s_const, 7)
            for q in range(4):
                k = slice(q * 32, (q + 1) * 32)
                ins = nc.vector.tensor_copy(rowsel[k, :, :],
                                            ident[k, q * 32:q * 32 + TS].unsqueeze(2).broadcast_to([32, TS, P]))
            ins.then_inc(s_const, 1)

            def edge_turn(n, i, per_turn):
                steps = Steps(dve, s_dve[n], i, per_turn)
                key = 0 if n == 0 else 32
                for c in range(GT):
                    dve.wait_ge(s_put[n][c], i * (16 * NG) + FIRST)
                    if n:
                        dve.wait_ge(s_lastput[c], i * (16 * NG) + FIRST)
                dve.wait_ge(s_cols[n], i + 1)
                steps.done(nc.vector.tensor_copy(cols[:], cols_ps[:, 0:P]))
                kcols = cols[:, key:key + TS]
                if n == 0:
                    steps.done(nc.vector.tensor_copy(idx_a[:], cols[:, 32:32 + TS]))
                else:
                    steps.done(nc.vector.tensor_copy(et_i[:], cols[:, 64:64 + TS]))
                    steps.done(nc.vector.tensor_scalar(et_i[:], et_i[:], 1, None, ALU.bitwise_and))
                    steps.done(nc.vector.tensor_copy(odd[:, :, 1:2], et_i[:].unsqueeze(2)))
                    steps.done(nc.vector.tensor_scalar(odd[:, :, 0:1], odd[:, :, 1:2], -1.0, 1.0, ALU.mult, ALU.add))
                    steps.done(nc.vector.scalar_tensor_tensor(out=picked[:], in0=cols[:, 0:TS], scalar=float(R),
                                                              in1=cols[:, 64:64 + TS], op0=ALU.mult, op1=ALU.add))
                    steps.done(nc.vector.tensor_tensor(picked[:].unsqueeze(2), picked[:].unsqueeze(2), odd[:, :, 1:2], ALU.subtract))
                    steps.done(nc.vector.tensor_scalar(idx_a[:], picked[:], 0.5, None, ALU.mult))
                    steps.done(nc.vector.tensor_copy(idx_b[:], cols[:, 32:32 + TS]))
                    steps.done(nc.vector.tensor_copy(lastrow[:, :, 0:1], eno[:].unsqueeze(2)))
                    steps.done(nc.vector.tensor_scalar(lastrow[:, :, 1:2], cols[:, 0:TS].unsqueeze(2), 1.0, None, ALU.add))
                    steps.done(nc.vector.tensor_scalar(eno[:], eno[:], float(SE), None, ALU.add))
                nc.vector.tensor_scalar(shifted[:], kcols, trash[:, 0:1], None, ALU.subtract).then_inc(s_stage[n], 1)
                for g in range(NG):
                    a, b = g * GT, (g + 1) * GT
                    for t in range(a, b):
                        dve.wait_ge(s_row[n], i * TS + (t + 1) + ONE)
                        nc.vector.scalar_tensor_tensor(out=eq[:, t, :], in0=row_ps[t % 2],
                                                       scalar=cols[:, key + t:key + t + 1], in1=tri[:],
                                                       op0=ALU.is_equal, op1=ALU.mult,
                                                       accum_out=cnt[:, t:t + 1]).then_inc(s_eq[n], 1)
                    dve.wait_ge(s_eq[n], i * TS + b + ONE)
                    dve.wait_ge(s_stage[n], i + 1 + ONE)
                    steps.done(nc.vector.scalar_tensor_tensor(out=picked[:, a:b], in0=cnt[:, a:b], scalar=1.0,
                                                              in1=shifted[:, a:b], op0=ALU.is_equal, op1=ALU.mult))
                    nc.vector.tensor_scalar(idx_s[:, a:b], picked[:, a:b], trash[:, 0:1], None,
                                            ALU.add).then_inc(s_sidx[n], 1)
                    dve.wait_ge(s_got[n][g], i * (16 * GT * (n + 1)) + 16 * GT * (n + 1))
                    if n == 0:
                        w = cols[:, 64 + a:64 + b].unsqueeze(2)
                        steps.done(nc.vector.tensor_copy(val[:, a:b, F:F + 1], w))
                        nc.vector.tensor_tensor(val[:, a:b, 0:F], rows_b[:, a:b, :], w.broadcast_to([P, GT, F]),
                                                ALU.mult).then_inc(s_val[n], 1)
                    else:
                        pair = rows_a[:, a:b, 0:2 * M1].rearrange("p t (h c) -> p t h c", h=2)
                        steps.done(nc.vector.tensor_tensor(prod[:, a:b, 0:F], rows_a[:, a:b, 2 * M1:TR], rows_b[:, a:b, :], ALU.mult))
                        steps.done(nc.vector.tensor_tensor(prod[:, a:b, F:F + 2].unsqueeze(3), pair[:, :, :, F:M1],
                                                           odd[:, a:b, :].unsqueeze(3), ALU.mult))
                        steps.done(nc.vector.tensor_reduce(score[:, 0, a:b], prod[:, a:b, :], AX_X, ALU.add))
                        nc.vector.tensor_scalar(score[:, 1, a:b], score[:, 0, a:b], 0.0, None, ALU.max).then_inc(s_score, 1)
                        dve.wait_ge(s_att, i * NG + (g + 1))
                        steps.done(nc.vector.scalar_tensor_tensor(out=weight2[:, a:b, :], in0=score[:, 2, a:b].unsqueeze(2).broadcast_to([P, GT, 2]),
                                                                  scalar=0.0, in1=odd[:, a:b, :], op0=ALU.max, op1=ALU.mult))
                        nc.vector.tensor_tensor(val2[:, a:b, :, :], pair[:, :, :, 0:F],
                                                weight2[:, a:b, :].unsqueeze(3).broadcast_to([P, GT, 2, F]),
                                                ALU.mult).then_inc(s_val[n], 1)
                assert steps.n == per_turn, steps.n

            dve.wait_ge(s_const, 8)
            with dve.Fori(0, S) as i:
                edge_turn(0, i, 12)

            accv = acc_flat
            inv = part_flat
            for c in range(GT):
                dve.wait_ge(s_part, 16 * (c + 1))
                if c == 0:
                    ins = nc.vector.tensor_copy(accv, inv)
                else:
                    dve.wait_ge(s_partused, c)
                    ins = nc.vector.tensor_tensor(accv, accv, inv, ALU.add)
                ins.then_inc(s_partused, 1)
            dve.wait_ge(s_partused, GT)
            dve.wait_ge(s_h0, 1)
            dve.wait_ge(s_h0d, 16)
            steps.done(nc.vector.tensor_tensor(hn[:], hn[:], acc[:, :, F:F + 1].broadcast_to([P, J, F]), ALU.mult))
            steps.done(nc.vector.tensor_tensor(sq[:], acc[:, :, 0:F], hn[:], ALU.subtract))
            steps.done(nc.vector.tensor_tensor(xn[:], xn[:], sq[:], ALU.add))
            layer_norm(1)

            dve.wait_ge(s_h1, 1)
            dve.sem_inc(s_cv, V_CHUNKS)
            with dve.Fori(0, J // 2) as i:
                for b in range(2):
                    j = i * 2 + b
                    dve.wait_ge(s_hst, j + ONE)
                    nc.vector.tensor_copy(hs[:, b, :], hn[:, bass.ds(j, 1), :].rearrange("p j f -> p (j f)")).then_inc(s_hs, 1)
                    dve.wait_ge(s_np, j + 1)
                    dve.wait_ge(s_npc, j + ONE)
                    nc.vector.tensor_copy(nrow[:, b, :], node_ps[:, 0:3 * F]).then_inc(s_xh, 1)
                    dve.wait_ge(s_xh, j + 1 + ONE)
                    dve.wait_ge(s_tst[b], i * 16 + FIRST)
                    nc.vector.tensor_copy(tb[b][:, :, 2 * M1:TR], nrow[:, b, 0:F].unsqueeze(1).broadcast_to([P, H, F])).then_inc(s_v, 1)
                    for q, (r, n) in enumerate(CHUNKS):
                        if q % 2:
                            dve.wait_ge(s_tp, i * (2 * len(CHUNKS)) + (b * len(CHUNKS) + q + 1))
                            ins = nc.vector.tensor_copy(tb[b][:, r // 2:(r + n) // 2, 0:2 * M1],
                                                        chunk_ps[q][:, 0:n * M1].rearrange("p (h c) -> p h c", c=2 * M1))
                            ins.then_inc(s_cv, 1)

            with dve.Fori(0, S) as i:
                edge_turn(1, i, 37)

            sq_flat = sq[:].rearrange("p j f -> p (j f)")
            for c in range(GT):
                dve.wait_ge(s_part, 16 * (2 * GT + c + 1))
                if c == 0:
                    ins = nc.vector.tensor_copy(sq_flat, part_flat[:, 0:J * F])
                else:
                    dve.wait_ge(s_partused, GT + c)
                    ins = nc.vector.tensor_tensor(sq_flat, sq_flat, part_flat[:, 0:J * F], ALU.add)
                ins.then_inc(s_partused, 1)
            tail_steps = Steps(dve, s_tail)
            latest, hit, found, source = (stat[:, q, :] for q in range(4))
            tail_steps.done(nc.vector.tensor_copy(latest, last_in[:, 0, :, 0]))
            for c in range(1, GT):
                tail_steps.done(nc.vector.tensor_tensor(latest, latest, last_in[:, c, :, 0], ALU.max))
            for c in range(GT):
                tail_steps.done(nc.vector.tensor_tensor(hit, latest, last_in[:, c, :, 0], ALU.is_equal))
                if c == 0:
                    tail_steps.done(nc.vector.tensor_tensor(source, hit, last_in[:, c, :, 1], ALU.mult))
                else:
                    tail_steps.done(nc.vector.tensor_tensor(found, hit, last_in[:, c, :, 1], ALU.mult))
                    tail_steps.done(nc.vector.tensor_tensor(source, source, found, ALU.add))
            tail_steps.done(nc.vector.tensor_scalar(cidx[:], source, -1.0, 0.0, ALU.add, ALU.max))
            tail_steps.done(nc.vector.tensor_scalar(hit, source, 1.0, None, ALU.min))
            dve.wait_ge(s_nst, 32)
            with dve.Fori(0, J // 7) as i:
                nc.vector.tensor_copy(cidx_s[:], cidx[:, bass.ds(i * 7, 7)]).then_inc(s_ci, 1)
                dve.wait_ge(s_cg, i * (16 * 7) + 16 * 7)
                nc.vector.tensor_copy(yhn[:, bass.ds(i * 7, 7), :], cg[:]).then_inc(s_cgc, 1)
            dve.wait_ge(s_cgc, J // 7)
            tail_steps.done(nc.vector.tensor_tensor(sq[:], sq[:], yhn[:], ALU.add))
            tail_steps.done(nc.vector.tensor_tensor(sq[:], sq[:], bc(hit), ALU.mult))
            tail_steps.done(nc.vector.tensor_scalar(sq[:], sq[:], 0.0, None, ALU.max))
            nc.vector.tensor_tensor(xn[:], xn[:], sq[:], ALU.add).then_inc(s_res, 1)


_INS = ['x', 'src', 'dst', 'edge_type_86', 'edge_weight', 'L1_gnn_weight', 'L1_gnn_w_comp',
        'L1_gnn_self_loop_weight', 'L1_gnn_A1_w', 'L1_gnn_A1_b', 'L1_gnn_A2_w', 'L1_gnn_A2_b',
        'L1_gnn_rel_emb']


def kernel(**inputs):
    import numpy as _np
    import concourse.bacc as _bacc
    from concourse import mybir as _mybir
    from concourse.bass_utils import run_bass_kernel_spmd as _run

    nc = _bacc.Bacc("TRN2", target_bir_lowering=False, num_devices=1)
    arrays, args = {}, []
    for name in _INS:
        a = _np.ascontiguousarray(inputs[name])
        arrays[f"in_{name}_dram"] = a
        args.append(nc.dram_tensor(f"in_{name}_dram", a.shape, _mybir.dt.from_np(a.dtype), kind="ExternalInput").ap())
    out = nc.dram_tensor("out_0_dram", inputs["x"].shape, _mybir.dt.float32, kind="ExternalOutput").ap()
    gnn_kernel(nc, *args, out)
    r = _run(nc, [arrays], core_ids=[0])
    return r.results[0]["out_0_dram"]
```

```python
from contextlib import ExitStack

import concourse.bass as bass
from concourse import mybir

ALU = mybir.AluOpType
ACT = mybir.ActivationFunctionType
AX_X = mybir.AxisListType.X
F32 = mybir.dt.float32
I32 = mybir.dt.int32
U32 = mybir.dt.uint32
BF16 = mybir.dt.bfloat16

P = 128
TS = 25
GT = 5
DELAY = (4, 5)
STAGE_STEPS = 7
NG = TS // GT
SE = TS * P
EPS = 1e-5
ONE = 1
FIRST = 16


class Steps:

    def __init__(self, eng, sem, turn=None, per_turn=0, start=0):
        self.eng, self.sem, self.turn, self.per_turn, self.start, self.n = eng, sem, turn, per_turn, start, 0

    def value(self):
        v = self.start + self.n
        return v if self.turn is None else self.turn * self.per_turn + v

    def done(self, ins):
        ins.then_inc(self.sem, 1)
        self.n += 1
        self.eng.wait_ge(self.sem, self.value())


def gnn_kernel(nc, x, src, dst, edge_type_86, edge_weight, L1_gnn_weight, L1_gnn_w_comp,
               L1_gnn_self_loop_weight, L1_gnn_A1_w, L1_gnn_A1_b, L1_gnn_A2_w, L1_gnn_A2_b,
               L1_gnn_rel_emb, out):
    N, F = x.shape
    E = src.shape[0]
    R, B = L1_gnn_w_comp.shape
    S = E // SE
    J = -(-N // P)
    NP = J * P
    NT = NP + P
    M1 = F + 1
    H = R // 2
    TR = 2 * M1 + F
    RC = 14
    CHUNKS = [(r, min(RC, R - r)) for r in range(0, R, RC)]
    assert S * SE == E and F == 32 and R <= P and 2 * H == R and RC % 2 == 0 and RC * M1 <= 512 and J % 2 == 0 and J % 7 == 0
    tail = N - (P - 1) * J
    SPLIT = ((0, 112), (112, 127))

    h0_dram = nc.dram_tensor("h0", (NT, F), F32).ap()
    yh_dram = nc.dram_tensor("yh", (NT, F), F32).ap()
    self_dram = nc.dram_tensor("self_rows", (NP, F), F32).ap()
    table = nc.dram_tensor("relation_table", (NP * H, TR), F32).ap()
    lap_sums = [nc.dram_tensor(f"lap_sums{c}", (NT, F + 1), F32).ap() for c in range(GT)]
    window_sums = nc.dram_tensor("window_sums", (NT, M1), F32).ap()
    dst_next = nc.dram_tensor("dst_next", (E,), I32).ap()
    nei_sums = [nc.dram_tensor(f"nei_sums{c}", (NT, F), F32).ap() for c in range(GT)]
    last_rows = [nc.dram_tensor(f"last_rows{c}", (NT, 2), F32).ap() for c in range(GT)]

    src_rows = src.rearrange("(t p) -> t p", p=P)
    dst_rows = dst.rearrange("(t p) -> t p", p=P)
    et_rows = edge_type_86.rearrange("(t p) -> t p", p=P)
    next_rows = dst_next.rearrange("(t p) -> t p", p=P)
    w_rows = edge_weight.rearrange("(t p) -> t p", p=P)

    with ExitStack() as ctx:
        def sb(name, shape, dt=F32):
            return ctx.enter_context(nc.sbuf_tensor(name, shape, dt))

        def sem(name):
            return ctx.enter_context(nc.semaphore(name))

        banks = [ctx.enter_context(nc.psum_tensor(f"bank{b}", [P, 512], F32)) for b in range(8)]
        cols_ps, sum_ps = banks[0], banks[1:3]
        row_ps = [b[:, 0:P] for b in banks[3:5]]
        chunk_ps = banks[0:len(CHUNKS)]
        turn_ps, node_ps = banks[6], banks[7]
        A_CHUNKS, V_CHUNKS = (len(CHUNKS) + 1) // 2, len(CHUNKS) // 2

        ident = sb("ident", [P, P])
        tri = sb("tri", [P, P])
        row_of_src, row_of_dst = sb("row_of_src", [P, TS, P]), sb("row_of_dst", [P, TS, P])
        trash = sb("trash", [P, 1])
        part = sb("part", [P, 1])
        xn = sb("xn", [P, J, F])
        hn = sb("hn", [P, J, F])
        sq = sb("sq", [P, J, F])
        stat = sb("stat", [P, 4, J])
        last_in = sb("last_in", [P, GT, J, 2])
        cidx = sb("cidx", [P, J], U32)
        relT = sb("relT", [F, R])
        wcT = sb("wcT", [B, R])
        rel_sb = sb("rel_sb", [R, F])
        wc_sb = sb("wc_sb", [R, B])
        w_sb = sb("w_sb", [B, F, F])
        a1 = sb("a1", [F, F + 1])
        a2 = sb("a2", [F, F + 1])
        TW = sb("TW", [F + 1, R, M1])
        NW = sb("NW", [F + 1, 3 * F])
        hs = sb("hs", [P, 2, F])
        hT = sb("hT", [F + 1, 2, P])
        tb = [sb(f"tb{b}", [P, H, TR]) for b in range(2)]
        nrow = sb("nrow", [P, 2, 3 * F])
        acc_flat, part_flat = (tb[b][:].rearrange("p r c -> p (r c)")[:, 0:J * M1] for b in range(2))
        part_rows = part_flat.rearrange("p (j f) -> p j f", j=J)
        acc = acc_flat.rearrange("p (j f) -> p j f", j=J)
        node_rows = sb("node_rows", [P, 2, J, F])
        yhn, sfn = node_rows[:, 0], node_rows[:, 1]
        zeros = node_rows[:].rearrange("p a j f -> p (a j f)")[:, 0:NT // P * M1]
        CE = E // P
        chk = tb[0][:].rearrange("p r c -> p (r c)")[:, 0:CE + 1].bitcast(I32)
        rises = tb[1][:].rearrange("p r c -> p (r c)")[:, 0:CE]
        ends = sb("ends", [P, 2], I32)
        odds = sb("odds", [P, 4])
        flag = sb("flag", [1, 1], I32)
        first_dst = sb("first_dst", [1, S], I32)
        iota_row = sb("iota_row", [P, P])
        window = sb("window", [P, F])
        base = sb("base", [P, 2])
        at_window = sb("at_window", [P, GT, P], BF16)
        wraw = sb("wraw", [32, P])
        wide_window = sb("wide_window", [P, F])
        window3 = sb("window3", [P, 3, F], BF16)
        rowi = sb("rowi", [P, P], I32)
        row_mask = sb("row_mask", [P, 1], I32)
        rowm = sb("rowm", [P, P], I32)
        rowb = sb("rowb", [P, P], BF16)
        cols_next = sb("cols_next", [P, P])
        odd_next = sb("odd_next", [P, TS, 2])
        double_idx = sb("double_idx", [P, TS])
        in_window = sb("in_window", [P, TS])
        last_val = sb("last_val", [P, TS])
        win_sb = sb("win_sb", [P, M1])
        raw = sb("raw", [P, P], I32)
        rawf = sb("rawf", [P, P])
        cols = sb("cols", [P, P])
        idx_a = sb("idx_a", [P, TS], U32)
        idx_b = sb("idx_b", [P, TS], U32)
        idx_s = sb("idx_s", [P, TS], U32)
        shifted = sb("shifted", [P, TS])
        picked = sb("picked", [P, TS])
        cnt = sb("cnt", [P, TS])
        eq = sb("eq", [P, TS, P])
        rows_a = sb("rows_a", [P, TS, TR])
        rows_b = sb("rows_b", [P, TS, F])
        val = sb("val", [P, TS, F + 1])
        prod = sb("prod", [P, TS, F + 2])
        et_i = sb("et_i", [P, TS], I32)
        odd = sb("odd", [P, TS, 2])
        weight2 = sb("weight2", [P, TS, 2])
        val2 = sb("val2", [P, TS, 2, M1])
        wide = sb("wide", [P, GT, 2 * M1])
        halves = [t[:].rearrange("p t q -> p (t q)").bitcast(BF16) for t in (row_of_src, row_of_dst, eq)]
        src_bits, dst_bits, same = (h[:, 0:TS * P].rearrange("p (t q) -> p t q", q=P) for h in halves)
        parts3 = [h[:, TS * P:TS * P + TS * 2 * M1].rearrange("p (t h c) -> p t h c", h=2, c=M1) for h in halves]
        score = sb("score", [P, 4, TS])
        sums = sb("sums", [P, TS, F + 1])
        eno = sb("eno", [P, TS])
        lastrow = sb("lastrow", [P, TS, 2])
        cidx_s = sb("cidx_s", [P, 7], U32)
        cg = sb("cg", [P, 7, F])

        s_const = sem("const_ready")
        s_x = sem("x_loaded")
        s_w = sem("weights_loaded")
        s_zero = sem("tables_zeroed")
        s_zt = sem("zeros_ready")
        s_wt = sem("weight_transposed")
        s_wtc = sem("weight_copied")
        s_wp = sem("weight_products")
        s_wready = sem("table_weights_ready")
        s_v = sem("dve_steps")
        s_var = sem("variance_ready")
        s_std = sem("deviation_ready")
        s_h0 = sem("h0_ready")
        s_h0d = sem("h0_stored")
        s_rawld = [sem(f"edges_loaded{n}") for n in (0, 1)]
        s_cast = [sem(f"edges_cast{n}") for n in (0, 1)]
        s_cols = [sem(f"columns_turned{n}") for n in (0, 1)]
        s_stage = [sem(f"columns_staged{n}") for n in (0, 1)]
        s_row = [sem(f"rows_spread{n}") for n in (0, 1)]
        s_eq = [sem(f"equal_ready{n}") for n in (0, 1)]
        s_val = [sem(f"values_ready{n}") for n in (0, 1)]
        s_sum = [sem(f"sums_ready{n}") for n in (0, 1)]
        s_out = [sem(f"sums_copied{n}") for n in (0, 1)]
        s_sidx = [sem(f"scatter_index_ready{n}") for n in (0, 1)]
        s_got = [[sem(f"gathered{n}_{g}") for g in range(NG)] for n in (0, 1)]
        s_put = [[sem(f"scattered{n}_{c}") for c in range(GT)] for n in (0, 1)]
        s_lastput = [sem(f"last_scattered{c}") for c in range(GT)]
        s_dve = [sem(f"dve_edge_steps{n}") for n in (0, 1)]
        s_chk0 = sem("check_edges_set")
        s_chk = sem("check_loaded")
        s_dn = sem("next_dst_stored")
        s_bad = sem("unfit_counted_by_partition")
        s_badsum = sem("unfit_counted")
        s_flag = sem("flag_ready")
        s_winld = [sem(f"window_loaded{n}") for n in (0, 1)]
        s_cmp = [sem(f"rows_compared{n}") for n in (0, 1)]
        s_sel = [sem(f"window_rows_selected{n}") for n in (0, 1)]
        s_landed = sem("scatter_groups_landed")
        s_selectors = sem("selectors_ready")
        s_rowld = [sem(f"key_rows_loaded{n}") for n in (0, 1)]
        s_rowm = [sem(f"key_rows_masked{n}") for n in (0, 1)]
        s_rowb = [sem(f"key_rows_cast{n}") for n in (0, 1)]
        s_whi = [sem(f"window_first_part{n}") for n in (0, 1)]
        s_wrest = [sem(f"window_rest{n}") for n in (0, 1)]
        s_wmid = [sem(f"window_second_part{n}") for n in (0, 1)]
        s_wpart = [sem(f"window_parts{n}") for n in (0, 1)]
        s_hi = [sem(f"values_first_part{n}") for n in (0, 1)]
        s_rest = [sem(f"values_rest{n}") for n in (0, 1)]
        s_mid = [sem(f"values_second_part{n}") for n in (0, 1)]
        s_parts = [sem(f"values_parts{n}") for n in (0, 1)]
        s_idx = sem("gather_index_ready")
        s_wout = sem("window_sums_copied")
        s_wadd = sem("window_added")
        s_edge = [sem(f"dve_window_steps{n}") for n in (0, 1)]
        s_score = sem("score_ready")
        s_att = sem("attention_ready")
        s_gate = sem("pool_gate")
        s_agate = sem("act_gate")
        s_sgate = sem("sp_gate")
        s_part = sem("partial_sums_loaded")
        s_partused = sem("partial_sums_used")
        s_h1 = sem("h1_ready")
        s_xh = sem("source_rows_copied")
        s_hs = sem("node_rows_staged")
        s_hst = sem("node_rows_turned")
        s_hT = sem("node_rows_copied")
        s_np = sem("node_products")
        s_npc = sem("node_products_copied")
        s_tp = sem("table_products")
        s_ca = sem("chunks_free_act")
        s_cv = sem("chunks_free_dve")
        s_tst = [sem(f"table_stored{b}") for b in range(2)]
        s_nst = sem("node_tables_stored")
        s_ci = sem("self_index_ready")
        s_cg = sem("self_gathered")
        s_cgc = sem("self_copied")
        s_tail = sem("dve_last_sum_steps")
        s_done = sem("neighbours_summed")
        s_tail2 = sem("dve_tail_steps")
        s_res = sem("result_ready")
        s_fin = sem("result_stored")

        block = ctx.enter_context(nc.Block())
        NW_DMAS = 9

        def node_parts(t):
            for a, b in SPLIT:
                yield slice(a, b), J, t[a * J:b * J, :].rearrange("(p j) f -> p j f", j=J)
            yield slice(P - 1, P), tail, t[(P - 1) * J:N, :].rearrange("(p j) f -> p j f", j=tail)

        def count_from_one(eng, *sems):
            for s in sems:
                eng.sem_inc(s, ONE)

        def whole(t):
            return t.rearrange("(p j) f -> p (j f)", p=P)

        @block.sync
        def _(sp):
            with nc.allow_non_contiguous_dma(reason="small weights"):
                sp.wait_ge(s_zt, 2)
                for parts, n, dram in node_parts(x):
                    sp.dma_start(xn[parts, 0:n, :], dram).then_inc(s_x, 16)
                dst_parts = dst.rearrange("(p c) -> p c", p=P)
                dst_supers = dst.rearrange("(s c) -> s c", c=SE)
                sp.wait_ge(s_chk0, 2)
                sp.dma_start(chk[:, 0:CE], dst_parts).then_inc(s_chk, 16)
                sp.dma_start(chk[0:P - 1, CE:CE + 1], dst_parts[1:P, 0:1]).then_inc(s_chk, 16)
                sp.dma_start(ends[0:S, 0:1], dst_supers[:, 0:1]).then_inc(s_chk, 16)
                sp.dma_start(ends[0:S, 1:2], dst_supers[:, SE - 1:SE]).then_inc(s_chk, 16)
                sp.dma_start(first_dst[0:1, :], dst_supers[:, 0:1].rearrange("s c -> c s")).then_inc(s_chk, 16)
                sp.dma_start(rel_sb[:], L1_gnn_rel_emb).then_inc(s_w, 16)
                sp.dma_start(wc_sb[:], L1_gnn_w_comp).then_inc(s_w, 16)
                sp.dma_start(w_sb[:], L1_gnn_weight).then_inc(s_w, 16)
                sp.dma_start(a1[:, 0:F], L1_gnn_A1_w).then_inc(s_w, 16)
                sp.dma_start(a1[:, F:F + 1], L1_gnn_A1_b.rearrange("(a b) -> a b", b=1)).then_inc(s_w, 16)
                sp.dma_start(a2[:, 0:F], L1_gnn_A2_w).then_inc(s_w, 16)
                sp.dma_start(a2[:, F:F + 1], L1_gnn_A2_b.rearrange("(a b) -> a b", b=1)).then_inc(s_w, 16)
                sp.dma_start(NW[0:F, 2 * F:3 * F], L1_gnn_self_loop_weight).then_inc(s_w, 16)
                sp.dma_start(NW[F:F + 1, 2 * F:3 * F], zeros[0:1, 0:F]).then_inc(s_w, 16)
                sp.dma_start(h0_dram[NP:NT, :], zeros[:, 0:F]).then_inc(s_tst[0], 16)
                sp.dma_start(yh_dram[NP:NT, :], zeros[:, 0:F]).then_inc(s_tst[1], 16)
                sp.wait_ge(s_h0, 1)
                sp.dma_start(whole(h0_dram[0:NP, :]), hn[:].rearrange("p j f -> p (j f)")).then_inc(s_h0d, 16)

                def edge_rows(n, i):
                    sp.wait_ge(s_row[n], i * TS + ONE)
                    sp.sem_inc(s_sgate, 1)
                    sp.wait_ge(s_cast[n], i + ONE)
                    sp.sem_inc(s_sgate, 1)
                    rows = bass.ds(i * TS, TS)
                    sp.dma_start(raw[0:TS, :], src_rows[rows, :]).then_inc(s_rawld[n], 16)
                    sp.dma_start(raw[32:32 + TS, :], dst_rows[rows, :]).then_inc(s_rawld[n], 16)
                    if n == 0:
                        sp.dma_start(rawf[64:64 + TS, :], w_rows[rows, :]).then_inc(s_rawld[n], 16)
                    else:
                        sp.dma_start(raw[64:64 + TS, :], et_rows[rows, :]).then_inc(s_rawld[n], 16)

                sp.wait_ge(s_chk, 16 * 5)
                sp.dma_start(dst_next.rearrange("(p c) -> p c", p=P), chk[:, 1:CE + 1]).then_inc(s_dn, 16)
                sp.wait_ge(s_dn, 16)
                sp.wait_ge(s_flag, 1)
                sp.wait_ge(s_h0d, 16)
                sp.wait_ge(s_tst[0], FIRST)
                sp.wait_ge(s_tst[1], FIRST)
                unfit = sp.value_load(flag[0:1, 0:1], min_val=0, max_val=2 * P)

                def window_edges(n, k):
                    sp.wait_ge(s_cast[n], k + ONE)
                    sp.sem_inc(s_sgate, 1)
                    rows = bass.ds(k * TS, TS)
                    sp.dma_start(raw[0:TS, :], src_rows[rows, :]).then_inc(s_rawld[n], 16)
                    sp.dma_start(raw[32:32 + TS, :], dst_rows[rows, :]).then_inc(s_rawld[n], 16)
                    if n == 0:
                        sp.dma_start(wraw[0:TS, :], w_rows[rows, :]).then_inc(s_rawld[n], 16)
                    else:
                        sp.dma_start(raw[64:64 + TS, :], et_rows[rows, :]).then_inc(s_rawld[n], 16)
                        sp.dma_start(raw[96:96 + TS, :], next_rows[rows, :]).then_inc(s_rawld[n], 16)

                def key_rows(n, k):
                    sp.wait_ge(s_rowm[n], k + ONE)
                    sp.sem_inc(s_sgate, 1)
                    rows = bass.ds(k * TS, TS)
                    for q in range(0 if n == 0 else 2, 4):
                        sp.dma_start(rowi[q * 32:q * 32 + TS, :], (src_rows if q < 2 else dst_rows)[rows, :]).then_inc(s_rowld[n], 16)

                def window_load(n, i):
                    sp.wait_ge(s_wpart[n], i + ONE)
                    sp.sem_inc(s_sgate, 1)
                    d0 = sp.value_load(first_dst[0:1, bass.ds(i, 1)], min_val=0, max_val=NP - 1)
                    sp.dma_start(window[:], (h0_dram, yh_dram)[n][bass.ds(d0, P), :]).then_inc(s_winld[n], 16)

                sp.wait_ge(s_agate, 3)
                with sp.If(unfit == 0):
                    with sp.Fori(0, S) as i:
                        window_edges(0, i)
                        key_rows(0, i)
                        window_load(0, i)
                with sp.Else():
                    with sp.Fori(0, S) as i:
                        edge_rows(0, i)

                for c in range(GT):
                    for d in range(GT):
                        if c == 0:
                            sp.wait_ge(s_put[0][d], 16 * S * NG + FIRST)
                    if c:
                        sp.wait_ge(s_partused, c)
                    sp.dma_start(part_flat, whole(lap_sums[c][0:NP, :])).then_inc(s_part, 16)

                tv = table.rearrange("(p j h) c -> p j (h c)", p=P, j=J)
                with sp.Fori(0, J // 2) as i:
                    for b in range(2):
                        sp.wait_ge(s_ca, i * (2 * A_CHUNKS) + (b + 2) * A_CHUNKS)
                        sp.sem_inc(s_sgate, 1)
                        sp.wait_ge(s_cv, i * (2 * V_CHUNKS) + (b + 2) * V_CHUNKS)
                        sp.sem_inc(s_sgate, 1)
                        sp.dma_start(tv[:, bass.ds(i * 2 + b, 1), :].rearrange("p j c -> p (j c)"),
                                     tb[b][:].rearrange("p r c -> p (r c)")).then_inc(s_tst[b], 16)
                sp.wait_ge(s_npc, J + ONE)
                sp.dma_start(whole(yh_dram[0:NP, :]), yhn.rearrange("p j f -> p (j f)")).then_inc(s_nst, 16)
                sp.dma_start(whole(self_dram), sfn.rearrange("p j f -> p (j f)")).then_inc(s_nst, 16)

                def last_loads():
                    for d in range(GT):
                        sp.wait_ge(s_put[1][d], 16 * S * NG + FIRST)
                        sp.wait_ge(s_lastput[d], 16 * S * NG + FIRST)
                    for d in range(GT):
                        sp.dma_start(last_in[:, d, :, :].rearrange("p j f -> p (j f)"),
                                     whole(last_rows[d][0:NP, :])).then_inc(s_part, 16)
                    for c in range(GT):
                        sp.wait_ge(s_partused, GT + c)
                        sp.dma_start(part_flat[:, 0:J * F], whole(nei_sums[c][0:NP, :])).then_inc(s_part, 16)

                sp.wait_ge(s_nst, 32)
                with sp.If(unfit == 0):
                    window_edges(1, 0)
                    with sp.Fori(0, S - 1) as i:
                        key_rows(1, i)
                        window_load(1, i)
                        window_edges(1, i + 1)
                    key_rows(1, S - 1)
                    window_load(1, S - 1)
                    sp.wait_ge(s_wadd, 16 * S + FIRST)
                    sp.dma_start(part_flat, whole(window_sums[0:NP, :])).then_inc(s_part, 16)
                with sp.Else():
                    with sp.Fori(0, S) as i:
                        edge_rows(1, i)
                    last_loads()

                sp.wait_ge(s_res, 1)
                for parts, n, dram in node_parts(out):
                    sp.dma_start(dram, xn[parts, 0:n, :]).then_inc(s_fin, 16)
                sp.wait_ge(s_fin, 16 * 3)

        @block.gpsimd
        def _(pool):
            nc.gpsimd.memset(zeros, 0.0).then_inc(s_zt, 1)
            nc.gpsimd.memset(xn[:], 0.0).then_inc(s_zt, 1)
            pool.wait_ge(s_zt, 2)
            pool.dma_start(whole(window_sums), zeros[:, 0:NT // P * M1]).then_inc(s_wadd, 16)
            for c in range(GT):
                pool.dma_start(whole(lap_sums[c]), zeros[:, 0:NT // P * M1]).then_inc(s_put[0][c], 16)
                pool.dma_start(whole(nei_sums[c]), zeros[:, 0:NT // P * F]).then_inc(s_put[1][c], 16)
                pool.dma_start(whole(last_rows[c]), zeros[:, 0:NT // P * 2]).then_inc(s_lastput[c], 16)
            nc.gpsimd.memset(ident[:], 0.0).then_inc(s_const, 1)
            nc.gpsimd.memset(tri[:], 1.0).then_inc(s_const, 1)
            nc.gpsimd.iota(part[:], pattern=[[0, 1]], base=0, channel_multiplier=1,
                           allow_small_or_imprecise_dtypes=True).then_inc(s_const, 1)
            nc.gpsimd.iota(trash[:], pattern=[[0, 1]], base=NP, channel_multiplier=1,
                           allow_small_or_imprecise_dtypes=True).then_inc(s_const, 1)
            nc.gpsimd.iota(iota_row[:], pattern=[[1, P]], base=0, channel_multiplier=0,
                           allow_small_or_imprecise_dtypes=True).then_inc(s_const, 1)
            nc.gpsimd.iota(eno[:], pattern=[[P, TS]], base=1, channel_multiplier=1,
                           allow_small_or_imprecise_dtypes=True).then_inc(s_const, 1)
            pool.wait_ge(s_const, 6)
            nc.gpsimd.affine_select(out=ident[:], in_=ident[:], compare_op=ALU.not_equal, fill=1.0, base=0,
                                    pattern=[[-1, P]], channel_multiplier=1).then_inc(s_const, 1)
            nc.gpsimd.affine_select(out=tri[:], in_=tri[:], compare_op=ALU.is_ge, fill=0.0, base=0,
                                    pattern=[[1, P]], channel_multiplier=-1).then_inc(s_const, 1)

            pool.wait_ge(s_h0d, 16)
            pool.wait_ge(s_wadd, FIRST)
            for c in range(GT):
                pool.wait_ge(s_put[1][c], FIRST)
                pool.wait_ge(s_lastput[c], FIRST)
            pool.wait_ge(s_tst[0], FIRST)
            pool.wait_ge(s_tst[1], FIRST)
            pool.sem_inc(s_gate, 1)

            def gather(n, i, g):
                for t in range(g * GT, (g + 1) * GT):
                    if n == 0:
                        nc.gpsimd.indirect_dma_start(
                            rows_b[:, t, :], None, h0_dram,
                            bass.IndirectOffsetOnAxis(ap=idx_a[:, t:t + 1], axis=0)).then_inc(s_got[n][g], 16)
                    else:
                        nc.gpsimd.indirect_dma_start(
                            rows_a[:, t, :], None, table,
                            bass.IndirectOffsetOnAxis(ap=idx_a[:, t:t + 1], axis=0)).then_inc(s_got[n][g], 16)
                        nc.gpsimd.indirect_dma_start(
                            rows_b[:, t, :], None, yh_dram,
                            bass.IndirectOffsetOnAxis(ap=idx_b[:, t:t + 1], axis=0)).then_inc(s_got[n][g], 16)

            def scatter(n, i, g):
                pool.wait_ge(s_out[n], i * NG + (g + 1) + ONE)
                pool.wait_ge(s_sidx[n], i * NG + (g + 1))
                for c in range(GT):
                    pool.wait_ge(s_put[n][c], i * (16 * NG) + 16 * g + FIRST)
                    if n:
                        pool.wait_ge(s_lastput[c], i * (16 * NG) + 16 * g + FIRST)
                pool.sem_inc(s_gate, 1)
                for c in range(GT):
                    t = g * GT + c
                    to = bass.IndirectOffsetOnAxis(ap=idx_s[:, t:t + 1], axis=0)
                    if n == 0:
                        nc.gpsimd.indirect_dma_start(lap_sums[c], to, sums[:, t, :], None,
                                                     compute_op=ALU.add).then_inc(s_put[n][c], 16)
                    else:
                        nc.gpsimd.indirect_dma_start(nei_sums[c], to, sums[:, t, 0:F], None,
                                                     compute_op=ALU.add).then_inc(s_put[n][c], 16)
                        nc.gpsimd.indirect_dma_start(last_rows[c], to, lastrow[:, t, :],
                                                     None).then_inc(s_lastput[c], 16)

            def edge_turn(n, i):
                pool.wait_ge(s_stage[n], i + 1 + ONE)
                pool.sem_inc(s_gate, 1)
                gather(n, i, 0)
                for g in range(NG):
                    if g + 1 < NG:
                        gather(n, i, g + 1)
                    scatter(n, i, g)

            def window_scatter(i, g):
                pool.wait_ge(s_out[0], i * NG + (g + 1 + ONE))
                pool.wait_ge(s_sidx[0], i * NG + (g + 1))
                pool.sem_inc(s_gate, 1)
                for c in range(GT):
                    t = g * GT + c
                    pool.wait_ge(s_put[0][c], i * (16 * NG) + (16 * g + FIRST))
                    pool.sem_inc(s_landed if c == GT - 1 else s_gate, 1)
                    nc.gpsimd.indirect_dma_start(lap_sums[c], bass.IndirectOffsetOnAxis(ap=idx_s[:, t:t + 1], axis=0),
                                                 sums[:, t, :], None, compute_op=ALU.add).then_inc(s_put[0][c], 16)

            def table_gather(i, g):
                pool.wait_ge(s_idx, i * NG + (g + 1))
                pool.sem_inc(s_gate, 1)
                for t in range(g * GT, (g + 1) * GT):
                    nc.gpsimd.indirect_dma_start(
                        rows_a[:, t, :], None, table,
                        bass.IndirectOffsetOnAxis(ap=idx_a[:, t:t + 1], axis=0)).then_inc(s_got[1][g], 16)

            def window_add(k):
                pool.wait_ge(s_wout, k + (1 + ONE))
                pool.sem_inc(s_gate, 1)
                pool.wait_ge(s_wadd, k * 16 + FIRST)
                pool.sem_inc(s_gate, 1)
                d0 = pool.value_load(first_dst[0:1, bass.ds(k, 1)], min_val=0, max_val=NP - 1)
                pool.dma_start(window_sums[bass.ds(d0, P), :], win_sb[:], accum_op=ALU.add).then_inc(s_wadd, 16)

            def gather_turn(i, first=False):
                for g in range(NG):
                    table_gather(i, g)
                    if g == 2 and not first:
                        window_add(i - 1)

            pool.wait_ge(s_flag, 1)
            unfit = pool.value_load(flag[0:1, 0:1], min_val=0, max_val=2 * P)
            with pool.If(unfit == 0):
                pool.sem_inc(s_landed, NG - 1)
                with pool.Fori(0, S) as i:
                    for g in range(NG):
                        window_scatter(i, g)
            with pool.Else():
                with pool.Fori(0, S) as i:
                    edge_turn(0, i)
            for b in range(2):
                pool.wait_ge(s_tst[b], 16 * (J // 2) + FIRST)
            pool.wait_ge(s_nst, 32)
            pool.sem_inc(s_gate, 1)
            with pool.If(unfit == 0):
                gather_turn(0, first=True)
                with pool.Fori(1, S) as i:
                    gather_turn(i)
                window_add(S - 1)
            with pool.Else():
                with pool.Fori(0, S) as i:
                    edge_turn(1, i)

            with pool.Fori(0, J // 7) as i:
                pool.wait_ge(s_ci, i + 1)
                pool.sem_inc(s_gate, 1)
                for t in range(7):
                    nc.gpsimd.indirect_dma_start(
                        cg[:, t, :], None, self_dram,
                        bass.IndirectOffsetOnAxis(ap=cidx_s[:, t:t + 1], axis=0)).then_inc(s_cg, 16)

        @block.scalar
        def _(act):
            count_from_one(act, *s_rowb, *s_cast, *s_out, s_hT, s_npc, s_wout)

            def deviation(n):
                act.wait_ge(s_var, n + 1)
                nc.scalar.activation(stat[:, 2, :], stat[:, 1, :], ACT.Sqrt).then_inc(s_std, 1)

            def edge_turn(n, i):
                act.wait_ge(s_rawld[n], i * 48 + 48)
                act.sem_inc(s_agate, 1)
                rows = 64 if n == 0 else 96
                nc.scalar.copy(rawf[0:rows, :], raw[0:rows, :]).then_inc(s_cast[n], 1)
                for g in range(NG):
                    a, b = g * GT, (g + 1) * GT
                    if n == 1:
                        act.wait_ge(s_score, i * NG + (g + 1))
                        act.sem_inc(s_agate, 1)
                        nc.scalar.activation(score[:, 2, a:b], score[:, 1, a:b], ACT.Tanh,
                                             scale=float(F) ** -0.5).then_inc(s_att, 1)
                    act.wait_ge(s_sum[n], i * TS + (g + 1) * GT)
                    act.sem_inc(s_agate, 1)
                    o = (g // 2) * GT * M1
                    width = M1 if n == 0 else F
                    nc.scalar.copy(sums[:, a:b, 0:width], sum_ps[g % 2][:, o:o + GT * M1].rearrange(
                        "p (t f) -> p t f", f=M1)[:, :, 0:width]).then_inc(s_out[n], 1)

            act.wait_ge(s_zt, 2)
            nc.scalar.copy(raw[:], zeros[:, 0:P]).then_inc(s_agate, 1)
            nc.scalar.copy(rawf[:], zeros[:, 0:P]).then_inc(s_agate, 1)
            nc.scalar.copy(rowi[:], zeros[:, 0:P]).then_inc(s_agate, 1)
            deviation(0)
            act.wait_ge(s_agate, 3)
            def start_turn(n, i):
                act.wait_ge(s_rowm[n], i + (1 + ONE))
                act.wait_ge(s_row[n], i * TS + ONE)
                act.sem_inc(s_agate, 1)
                nc.scalar.copy(rowb[:], rowm[:]).then_inc(s_rowb[n], 1)
                act.wait_ge(s_winld[n], i * 16 + 16)
                act.wait_ge(s_sel[n], i * TS + ONE)
                act.sem_inc(s_agate, 1)
                nc.scalar.copy(window3[:, 0, :], window[:]).then_inc(s_whi[n], 1)
                act.wait_ge(s_wrest[n], i + 1)
                act.sem_inc(s_agate, 1)
                nc.scalar.copy(window3[:, 1, :], wide_window[:]).then_inc(s_wmid[n], 1)

            def first_part(n, i, g):
                act.wait_ge(s_val[n], i * NG + (g + 1 + ONE))
                act.sem_inc(s_agate, 1)
                c = 1 + n
                nc.scalar.copy(parts3[0][:, g * GT:(g + 1) * GT, 0:c, :], val2[:, g * GT:(g + 1) * GT, 0:c, :]).then_inc(s_hi[n], 1)

            def second_part(n, i, g):
                act.wait_ge(s_rest[n], i * NG + (g + 1))
                act.sem_inc(s_agate, 1)
                c = 1 + n
                nc.scalar.copy(parts3[1][:, g * GT:(g + 1) * GT, 0:c, :],
                               wide[:, :, 0:c * M1].rearrange("p t (h c) -> p t h c", c=M1)).then_inc(s_mid[n], 1)

            def window_turn0(i):
                act.wait_ge(s_rawld[0], i * 48 + 48)
                act.wait_ge(s_cols[0], i + ONE)
                act.sem_inc(s_agate, 1)
                nc.scalar.copy(rawf[0:64, :], raw[0:64, :]).then_inc(s_agate, 1)
                nc.scalar.copy(rawf[64:64 + TS, :], wraw[0:TS, :]).then_inc(s_cast[0], 1)
                start_turn(0, i)
                for g in range(NG):
                    first_part(0, i, g)
                    second_part(0, i, g)
                    act.wait_ge(s_landed, i * NG + (g + 1))
                    act.wait_ge(s_sum[0], i * NG + (g + 1 + NG))
                    act.sem_inc(s_agate, 1)
                    nc.scalar.copy(sums[:, g * GT:(g + 1) * GT, :], sum_ps[g % 2][:, 0:GT * M1].rearrange(
                        "p (t f) -> p t f", f=M1)).then_inc(s_out[0], 1)

            def cast1(k):
                act.wait_ge(s_rawld[1], k * 64 + 64)
                act.sem_inc(s_agate, 1)
                nc.scalar.copy(rawf[:], raw[:]).then_inc(s_cast[1], 1)

            def window_out(k):
                act.wait_ge(s_sum[1], k * NG + 2 * NG)
                act.wait_ge(s_wadd, k * 16 + FIRST)
                act.sem_inc(s_agate, 1)
                nc.scalar.copy(win_sb[:], banks[1][:, 0:M1]).then_inc(s_wout, 1)

            def window_turn1(i, first=False, last=False):
                start_turn(1, i)
                if not last:
                    act.wait_ge(s_cols[1], i + (1 + ONE))
                    act.sem_inc(s_agate, 1)
                    cast1(i + 1)
                for g in range(NG):
                    act.wait_ge(s_score, i * NG + (g + 1))
                    act.sem_inc(s_agate, 1)
                    nc.scalar.activation(score[:, 2, g * GT:(g + 1) * GT], score[:, 1, g * GT:(g + 1) * GT], ACT.Tanh,
                                         scale=float(F) ** -0.5).then_inc(s_att, 1)
                    if g == 0 and not first:
                        window_out(i - 1)
                    first_part(1, i, g)
                    second_part(1, i, g)

            act.wait_ge(s_flag, 1)
            unfit = act.value_load(flag[0:1, 0:1], min_val=0, max_val=2 * P)
            with act.If(unfit == 0):
                with act.Fori(0, S) as i:
                    window_turn0(i)
            with act.Else():
                with act.Fori(0, S) as i:
                    edge_turn(0, i)
            deviation(1)
            act.wait_ge(s_wready, 1)
            act.sem_inc(s_ca, A_CHUNKS)
            with act.Fori(0, J // 2) as i:
                for b in range(2):
                    j = i * 2 + b
                    act.wait_ge(s_hst, j + 1 + ONE)
                    act.sem_inc(s_agate, 1)
                    nc.scalar.copy(hT[0:F, b, :], turn_ps[0:F, 0:P]).then_inc(s_hT, 1)
                    act.wait_ge(s_xh, j + 1 + ONE)
                    act.sem_inc(s_agate, 1)
                    nc.scalar.copy(yhn[:, bass.ds(j, 1), :].rearrange("p j f -> p (j f)"),
                                   nrow[:, b, F:2 * F]).then_inc(s_agate, 1)
                    nc.scalar.copy(sfn[:, bass.ds(j, 1), :].rearrange("p j f -> p (j f)"),
                                   nrow[:, b, 2 * F:3 * F]).then_inc(s_npc, 1)
                    act.wait_ge(s_tst[b], i * 16 + FIRST)
                    for q, (r, n) in enumerate(CHUNKS):
                        if q % 2:
                            continue
                        act.wait_ge(s_tp, i * (2 * len(CHUNKS)) + (b * len(CHUNKS) + q + 1))
                        act.sem_inc(s_agate, 1)
                        ins = nc.scalar.copy(tb[b][:, r // 2:(r + n) // 2, 0:2 * M1],
                                             chunk_ps[q][:, 0:n * M1].rearrange("p (h c) -> p h c", c=2 * M1))
                        ins.then_inc(s_ca, 1)
            with act.If(unfit == 0):
                cast1(0)
                window_turn1(0, first=True)
                with act.Fori(1, S - 1) as i:
                    window_turn1(i)
                window_turn1(S - 1, last=True)
                window_out(S - 1)
            with act.Else():
                with act.Fori(0, S) as i:
                    edge_turn(1, i)

        @block.tensor
        def _(pe):
            count_from_one(pe, *s_row, s_hst, *s_sel, *s_cols)
            pe.wait_ge(s_const, 8)
            pe.wait_ge(s_w, 16 * NW_DMAS)
            nc.tensor.transpose(banks[0][0:F, 0:R], rel_sb[:], ident[0:R, 0:R])
            nc.tensor.transpose(banks[1][0:B, 0:R], wc_sb[:], ident[0:R, 0:R])
            nc.tensor.matmul(banks[2][0:F + 1, 0:F], a1[:], ident[0:F, 0:F], start=True, stop=True)
            nc.tensor.matmul(banks[3][0:F + 1, 0:F], a2[:], ident[0:F, 0:F], start=True, stop=True).then_inc(s_wt, 1)
            pe.wait_ge(s_wtc, 1)
            for q in range(7):
                k = 5 if q < 6 else 2
                if q >= 1:
                    pe.wait_ge(s_wtc, q + 1)
                for m in range(k):
                    o = q * 5 + m
                    ins = nc.tensor.matmul(banks[q % 2][0:F, m * R:(m + 1) * R], w_sb[:, :, o], wcT[:],
                                           start=True, stop=True)
                ins.then_inc(s_wp, 1)
            nc.tensor.matmul(banks[2][0:F + 1, 0:R], a1[:], relT[:], start=True, stop=True).then_inc(s_wp, 1)

            def edge_turn(n, i):
                pe.wait_ge(s_cast[n], i + 1 + ONE)
                pe.wait_ge(s_rawld[n], i * 48 + 48)
                pe.wait_ge(s_stage[n], i + ONE)
                nc.tensor.transpose(cols_ps[:, 0:P], rawf[:], ident[:]).then_inc(s_cols[n], 1)
                key = 0 if n == 0 else 32
                width = M1 if n == 0 else F
                for t in range(TS):
                    pe.wait_ge(s_eq[n], i * TS + max(t - 1, 0) + ONE)
                    nc.tensor.matmul(row_ps[t % 2], (row_of_dst if n else row_of_src)[:, t, :], rawf[:],
                                     start=True, stop=True).then_inc(s_row[n], 1)
                    if t >= GT - 1 and t % GT == GT - 1:
                        g = t // GT
                        pe.wait_ge(s_eq[n], i * TS + (t + 1) + ONE)
                        pe.wait_ge(s_val[n], i * NG + (g + 1))
                        pe.wait_ge(s_out[n], i * NG + max(g - 1, 0) + ONE)
                        for c in range(GT):
                            o = (g // 2) * GT * M1 + c * M1
                            k = g * GT + c
                            if n == 0:
                                ins = nc.tensor.matmul(sum_ps[g % 2][:, o:o + M1], eq[:, k, :], val[:, k, :],
                                                       start=True, stop=True)
                            else:
                                for h in range(2):
                                    ins = nc.tensor.matmul(sum_ps[g % 2][:, o:o + F], eq[:, k, :], val2[:, k, h, 0:F],
                                                           start=h == 0, stop=h == 1)
                            ins.then_inc(s_sum[n], 1)

            def spread(n, i, t):
                pe.wait_ge(s_cmp[n], i * TS + (max(t - 1, 0) + ONE))
                if n == 0:
                    nc.tensor.matmul(row_ps[t % 2], src_bits[:, t, :], rowb[:], start=True, stop=True)
                    nc.tensor.matmul(banks[3 + t % 2][:, P:2 * P], dst_bits[:, t, :], rowb[:],
                                     start=True, stop=True).then_inc(s_row[n], 1)
                else:
                    nc.tensor.matmul(row_ps[t % 2], dst_bits[:, t, :], rowb[:],
                                     start=True, stop=True).then_inc(s_row[n], 1)

            def select(n, i, t):
                g = t // GT
                pe.wait_ge(s_cmp[n], i * TS + (t + 1 + ONE))
                if t == 0:
                    pe.wait_ge(s_wpart[n], i + (1 + ONE))
                if t % GT == 0:
                    pe.wait_ge(s_val[n], i * NG + (max(g - 1, 0) + ONE))
                for q in range(3):
                    ins = nc.tensor.matmul(banks[5 + g % 2][:, (t % GT) * F:(t % GT + 1) * F], at_window[:, t % GT, :],
                                           window3[:, q, :], start=q == 0, stop=q == 2)
                ins.then_inc(s_sel[n], 1)

            def turn_columns(n, k):
                pe.wait_ge(s_cast[n], k + (1 + ONE))
                pe.wait_ge(s_stage[n], k + ONE)
                nc.tensor.transpose(cols_ps[:, 0:P], rawf[:], ident[:]).then_inc(s_cols[n], 1)

            def group_sums(i, g):
                pe.wait_ge(s_parts[0], i * NG + (g + 1))
                pe.wait_ge(s_out[0], i * NG + (max(g - 1, 0) + ONE))
                for c in range(GT):
                    k = g * GT + c
                    for q in range(3):
                        ins = nc.tensor.matmul(sum_ps[g % 2][:, c * M1:(c + 1) * M1], same[:, k, :], parts3[q][:, k, 0, :],
                                               start=q == 0, stop=q == 2)
                ins.then_inc(s_sum[0], 1)

            def window_sum(i, g):
                pe.wait_ge(s_parts[1], i * NG + (g + 1))
                if g == 0:
                    pe.wait_ge(s_wout, i + ONE)
                for k in range(g * GT, (g + 1) * GT):
                    for q, h in ((q, h) for q in range(3) for h in range(2)):
                        ins = nc.tensor.matmul(banks[1][:, 0:M1], same[:, k, :], parts3[q][:, k, h, :],
                                               start=k == 0 and q + h == 0, stop=k == TS - 1 and q + h == 3)
                ins.then_inc(s_sum[1], 1)

            def window_turn(n, i, last=False):
                if n == 0:
                    turn_columns(0, i)
                pe.wait_ge(s_rowb[n], i + (1 + ONE))
                for t in range(TS + 1):
                    if t < TS:
                        spread(n, i, t)
                    if t >= 1:
                        select(n, i, t - 1)
                    if n == 1 and t == 1 and not last:
                        turn_columns(1, i + 1)
                    if t >= GT + DELAY[n] and (t - DELAY[n]) % GT == 0:
                        (group_sums if n == 0 else window_sum)(i, (t - DELAY[n]) // GT - 1)
                (group_sums if n == 0 else window_sum)(i, NG - 1)

            pe.wait_ge(s_bad, 1)
            nc.tensor.matmul(banks[5][0:1, 0:1], odds[:, 2:3], tri[:, P - 1:P], start=True, stop=True).then_inc(s_badsum, 1)
            pe.wait_ge(s_const, 9)
            pe.wait_ge(s_flag, 1)
            unfit = pe.value_load(flag[0:1, 0:1], min_val=0, max_val=2 * P)
            with pe.If(unfit == 0):
                pe.sem_inc(s_sum[0], NG)
                pe.wait_ge(s_selectors, 1)
                with pe.Fori(0, S) as i:
                    window_turn(0, i)
            with pe.Else():
                with pe.Fori(0, S) as i:
                    edge_turn(0, i)

            pe.wait_ge(s_wready, 1)
            with pe.Fori(0, J // 2) as i:
                for b in range(2):
                    j = i * 2 + b
                    pe.wait_ge(s_hs, j + 1)
                    pe.wait_ge(s_hT, j + ONE)
                    pe.wait_ge(s_ca, i * (2 * A_CHUNKS) + (b + 1) * A_CHUNKS)
                    nc.tensor.transpose(turn_ps[0:F, 0:P], hs[:, b, :], ident[:]).then_inc(s_hst, 1)
                    pe.wait_ge(s_hT, j + 1 + ONE)
                    pe.wait_ge(s_xh, j + ONE)
                    nc.tensor.matmul(node_ps[:, 0:3 * F], hT[:, b, :], NW[:], start=True, stop=True).then_inc(s_np, 1)
                    for q, (r, n) in enumerate(CHUNKS):
                        if q % 2 == 0:
                            pe.wait_ge(s_ca, i * (2 * A_CHUNKS) + (b * A_CHUNKS + q // 2 + 1))
                        else:
                            pe.wait_ge(s_cv, i * (2 * V_CHUNKS) + (b * V_CHUNKS + q // 2 + 1))
                        nc.tensor.matmul(chunk_ps[q][:, 0:n * M1], hT[:, b, :],
                                         TW[:, r:r + n, :].rearrange("p r c -> p (r c)"),
                                         start=True, stop=True).then_inc(s_tp, 1)
            with pe.If(unfit == 0):
                pe.sem_inc(s_sum[1], NG)
                turn_columns(1, 0)
                with pe.Fori(0, S - 1) as i:
                    window_turn(1, i)
                window_turn(1, S - 1, last=True)
            with pe.Else():
                with pe.Fori(0, S) as i:
                    edge_turn(1, i)

        @block.vector
        def _(dve):
            count_from_one(dve, *s_stage, *s_eq, s_xh, *s_cmp, *s_rowm, *s_wpart)
            steps = Steps(dve, s_v)

            def bc(a):
                return a.unsqueeze(2).broadcast_to([P, J, F])

            def layer_norm(n):
                steps.done(nc.vector.tensor_reduce(stat[:, 0, :], xn[:], AX_X, ALU.add))
                steps.done(nc.vector.tensor_scalar(stat[:, 1, :], stat[:, 0, :], 1.0 / F, None, ALU.mult))
                steps.done(nc.vector.tensor_tensor(hn[:], xn[:], bc(stat[:, 1, :]), ALU.subtract))
                steps.done(nc.vector.tensor_tensor(sq[:], hn[:], hn[:], ALU.mult))
                steps.done(nc.vector.tensor_reduce(stat[:, 0, :], sq[:], AX_X, ALU.add))
                nc.vector.tensor_scalar(stat[:, 1, :], stat[:, 0, :], 1.0 / F, EPS, ALU.mult, ALU.add).then_inc(s_var, 1)
                dve.wait_ge(s_std, n + 1)
                steps.done(nc.vector.reciprocal(stat[:, 3, :], stat[:, 2, :]))
                steps.done(nc.vector.tensor_tensor(hn[:], hn[:], bc(stat[:, 3, :]), ALU.mult))
                nc.vector.tensor_scalar(hn[:], hn[:], 0.0, None, ALU.max).then_inc(s_h1 if n else s_h0, 1)

            nc.vector.memset(chk[:, CE:CE + 1], 1 << 20).then_inc(s_chk0, 1)
            nc.vector.memset(ends[:], 0).then_inc(s_chk0, 1)
            dve.wait_ge(s_x, 48)
            layer_norm(0)

            dve.wait_ge(s_chk, 16 * 5)
            steps.done(nc.vector.tensor_tensor(rises, chk[:, 1:CE + 1], chk[:, 0:CE], ALU.subtract))
            steps.done(nc.vector.tensor_reduce(odds[:, 0:1], rises, AX_X, ALU.min))
            steps.done(nc.vector.tensor_tensor(odds[:, 1:2], ends[:, 1:2], ends[:, 0:1], ALU.subtract))
            steps.done(nc.vector.tensor_scalar(odds[:, 0:1], odds[:, 0:1], 0.0, None, ALU.is_lt))
            steps.done(nc.vector.tensor_scalar(odds[:, 1:2], odds[:, 1:2], float(P - 1), None, ALU.is_gt))
            nc.vector.tensor_tensor(odds[:, 2:3], odds[:, 0:1], odds[:, 1:2], ALU.add).then_inc(s_bad, 1)

            dve.wait_ge(s_wt, 1)
            nc.vector.tensor_copy(NW[:, 0:F], banks[2][0:F + 1, 0:F]).then_inc(s_v, 1)
            nc.vector.tensor_copy(NW[:, F:2 * F], banks[3][0:F + 1, 0:F]).then_inc(s_v, 1)
            nc.vector.tensor_copy(relT[:], banks[0][0:F, 0:R]).then_inc(s_v, 1)
            steps.n += 3
            nc.vector.tensor_copy(wcT[:], banks[1][0:B, 0:R]).then_inc(s_v, 1)
            steps.n += 1
            nc.vector.memset(TW[F:F + 1, :, 0:F], 0.0).then_inc(s_v, 1)
            steps.n += 1
            dve.wait_ge(s_v, steps.value())
            nc.vector.memset(hT[F:F + 1, :, :], 1.0).then_inc(s_wtc, 1)
            for q in range(7):
                k = 5 if q < 6 else 2
                dve.wait_ge(s_wp, q + 1)
                nc.vector.tensor_copy(TW[0:F, :, q * 5:q * 5 + k],
                                      banks[q % 2][0:F, 0:k * R].rearrange("p (o r) -> p r o", o=k)).then_inc(s_wtc, 1)
            dve.wait_ge(s_wp, 8)
            dve.wait_ge(s_wtc, 8)
            nc.vector.tensor_copy(TW[:, :, F:F + 1], banks[2][0:F + 1, 0:R].unsqueeze(2)).then_inc(s_wready, 1)
            dve.wait_ge(s_const, 8)
            nc.vector.tensor_copy(row_of_src[:], ident[:, 0:TS].unsqueeze(2).broadcast_to([P, TS, P])).then_inc(s_v, 1)
            nc.vector.tensor_copy(row_of_dst[:], ident[:, 32:32 + TS].unsqueeze(2).broadcast_to([P, TS, P])).then_inc(s_const, 1)
            steps.n += 1

            def edge_turn(n, i, per_turn):
                steps = Steps(dve, s_dve[n], i, per_turn)
                key = 0 if n == 0 else 32
                for c in range(GT):
                    dve.wait_ge(s_put[n][c], i * (16 * NG) + FIRST)
                    if n:
                        dve.wait_ge(s_lastput[c], i * (16 * NG) + FIRST)
                dve.wait_ge(s_cols[n], i + (1 + ONE))
                steps.done(nc.vector.tensor_copy(cols[:], cols_ps[:, 0:P]))
                kcols = cols[:, key:key + TS]
                if n == 0:
                    steps.done(nc.vector.tensor_copy(idx_a[:], cols[:, 32:32 + TS]))
                else:
                    steps.done(nc.vector.tensor_copy(et_i[:], cols[:, 64:64 + TS]))
                    steps.done(nc.vector.tensor_scalar(et_i[:], et_i[:], 1, None, ALU.bitwise_and))
                    steps.done(nc.vector.tensor_copy(odd[:, :, 1:2], et_i[:].unsqueeze(2)))
                    steps.done(nc.vector.tensor_scalar(odd[:, :, 0:1], odd[:, :, 1:2], -1.0, 1.0, ALU.mult, ALU.add))
                    steps.done(nc.vector.scalar_tensor_tensor(out=picked[:], in0=cols[:, 0:TS], scalar=float(R),
                                                              in1=cols[:, 64:64 + TS], op0=ALU.mult, op1=ALU.add))
                    steps.done(nc.vector.tensor_tensor(picked[:].unsqueeze(2), picked[:].unsqueeze(2), odd[:, :, 1:2], ALU.subtract))
                    steps.done(nc.vector.tensor_scalar(idx_a[:], picked[:], 0.5, None, ALU.mult))
                    steps.done(nc.vector.tensor_copy(idx_b[:], cols[:, 32:32 + TS]))
                    steps.done(nc.vector.tensor_copy(lastrow[:, :, 0:1], eno[:].unsqueeze(2)))
                    steps.done(nc.vector.tensor_scalar(lastrow[:, :, 1:2], cols[:, 0:TS].unsqueeze(2), 1.0, None, ALU.add))
                    steps.done(nc.vector.tensor_scalar(eno[:], eno[:], float(SE), None, ALU.add))
                nc.vector.tensor_scalar(shifted[:], kcols, trash[:, 0:1], None, ALU.subtract).then_inc(s_stage[n], 1)
                for g in range(NG):
                    a, b = g * GT, (g + 1) * GT
                    for t in range(a, b):
                        dve.wait_ge(s_row[n], i * TS + (t + 1) + ONE)
                        nc.vector.scalar_tensor_tensor(out=eq[:, t, :], in0=row_ps[t % 2],
                                                       scalar=cols[:, key + t:key + t + 1], in1=tri[:],
                                                       op0=ALU.is_equal, op1=ALU.mult,
                                                       accum_out=cnt[:, t:t + 1]).then_inc(s_eq[n], 1)
                    dve.wait_ge(s_eq[n], i * TS + b + ONE)
                    dve.wait_ge(s_stage[n], i + 1 + ONE)
                    steps.done(nc.vector.scalar_tensor_tensor(out=picked[:, a:b], in0=cnt[:, a:b], scalar=1.0,
                                                              in1=shifted[:, a:b], op0=ALU.is_equal, op1=ALU.mult))
                    nc.vector.tensor_scalar(idx_s[:, a:b], picked[:, a:b], trash[:, 0:1], None,
                                            ALU.add).then_inc(s_sidx[n], 1)
                    dve.wait_ge(s_got[n][g], i * (16 * GT * (n + 1)) + 16 * GT * (n + 1))
                    if n == 0:
                        w = cols[:, 64 + a:64 + b].unsqueeze(2)
                        steps.done(nc.vector.tensor_copy(val[:, a:b, F:F + 1], w))
                        nc.vector.tensor_tensor(val[:, a:b, 0:F], rows_b[:, a:b, :], w.broadcast_to([P, GT, F]),
                                                ALU.mult).then_inc(s_val[n], 1)
                    else:
                        pair = rows_a[:, a:b, 0:2 * M1].rearrange("p t (h c) -> p t h c", h=2)
                        steps.done(nc.vector.tensor_tensor(prod[:, a:b, 0:F], rows_a[:, a:b, 2 * M1:TR], rows_b[:, a:b, :], ALU.mult))
                        steps.done(nc.vector.tensor_tensor(prod[:, a:b, F:F + 2].unsqueeze(3), pair[:, :, :, F:M1],
                                                           odd[:, a:b, :].unsqueeze(3), ALU.mult))
                        steps.done(nc.vector.tensor_reduce(score[:, 0, a:b], prod[:, a:b, :], AX_X, ALU.add))
                        nc.vector.tensor_scalar(score[:, 1, a:b], score[:, 0, a:b], 0.0, None, ALU.max).then_inc(s_score, 1)
                        dve.wait_ge(s_att, i * NG + (g + 1))
                        steps.done(nc.vector.scalar_tensor_tensor(out=weight2[:, a:b, :], in0=score[:, 2, a:b].unsqueeze(2).broadcast_to([P, GT, 2]),
                                                                  scalar=0.0, in1=odd[:, a:b, :], op0=ALU.max, op1=ALU.mult))
                        nc.vector.tensor_tensor(val2[:, a:b, :, 0:F], pair[:, :, :, 0:F],
                                                weight2[:, a:b, :].unsqueeze(3).broadcast_to([P, GT, 2, F]),
                                                ALU.mult).then_inc(s_val[n], 1)
                assert steps.n == per_turn, steps.n

            def compare(n, i, t, chain):
                dve.wait_ge(s_row[n], i * TS + (t + 1 + ONE))
                dst_ps = banks[3 + t % 2][:, P:2 * P] if n == 0 else row_ps[t % 2]
                if t == 0:
                    chain.done(nc.vector.tensor_copy(base[:, 0:1], dst_ps[:, 0:1]))
                    chain.done(nc.vector.tensor_scalar(base[:, 1:2], base[:, 0:1], part[:, 0:1], None, ALU.add))
                    if n:
                        chain.done(nc.vector.tensor_scalar(in_window[:], cols[:, 32:32 + TS], base[:, 0:1], None, ALU.subtract))
                dve.wait_ge(s_sel[n], i * TS + (max(t - GT + 1, 0) + ONE))
                if t % GT == 0:
                    dve.wait_ge(s_sum[n], i * NG + (t // GT + 1))
                ins = nc.vector.tensor_scalar(at_window[:, t % GT, :], dst_ps, base[:, 1:2], None, ALU.is_equal)
                if n == 0:
                    ins
                    nc.vector.scalar_tensor_tensor(out=same[:, t, :], in0=row_ps[t % 2], scalar=cols[:, t:t + 1], in1=tri[:],
                                                   op0=ALU.is_equal, op1=ALU.mult,
                                                   accum_out=cnt[:, t:t + 1]).then_inc(s_cmp[n], 1)
                else:
                    ins.then_inc(s_cmp[n], 1)
                    nc.vector.tensor_scalar(same[:, t, :], iota_row[:], in_window[:, t:t + 1], None, ALU.is_equal)

            def start_turn(n, i):
                dve.wait_ge(s_rowld[n], i * (64 // (1 + n)) + 64 // (1 + n))
                dve.wait_ge(s_rowb[n], i + ONE)
                nc.vector.tensor_scalar(rowm[:], rowi[:], row_mask[:, 0:1], None, ALU.bitwise_and).then_inc(s_rowm[n], 1)

            def window_parts(n, i):
                dve.wait_ge(s_whi[n], i + 1)
                nc.vector.tensor_tensor(wide_window[:], window[:], window3[:, 0, :], ALU.subtract).then_inc(s_wrest[n], 1)
                dve.wait_ge(s_wmid[n], i + 1)
                dve.wait_ge(s_wrest[n], i + 1)
                nc.vector.tensor_tensor(window3[:, 2, :], wide_window[:], window3[:, 1, :], ALU.subtract).then_inc(s_wpart[n], 1)

            def rest(n, i, g):
                c = 1 + n
                dve.wait_ge(s_hi[n], i * NG + (g + 1))
                nc.vector.tensor_tensor(wide[:, :, 0:c * M1].rearrange("p t (h c) -> p t h c", c=M1), val2[:, g * GT:(g + 1) * GT, 0:c, :],
                                        parts3[0][:, g * GT:(g + 1) * GT, 0:c, :], ALU.subtract).then_inc(s_rest[n], 1)

            def third_part(n, i, g):
                c = 1 + n
                dve.wait_ge(s_mid[n], i * NG + (g + 1))
                dve.wait_ge(s_rest[n], i * NG + (g + 1))
                nc.vector.tensor_tensor(parts3[2][:, g * GT:(g + 1) * GT, 0:c, :], wide[:, :, 0:c * M1].rearrange("p t (h c) -> p t h c", c=M1),
                                        parts3[1][:, g * GT:(g + 1) * GT, 0:c, :], ALU.subtract).then_inc(s_parts[n], 1)

            def values0(i, g, chain):
                a, b = g * GT, (g + 1) * GT
                w = cols[:, 64 + a:64 + b].unsqueeze(2)
                dve.wait_ge(s_cmp[0], i * TS + (b + ONE))
                chain.done(nc.vector.scalar_tensor_tensor(out=picked[:, a:b], in0=cnt[:, a:b], scalar=1.0,
                                                          in1=shifted[:, a:b], op0=ALU.is_equal, op1=ALU.mult))
                dve.wait_ge(s_landed, i * NG + (g + 1))
                nc.vector.tensor_scalar(idx_s[:, a:b], picked[:, a:b], trash[:, 0:1], None, ALU.add).then_inc(s_sidx[0], 1)
                dve.wait_ge(s_sel[0], i * TS + (b + ONE))
                nc.vector.tensor_copy(val2[:, a:b, 0, F:M1], w)
                nc.vector.tensor_tensor(val2[:, a:b, 0, 0:F], banks[5 + g % 2][:, 0:GT * F].rearrange("p (t f) -> p t f", f=F),
                                        w.broadcast_to([P, GT, F]), ALU.mult).then_inc(s_val[0], 1)

            def window_turn0(i):
                chain = Steps(dve, s_edge[0], i, 9)
                start_turn(0, i)
                dve.wait_ge(s_cols[0], i + (1 + ONE))
                chain.done(nc.vector.tensor_copy(cols[:], cols_ps[:, 0:P]))
                chain.done(nc.vector.tensor_scalar(shifted[:], cols[:, 0:TS], trash[:, 0:1], None, ALU.subtract))
                dve.sem_inc(s_stage[0], 1)
                for t in range(TS):
                    compare(0, i, t, chain)
                    if t == 0:
                        window_parts(0, i)
                    if t > GT and t % GT == 1:
                        values0(i, t // GT - 1, chain)
                    if t > GT and t % GT == 2:
                        rest(0, i, t // GT - 1)
                    if t > GT and t % GT == 3:
                        third_part(0, i, t // GT - 1)
                values0(i, NG - 1, chain)
                rest(0, i, NG - 1)
                third_part(0, i, NG - 1)
                assert chain.n == chain.per_turn, chain.n

            def stage1(chain):
                chain.done(nc.vector.tensor_copy(cols_next[:], cols_ps[:, 0:P]))
                dve.sem_inc(s_stage[1], 1)
                chain.done(nc.vector.tensor_copy(et_i[:], cols_next[:, 64:64 + TS]))
                chain.done(nc.vector.tensor_scalar(et_i[:], et_i[:], 1, None, ALU.bitwise_and))
                chain.done(nc.vector.tensor_copy(odd_next[:, :, 1:2], et_i[:].unsqueeze(2)))
                chain.done(nc.vector.tensor_scalar(odd_next[:, :, 0:1], odd_next[:, :, 1:2], -1.0, 1.0, ALU.mult, ALU.add))
                chain.done(nc.vector.scalar_tensor_tensor(out=double_idx[:], in0=cols_next[:, 0:TS], scalar=float(R),
                                                          in1=cols_next[:, 64:64 + TS], op0=ALU.mult, op1=ALU.add))
                chain.done(nc.vector.tensor_tensor(double_idx[:].unsqueeze(2), double_idx[:].unsqueeze(2),
                                                   odd_next[:, :, 1:2], ALU.subtract))

            def index1(g):
                a, b = g * GT, (g + 1) * GT
                nc.vector.tensor_scalar(idx_a[:, a:b], double_idx[:, a:b], 0.5, None, ALU.mult).then_inc(s_idx, 1)

            def scores1(i, g, chain):
                a, b = g * GT, (g + 1) * GT
                pair = rows_a[:, a:b, 0:2 * M1].rearrange("p t (h c) -> p t h c", h=2)
                dve.wait_ge(s_got[1][g], i * (16 * GT) + 16 * GT)
                dve.wait_ge(s_sel[1], i * TS + (b + ONE))
                nc.vector.tensor_tensor(prod[:, a:b, F:F + 2].unsqueeze(3), pair[:, :, :, F:M1],
                                        odd[:, a:b, :].unsqueeze(3), ALU.mult)
                chain.done(nc.vector.tensor_tensor(prod[:, a:b, 0:F], rows_a[:, a:b, 2 * M1:TR],
                                                   banks[5 + g % 2][:, 0:GT * F].rearrange("p (t f) -> p t f", f=F), ALU.mult))
                chain.done(nc.vector.tensor_reduce(score[:, 0, a:b], prod[:, a:b, :], AX_X, ALU.add))
                nc.vector.tensor_scalar(score[:, 1, a:b], score[:, 0, a:b], 0.0, None, ALU.max).then_inc(s_score, 1)

            def values1(i, g, chain, last):
                a, b = g * GT, (g + 1) * GT
                pair = rows_a[:, a:b, 0:2 * M1].rearrange("p t (h c) -> p t h c", h=2)
                dve.wait_ge(s_att, i * NG + (g + 1))
                chain.done(nc.vector.scalar_tensor_tensor(out=weight2[:, a:b, :], in0=score[:, 2, a:b].unsqueeze(2).broadcast_to([P, GT, 2]),
                                                          scalar=0.0, in1=odd[:, a:b, :], op0=ALU.max, op1=ALU.mult))
                nc.vector.tensor_copy(val2[:, a:b, 0, F:M1], last_val[:, a:b].unsqueeze(2))
                nc.vector.tensor_tensor(val2[:, a:b, :, 0:F], pair[:, :, :, 0:F],
                                        weight2[:, a:b, :].unsqueeze(3).broadcast_to([P, GT, 2, F]),
                                        ALU.mult).then_inc(s_val[1], 1)
                if not last:
                    index1(g)

            def window_turn1(i, last=False):
                chain = Steps(dve, s_edge[1], i, 29, start=STAGE_STEPS)
                start_turn(1, i)
                chain.done(nc.vector.tensor_copy(cols[:], cols_next[:]))
                chain.done(nc.vector.tensor_copy(odd[:], odd_next[:]))
                chain.done(nc.vector.tensor_tensor(picked[:], cols[:, 32:32 + TS], cols[:, 96:96 + TS], ALU.not_equal))
                chain.done(nc.vector.scalar_tensor_tensor(out=last_val[:], in0=cols[:, 0:TS], scalar=1.0, in1=picked[:],
                                                          op0=ALU.add, op1=ALU.mult))
                for t in range(TS):
                    compare(1, i, t, chain)
                    if t == 0:
                        window_parts(1, i)
                    if t == 2:
                        if not last:
                            dve.wait_ge(s_cols[1], i + (2 + ONE))
                            stage1(chain)
                    if t > GT and t % GT == 1:
                        scores1(i, t // GT - 1, chain)
                    if t > GT and t % GT == 2:
                        values1(i, t // GT - 1, chain, last)
                    if t > GT and t % GT == 3:
                        rest(1, i, t // GT - 1)
                    if t > GT and t % GT == 4:
                        third_part(1, i, t // GT - 1)
                scores1(i, NG - 1, chain)
                values1(i, NG - 1, chain, last)
                rest(1, i, NG - 1)
                third_part(1, i, NG - 1)
                assert last or chain.n == chain.per_turn, chain.n

            dve.wait_ge(s_badsum, 1)
            nc.vector.tensor_copy(flag[:], banks[5][0:1, 0:1]).then_inc(s_flag, 1)
            dve.wait_ge(s_flag, 1)
            unfit = dve.value_load(flag[0:1, 0:1], min_val=0, max_val=2 * P)
            dve.wait_ge(s_const, 9)
            with dve.If(unfit == 0):
                dve.sem_inc(s_val[0], ONE)
                for bits, q in ((src_bits, 0), (dst_bits, 64)):
                    steps.done(nc.vector.tensor_tensor(bits, ident[:, q:q + TS].unsqueeze(2).broadcast_to([P, TS, P]),
                                                       ident[:, q + 32:q + 32 + TS].unsqueeze(2).broadcast_to([P, TS, P]), ALU.add))
                for q in range(4):
                    ins = nc.vector.memset(row_mask[q * 32:(q + 1) * 32, :], (P * 127, P - 1)[q % 2])
                    ins.then_inc(s_v, 1)
                steps.n += 4
                dve.wait_ge(s_v, steps.value())
                dve.sem_inc(s_selectors, 1)
                with dve.Fori(0, S) as i:
                    window_turn0(i)
            with dve.Else():
                with dve.Fori(0, S) as i:
                    edge_turn(0, i, 12)

            accv = acc_flat
            inv = part_flat
            for c in range(GT):
                dve.wait_ge(s_part, 16 * (c + 1))
                if c == 0:
                    ins = nc.vector.tensor_copy(accv, inv)
                else:
                    dve.wait_ge(s_partused, c)
                    ins = nc.vector.tensor_tensor(accv, accv, inv, ALU.add)
                ins.then_inc(s_partused, 1)
            dve.wait_ge(s_partused, GT)
            dve.wait_ge(s_h0, 1)
            dve.wait_ge(s_h0d, 16)
            steps.done(nc.vector.tensor_tensor(hn[:], hn[:], acc[:, :, F:F + 1].broadcast_to([P, J, F]), ALU.mult))
            steps.done(nc.vector.tensor_tensor(sq[:], acc[:, :, 0:F], hn[:], ALU.subtract))
            steps.done(nc.vector.tensor_tensor(xn[:], xn[:], sq[:], ALU.add))
            layer_norm(1)

            dve.wait_ge(s_h1, 1)
            dve.sem_inc(s_cv, V_CHUNKS)
            with dve.Fori(0, J // 2) as i:
                for b in range(2):
                    j = i * 2 + b
                    dve.wait_ge(s_hst, j + ONE)
                    nc.vector.tensor_copy(hs[:, b, :], hn[:, bass.ds(j, 1), :].rearrange("p j f -> p (j f)")).then_inc(s_hs, 1)
                    dve.wait_ge(s_np, j + 1)
                    dve.wait_ge(s_npc, j + ONE)
                    nc.vector.tensor_copy(nrow[:, b, :], node_ps[:, 0:3 * F]).then_inc(s_xh, 1)
                    dve.wait_ge(s_xh, j + 1 + ONE)
                    dve.wait_ge(s_tst[b], i * 16 + FIRST)
                    nc.vector.tensor_copy(tb[b][:, :, 2 * M1:TR], nrow[:, b, 0:F].unsqueeze(1).broadcast_to([P, H, F]))
                    for q, (r, n) in enumerate(CHUNKS):
                        if q % 2:
                            dve.wait_ge(s_tp, i * (2 * len(CHUNKS)) + (b * len(CHUNKS) + q + 1))
                            ins = nc.vector.tensor_copy(tb[b][:, r // 2:(r + n) // 2, 0:2 * M1],
                                                        chunk_ps[q][:, 0:n * M1].rearrange("p (h c) -> p h c", c=2 * M1))
                            ins.then_inc(s_cv, 1)

            tail_steps = Steps(dve, s_tail)
            latest, hit, found, source = (stat[:, q, :] for q in range(4))

            def last_sums():
                sq_flat = sq[:].rearrange("p j f -> p (j f)")
                for c in range(GT):
                    dve.wait_ge(s_part, 16 * (2 * GT + c + 1))
                    if c == 0:
                        ins = nc.vector.tensor_copy(sq_flat, part_flat[:, 0:J * F])
                    else:
                        dve.wait_ge(s_partused, GT + c)
                        ins = nc.vector.tensor_tensor(sq_flat, sq_flat, part_flat[:, 0:J * F], ALU.add)
                    ins.then_inc(s_partused, 1)
                tail_steps.done(nc.vector.tensor_copy(latest, last_in[:, 0, :, 0]))
                for c in range(1, GT):
                    tail_steps.done(nc.vector.tensor_tensor(latest, latest, last_in[:, c, :, 0], ALU.max))
                for c in range(GT):
                    tail_steps.done(nc.vector.tensor_tensor(hit, latest, last_in[:, c, :, 0], ALU.is_equal))
                    if c == 0:
                        tail_steps.done(nc.vector.tensor_tensor(source, hit, last_in[:, c, :, 1], ALU.mult))
                    else:
                        tail_steps.done(nc.vector.tensor_tensor(found, hit, last_in[:, c, :, 1], ALU.mult))
                        tail_steps.done(nc.vector.tensor_tensor(source, source, found, ALU.add))

            with dve.If(unfit == 0):
                steps.done(nc.vector.memset(val2[:], 0.0))
                dve.sem_inc(s_val[1], ONE)
                chain = Steps(dve, s_edge[1])
                dve.wait_ge(s_cols[1], 1 + ONE)
                stage1(chain)
                assert chain.n == STAGE_STEPS
                for g in range(NG):
                    index1(g)
                with dve.Fori(0, S - 1) as i:
                    window_turn1(i)
                window_turn1(S - 1, last=True)
                dve.wait_ge(s_part, 16 * (GT + 1))
                nc.vector.tensor_copy(sq[:], part_rows[:, :, 0:F]).then_inc(s_done, 1)
                nc.vector.tensor_copy(source.unsqueeze(2), part_rows[:, :, F:M1]).then_inc(s_done, 1)
            with dve.Else():
                with dve.Fori(0, S) as i:
                    edge_turn(1, i, 37)
                last_sums()
                dve.sem_inc(s_done, 2)
            dve.wait_ge(s_done, 2)
            tail_steps = Steps(dve, s_tail2)

            tail_steps.done(nc.vector.tensor_scalar(cidx[:], source, -1.0, 0.0, ALU.add, ALU.max))
            tail_steps.done(nc.vector.tensor_scalar(hit, source, 1.0, None, ALU.min))
            dve.wait_ge(s_nst, 32)
            with dve.Fori(0, J // 7) as i:
                nc.vector.tensor_copy(cidx_s[:], cidx[:, bass.ds(i * 7, 7)]).then_inc(s_ci, 1)
                dve.wait_ge(s_cg, i * (16 * 7) + 16 * 7)
                nc.vector.tensor_copy(yhn[:, bass.ds(i * 7, 7), :], cg[:]).then_inc(s_cgc, 1)
            dve.wait_ge(s_cgc, J // 7)
            tail_steps.done(nc.vector.tensor_tensor(sq[:], sq[:], yhn, ALU.add))
            tail_steps.done(nc.vector.tensor_tensor(sq[:], sq[:], bc(hit), ALU.mult))
            tail_steps.done(nc.vector.tensor_scalar(sq[:], sq[:], 0.0, None, ALU.max))
            nc.vector.tensor_tensor(xn[:], xn[:], sq[:], ALU.add).then_inc(s_res, 1)


_INS = ['x', 'src', 'dst', 'edge_type_86', 'edge_weight', 'L1_gnn_weight', 'L1_gnn_w_comp',
        'L1_gnn_self_loop_weight', 'L1_gnn_A1_w', 'L1_gnn_A1_b', 'L1_gnn_A2_w', 'L1_gnn_A2_b',
        'L1_gnn_rel_emb']


def kernel(**inputs):
    import numpy as _np
    import concourse.bacc as _bacc
    from concourse import mybir as _mybir
    from concourse.bass_utils import run_bass_kernel_spmd as _run

    nc = _bacc.Bacc("TRN2", target_bir_lowering=False, num_devices=1)
    arrays, args = {}, []
    for name in _INS:
        a = _np.ascontiguousarray(inputs[name])
        arrays[f"in_{name}_dram"] = a
        args.append(nc.dram_tensor(f"in_{name}_dram", a.shape, _mybir.dt.from_np(a.dtype), kind="ExternalInput").ap())
    out = nc.dram_tensor("out_0_dram", inputs["x"].shape, _mybir.dt.float32, kind="ExternalOutput").ap()
    gnn_kernel(nc, *args, out)
    r = _run(nc, [arrays], core_ids=[0])
    return r.results[0]["out_0_dram"]
```

```python
from contextlib import ExitStack

import concourse.bass as bass
from concourse import mybir

ALU = mybir.AluOpType
ACT = mybir.ActivationFunctionType
AX_X = mybir.AxisListType.X
F32 = mybir.dt.float32
I32 = mybir.dt.int32
U32 = mybir.dt.uint32
BF16 = mybir.dt.bfloat16

P = 128
TS = 25
GT = 5
DELAY = 4
SUM_LAG = 11
STAGE_STEPS = 7
NG = TS // GT
SE = TS * P
EPS = 1e-5
ONE = 1
GROUP_BANK = (5, 6, 5, 6, 7)
BANK_FREE = (-2, -1, 1, 2, 0)
VAL_START = 3
SEL_START = GT
FIRST = 16


class Steps:

    def __init__(self, eng, sem, turn=None, per_turn=0, start=0):
        self.eng, self.sem, self.turn, self.per_turn, self.start, self.n = eng, sem, turn, per_turn, start, 0

    def value(self):
        v = self.start + self.n
        return v if self.turn is None else self.turn * self.per_turn + v

    def done(self, ins):
        ins.then_inc(self.sem, 1)
        self.n += 1
        self.eng.wait_ge(self.sem, self.value())


def gnn_kernel(nc, x, src, dst, edge_type_86, edge_weight, L1_gnn_weight, L1_gnn_w_comp,
               L1_gnn_self_loop_weight, L1_gnn_A1_w, L1_gnn_A1_b, L1_gnn_A2_w, L1_gnn_A2_b,
               L1_gnn_rel_emb, out):
    N, F = x.shape
    E = src.shape[0]
    R, B = L1_gnn_w_comp.shape
    S = E // SE
    J = -(-N // P)
    NP = J * P
    NT = NP + P
    M1 = F + 1
    H = R // 2
    TR = 2 * M1 + F
    RC = 14
    CHUNKS = [(r, min(RC, R - r)) for r in range(0, R, RC)]
    assert S * SE == E and F == 32 and R <= P and 2 * H == R and RC % 2 == 0 and RC * M1 <= 512 and J % 2 == 0 and J % 7 == 0
    tail = N - (P - 1) * J
    SPLIT = ((0, 112), (112, 127))

    h0_dram = nc.dram_tensor("h0", (NT, F), F32).ap()
    yh_dram = nc.dram_tensor("yh", (NT, F), F32).ap()
    self_dram = nc.dram_tensor("self_rows", (NP, F), F32).ap()
    table = nc.dram_tensor("relation_table", (NP * H, TR), F32).ap()
    lap_sums = [nc.dram_tensor(f"lap_sums{c}", (NT, F + 1), F32).ap() for c in range(GT)]
    window_sums = nc.dram_tensor("window_sums", (NT, M1), F32).ap()
    dst_next = nc.dram_tensor("dst_next", (E,), I32).ap()
    nei_sums = [nc.dram_tensor(f"nei_sums{c}", (NT, F), F32).ap() for c in range(GT)]
    last_rows = [nc.dram_tensor(f"last_rows{c}", (NT, 2), F32).ap() for c in range(GT)]

    src_rows = src.rearrange("(t p) -> t p", p=P)
    dst_rows = dst.rearrange("(t p) -> t p", p=P)
    et_rows = edge_type_86.rearrange("(t p) -> t p", p=P)
    next_rows = dst_next.rearrange("(t p) -> t p", p=P)
    w_rows = edge_weight.rearrange("(t p) -> t p", p=P)

    with ExitStack() as ctx:
        def sb(name, shape, dt=F32):
            return ctx.enter_context(nc.sbuf_tensor(name, shape, dt))

        def sem(name):
            return ctx.enter_context(nc.semaphore(name))

        banks = [ctx.enter_context(nc.psum_tensor(f"bank{b}", [P, 512], F32)) for b in range(8)]
        cols_ps, sum_ps = banks[0], banks[1:3]
        row_ps = [b[:, 0:P] for b in banks[3:5]]
        full_chunks, last_chunk = CHUNKS[:-1], CHUNKS[-1]
        chunk_ps = banks[0:len(full_chunks)]
        turn_ps, node_ps = banks[6], banks[7]
        chunks_of_act, chunks_of_dve = len(full_chunks[0::2]), len(full_chunks[1::2])

        ident = sb("ident", [P, P])
        tri = sb("tri", [P, P])
        row_of_src, row_of_dst = sb("row_of_src", [P, TS, P]), sb("row_of_dst", [P, TS, P])
        trash = sb("trash", [P, 1])
        part = sb("part", [P, 1])
        xn = sb("xn", [P, J, F])
        hn = sb("hn", [P, J, F])
        sq = sb("sq", [P, J, F])
        stat = sb("stat", [P, 4, J])
        last_in = sb("last_in", [P, GT, J, 2])
        cidx = sb("cidx", [P, J], U32)
        relT = sb("relT", [F, R])
        wcT = sb("wcT", [B, R])
        rel_sb = sb("rel_sb", [R, F])
        wc_sb = sb("wc_sb", [R, B])
        a1 = sb("a1", [F, F + 1])
        a2 = sb("a2", [F, F + 1])
        NW = sb("NW", [F + 1, 3 * F])
        PR = 3 * F + 1
        TW3 = sb("TW3", [PR, 3, R, M1], BF16)
        NW3 = sb("NW3", [PR, 3, 3 * F], BF16)
        hs = sb("hs", [P, 2, PR + 1], BF16)
        hT = sb("hT", [PR, 2, P], BF16)
        ident16 = sb("ident16", [P, P], BF16)
        tb = [sb(f"tb{b}", [P, H, TR]) for b in range(2)]
        nrow = sb("nrow", [P, 2, 3 * F])
        acc_flat, part_flat = (tb[b][:].rearrange("p r c -> p (r c)")[:, 0:J * M1] for b in range(2))
        part_rows = part_flat.rearrange("p (j f) -> p j f", j=J)
        acc = acc_flat.rearrange("p (j f) -> p j f", j=J)
        node_rows = sb("node_rows", [P, 2, J, F])
        yhn, sfn = node_rows[:, 0], node_rows[:, 1]
        zeros = node_rows[:].rearrange("p a j f -> p (a j f)")[:, 0:NT // P * M1]
        CE = E // P
        chk = tb[0][:].rearrange("p r c -> p (r c)")[:, 0:CE + 1].bitcast(I32)
        rises = tb[1][:].rearrange("p r c -> p (r c)")[:, 0:CE]
        w_sb = tb[1][:].rearrange("p r c -> p (r c)")[0:B, CE:CE + F * F].rearrange("b (i o) -> b i o", i=F)
        ends = sb("ends", [P, 2], I32)
        odds = sb("odds", [P, 4])
        flag = sb("flag", [1, 1], I32)
        first_dst = sb("first_dst", [1, S], I32)
        iota_row = sb("iota_row", [P, P])
        window = sb("window", [P, F])
        base = sb("base", [P, 2])
        at_window = sb("at_window", [P, GT, P], BF16)
        wraw = sb("wraw", [32, P])
        wide_window = sb("wide_window", [P, F])
        window3 = sb("window3", [P, 3, F], BF16)
        rowi = sb("rowi", [P, P], I32)
        row_mask = sb("row_mask", [P, 1], I32)
        rowm = sb("rowm", [P, P], I32)
        rowb = sb("rowb", [P, P], BF16)
        cols_next = sb("cols_next", [P, P])
        odd_next = sb("odd_next", [P, TS, 2])
        double_idx = sb("double_idx", [P, TS])
        in_window = sb("in_window", [P, TS])
        last_val = sb("last_val", [P, TS])
        win_sb = sb("win_sb", [P, M1])
        raw = sb("raw", [P, P], I32)
        rawf = sb("rawf", [P, P])
        cols = sb("cols", [P, P])
        idx_a = sb("idx_a", [P, TS], U32)
        idx_b = sb("idx_b", [P, TS], U32)
        idx_s = sb("idx_s", [P, TS], U32)
        shifted = sb("shifted", [P, TS])
        picked = sb("picked", [P, TS])
        cnt = sb("cnt", [P, TS])
        edge_space = sb("edge_space", [P, TS * (P + TR)])
        eq = edge_space[:, 0:TS * P].rearrange("p (t q) -> p t q", q=P)
        rows_a = edge_space[:, TS * P:TS * (P + TR)].rearrange("p (t c) -> p t c", c=TR)
        h3 = edge_space[:].bitcast(BF16)[:, 0:J * (PR + 1)].rearrange("p (j c) -> p j c", c=PR + 1)
        TW = edge_space[0:F + 1, 0:R * M1].rearrange("p (r c) -> p r c", c=M1)
        rows_b = sb("rows_b", [P, TS, F])
        prod = sb("prod", [P, TS, F + 2])
        et_i = sb("et_i", [P, TS], I32)
        odd = sb("odd", [P, TS, 2])
        weight2 = sb("weight2", [P, TS, 2])
        val2 = sb("val2", [P, TS, 2, M1])
        val = val2[:].rearrange("p t h c -> p (t h c)")[:, 0:TS * M1].rearrange("p (t c) -> p t c", c=M1)
        wide = sb("wide", [P, GT, M1])
        halves = [t.rearrange("p t q -> p (t q)").bitcast(BF16) for t in (row_of_src[:], row_of_dst[:], eq)]
        src_bits, dst_bits, same = (h[:, 0:TS * P].rearrange("p (t q) -> p t q", q=P) for h in halves)
        parts3 = [h[:, TS * P:TS * (P + M1)].rearrange("p (t c) -> p t c", c=M1) for h in halves]
        score = sb("score", [P, 4, TS])
        sums = sb("sums", [P, TS, F + 1])
        eno = sb("eno", [P, TS])
        lastrow = sb("lastrow", [P, TS, 2])
        cidx_s = sb("cidx_s", [P, 7], U32)
        cg = sb("cg", [P, 7, F])

        s_const = sem("const_ready")
        s_x = sem("x_loaded")
        s_w = sem("weights_loaded")
        s_zt = sem("zeros_ready")
        s_wt = sem("weight_transposed")
        s_wtc = sem("weight_copied")
        s_wp = sem("weight_products")
        s_wready = sem("table_weights_ready")
        s_copies = sem("table_weights_copied")
        s_v = sem("dve_steps")
        s_var = sem("variance_ready")
        s_std = sem("deviation_ready")
        s_h0 = sem("h0_ready")
        s_h0d = sem("h0_stored")
        s_rawld = [sem(f"edges_loaded{n}") for n in (0, 1)]
        s_cast = [sem(f"edges_cast{n}") for n in (0, 1)]
        s_cols = [sem(f"columns_turned{n}") for n in (0, 1)]
        s_stage = [sem(f"columns_staged{n}") for n in (0, 1)]
        s_row = [sem(f"rows_spread{n}") for n in (0, 1)]
        s_eq = [sem(f"equal_ready{n}") for n in (0, 1)]
        s_val = [sem(f"values_ready{n}") for n in (0, 1)]
        s_sum = [sem(f"sums_ready{n}") for n in (0, 1)]
        s_out = [sem(f"sums_copied{n}") for n in (0, 1)]
        s_sidx = [sem(f"scatter_index_ready{n}") for n in (0, 1)]
        s_got = [[sem(f"gathered{n}_{g}") for g in range(NG)] for n in (0, 1)]
        s_put = [[sem(f"scattered{n}_{c}") for c in range(GT)] for n in (0, 1)]
        s_lastput = [sem(f"last_scattered{c}") for c in range(GT)]
        s_dve = [sem(f"dve_edge_steps{n}") for n in (0, 1)]
        s_chk0 = sem("check_edges_set")
        s_chk = sem("check_loaded")
        s_dn = sem("next_dst_stored")
        s_bad = sem("unfit_counted_by_partition")
        s_badsum = sem("unfit_counted")
        s_flag = sem("flag_ready")
        s_winld = [sem(f"window_loaded{n}") for n in (0, 1)]
        s_cmp = [sem(f"rows_compared{n}") for n in (0, 1)]
        s_sel = [sem(f"window_rows_selected{n}") for n in (0, 1)]
        s_landed = sem("scatter_groups_landed")
        s_selectors = sem("selectors_ready")
        s_rowld = [sem(f"key_rows_loaded{n}") for n in (0, 1)]
        s_rowm = [sem(f"key_rows_masked{n}") for n in (0, 1)]
        s_rowb = [sem(f"key_rows_cast{n}") for n in (0, 1)]
        s_whi = [sem(f"window_first_part{n}") for n in (0, 1)]
        s_wrest = [sem(f"window_rest{n}") for n in (0, 1)]
        s_wmid = [sem(f"window_second_part{n}") for n in (0, 1)]
        s_wpart = [sem(f"window_parts{n}") for n in (0, 1)]
        s_hi = [sem(f"values_first_part{n}") for n in (0, 1)]
        s_rest = [sem(f"values_rest{n}") for n in (0, 1)]
        s_mid = [sem(f"values_second_part{n}") for n in (0, 1)]
        s_parts = [sem(f"values_parts{n}") for n in (0, 1)]
        s_idx = sem("gather_index_ready")
        s_wout = sem("window_sums_copied")
        s_wadd = sem("window_added")
        s_edge = [sem(f"dve_window_steps{n}") for n in (0, 1)]
        s_score = sem("score_ready")
        s_att = sem("attention_ready")
        s_gate = sem("pool_gate")
        s_agate = sem("act_gate")
        s_sgate = sem("sp_gate")
        s_part = sem("partial_sums_loaded")
        s_partused = sem("partial_sums_used")
        s_h1 = sem("h1_ready")
        s_xh = sem("source_rows_copied")
        s_hs = sem("node_rows_staged")
        s_hst = sem("node_rows_turned")
        s_hT = sem("node_rows_copied")
        s_np = sem("node_products")
        s_npc = sem("node_products_copied")
        s_tp = sem("table_products")
        s_ca = sem("chunks_free_act")
        s_cv = sem("chunks_free_dve")
        s_tst = [sem(f"table_stored{b}") for b in range(2)]
        s_nst = sem("node_tables_stored")
        s_ci = sem("self_index_ready")
        s_cg = sem("self_gathered")
        s_cgc = sem("self_copied")
        s_tail = sem("dve_last_sum_steps")
        s_done = sem("neighbours_summed")
        s_tail2 = sem("dve_tail_steps")
        s_res = sem("result_ready")
        s_fin = sem("result_stored")

        block = ctx.enter_context(nc.Block())
        NW_DMAS = 9

        def node_parts(t):
            for a, b in SPLIT:
                yield slice(a, b), J, t[a * J:b * J, :].rearrange("(p j) f -> p j f", j=J)
            yield slice(P - 1, P), tail, t[(P - 1) * J:N, :].rearrange("(p j) f -> p j f", j=tail)

        def count_from_one(eng, *sems):
            for s in sems:
                eng.sem_inc(s, ONE)

        def whole(t):
            return t.rearrange("(p j) f -> p (j f)", p=P)

        @block.sync
        def _(sp):
            with nc.allow_non_contiguous_dma(reason="small weights"):
                sp.wait_ge(s_zt, 2)
                for parts, n, dram in node_parts(x):
                    sp.dma_start(xn[parts, 0:n, :], dram).then_inc(s_x, 16)
                dst_parts = dst.rearrange("(p c) -> p c", p=P)
                dst_supers = dst.rearrange("(s c) -> s c", c=SE)
                sp.wait_ge(s_chk0, 2)
                sp.dma_start(chk[:, 0:CE], dst_parts).then_inc(s_chk, 16)
                sp.dma_start(chk[0:P - 1, CE:CE + 1], dst_parts[1:P, 0:1]).then_inc(s_chk, 16)
                sp.dma_start(ends[0:S, 0:1], dst_supers[:, 0:1]).then_inc(s_chk, 16)
                sp.dma_start(ends[0:S, 1:2], dst_supers[:, SE - 1:SE]).then_inc(s_chk, 16)
                sp.dma_start(first_dst[0:1, :], dst_supers[:, 0:1].rearrange("s c -> c s")).then_inc(s_chk, 16)
                sp.dma_start(rel_sb[:], L1_gnn_rel_emb).then_inc(s_w, 16)
                sp.dma_start(wc_sb[:], L1_gnn_w_comp).then_inc(s_w, 16)
                sp.dma_start(w_sb, L1_gnn_weight).then_inc(s_w, 16)
                sp.dma_start(a1[:, 0:F], L1_gnn_A1_w).then_inc(s_w, 16)
                sp.dma_start(a1[:, F:F + 1], L1_gnn_A1_b.rearrange("(a b) -> a b", b=1)).then_inc(s_w, 16)
                sp.dma_start(a2[:, 0:F], L1_gnn_A2_w).then_inc(s_w, 16)
                sp.dma_start(a2[:, F:F + 1], L1_gnn_A2_b.rearrange("(a b) -> a b", b=1)).then_inc(s_w, 16)
                sp.dma_start(NW[0:F, 2 * F:3 * F], L1_gnn_self_loop_weight).then_inc(s_w, 16)
                sp.dma_start(NW[F:F + 1, 2 * F:3 * F], zeros[0:1, 0:F]).then_inc(s_w, 16)
                sp.dma_start(h0_dram[NP:NT, :], zeros[:, 0:F]).then_inc(s_tst[0], 16)
                sp.dma_start(yh_dram[NP:NT, :], zeros[:, 0:F]).then_inc(s_tst[1], 16)
                sp.wait_ge(s_wready, 1)
                sp.dma_start(TW3[3 * F:PR, :, :, :], TW3[F:F + 1, :, :, :]).then_inc(s_copies, 16)
                sp.dma_start(NW3[3 * F:PR, :, :], NW3[F:F + 1, :, :]).then_inc(s_copies, 16)
                sp.wait_ge(s_copies, 32)
                for q in (1, 2):
                    sp.dma_start(TW3[q * F:(q + 1) * F, :, :, :], TW3[0:F, :, :, :]).then_inc(s_copies, 16)
                    sp.dma_start(NW3[q * F:(q + 1) * F, :, :], NW3[0:F, :, :]).then_inc(s_copies, 16)
                sp.wait_ge(s_h0, 1)
                sp.dma_start(whole(h0_dram[0:NP, :]), hn[:].rearrange("p j f -> p (j f)")).then_inc(s_h0d, 16)

                def edge_rows(n, i):
                    sp.wait_ge(s_row[n], i * TS + ONE)
                    sp.sem_inc(s_sgate, 1)
                    sp.wait_ge(s_cast[n], i + ONE)
                    sp.sem_inc(s_sgate, 1)
                    rows = bass.ds(i * TS, TS)
                    sp.dma_start(raw[0:TS, :], src_rows[rows, :]).then_inc(s_rawld[n], 16)
                    sp.dma_start(raw[32:32 + TS, :], dst_rows[rows, :]).then_inc(s_rawld[n], 16)
                    if n == 0:
                        sp.dma_start(rawf[64:64 + TS, :], w_rows[rows, :]).then_inc(s_rawld[n], 16)
                    else:
                        sp.dma_start(raw[64:64 + TS, :], et_rows[rows, :]).then_inc(s_rawld[n], 16)

                sp.wait_ge(s_chk, 16 * 5)
                sp.dma_start(dst_next.rearrange("(p c) -> p c", p=P), chk[:, 1:CE + 1]).then_inc(s_dn, 16)
                sp.wait_ge(s_dn, 16)
                sp.wait_ge(s_flag, 1)
                sp.wait_ge(s_h0d, 16)
                sp.wait_ge(s_tst[0], FIRST)
                sp.wait_ge(s_tst[1], FIRST)
                unfit = sp.value_load(flag[0:1, 0:1], min_val=0, max_val=2 * P)

                def window_edges(n, k):
                    sp.wait_ge(s_cast[n], k + ONE)
                    sp.sem_inc(s_sgate, 1)
                    rows = bass.ds(k * TS, TS)
                    sp.dma_start(raw[0:TS, :], src_rows[rows, :]).then_inc(s_rawld[n], 16)
                    sp.dma_start(raw[32:32 + TS, :], dst_rows[rows, :]).then_inc(s_rawld[n], 16)
                    if n == 0:
                        sp.dma_start(wraw[0:TS, :], w_rows[rows, :]).then_inc(s_rawld[n], 16)
                    else:
                        sp.dma_start(raw[64:64 + TS, :], et_rows[rows, :]).then_inc(s_rawld[n], 16)
                        sp.dma_start(raw[96:96 + TS, :], next_rows[rows, :]).then_inc(s_rawld[n], 16)

                def key_rows(n, k):
                    sp.wait_ge(s_rowm[n], k + ONE)
                    sp.sem_inc(s_sgate, 1)
                    rows = bass.ds(k * TS, TS)
                    for q in range(0 if n == 0 else 2, 4):
                        sp.dma_start(rowi[q * 32:q * 32 + TS, :], (src_rows if q < 2 else dst_rows)[rows, :]).then_inc(s_rowld[n], 16)

                def window_load(n, i):
                    sp.wait_ge(s_wpart[n], i + ONE)
                    sp.sem_inc(s_sgate, 1)
                    d0 = sp.value_load(first_dst[0:1, bass.ds(i, 1)], min_val=0, max_val=NP - 1)
                    sp.dma_start(window[:], (h0_dram, yh_dram)[n][bass.ds(d0, P), :]).then_inc(s_winld[n], 16)

                sp.wait_ge(s_agate, 3)
                with sp.If(unfit == 0):
                    with sp.Fori(0, S) as i:
                        window_edges(0, i)
                        key_rows(0, i)
                        window_load(0, i)
                with sp.Else():
                    with sp.Fori(0, S) as i:
                        edge_rows(0, i)

                for c in range(GT):
                    for d in range(GT):
                        if c == 0:
                            sp.wait_ge(s_put[0][d], 16 * S * NG + FIRST)
                    if c:
                        sp.wait_ge(s_partused, c)
                    sp.dma_start(part_flat, whole(lap_sums[c][0:NP, :])).then_inc(s_part, 16)

                tv = table.rearrange("(p j h) c -> p j (h c)", p=P, j=J)
                with sp.Fori(0, J // 2) as i:
                    for b in range(2):
                        sp.wait_ge(s_ca, i * (2 * chunks_of_act) + (b + 2) * chunks_of_act)
                        sp.sem_inc(s_sgate, 1)
                        sp.wait_ge(s_cv, i * (2 * chunks_of_dve) + (b + 2) * chunks_of_dve)
                        sp.sem_inc(s_sgate, 1)
                        sp.dma_start(tv[:, bass.ds(i * 2 + b, 1), :].rearrange("p j c -> p (j c)"),
                                     tb[b][:].rearrange("p r c -> p (r c)")).then_inc(s_tst[b], 16)
                sp.wait_ge(s_npc, J + ONE + 1)
                sp.dma_start(whole(yh_dram[0:NP, :]), yhn.rearrange("p j f -> p (j f)")).then_inc(s_nst, 16)
                sp.dma_start(whole(self_dram), sfn.rearrange("p j f -> p (j f)")).then_inc(s_nst, 16)

                def last_loads():
                    for d in range(GT):
                        sp.wait_ge(s_put[1][d], 16 * S * NG + FIRST)
                        sp.wait_ge(s_lastput[d], 16 * S * NG + FIRST)
                    for d in range(GT):
                        sp.dma_start(last_in[:, d, :, :].rearrange("p j f -> p (j f)"),
                                     whole(last_rows[d][0:NP, :])).then_inc(s_part, 16)
                    for c in range(GT):
                        sp.wait_ge(s_partused, GT + c)
                        sp.dma_start(part_flat[:, 0:J * F], whole(nei_sums[c][0:NP, :])).then_inc(s_part, 16)

                sp.wait_ge(s_nst, 32)
                with sp.If(unfit == 0):
                    window_edges(1, 0)
                    with sp.Fori(0, S - 1) as i:
                        key_rows(1, i)
                        window_load(1, i)
                        window_edges(1, i + 1)
                    key_rows(1, S - 1)
                    window_load(1, S - 1)
                    sp.wait_ge(s_wadd, 16 * S + FIRST)
                    sp.dma_start(part_flat, whole(window_sums[0:NP, :])).then_inc(s_part, 16)
                with sp.Else():
                    with sp.Fori(0, S) as i:
                        edge_rows(1, i)
                    last_loads()

                sp.wait_ge(s_res, 1)
                for parts, n, dram in node_parts(out):
                    sp.dma_start(dram, xn[parts, 0:n, :]).then_inc(s_fin, 16)
                sp.wait_ge(s_fin, 16 * 3)

        @block.gpsimd
        def _(pool):
            nc.gpsimd.memset(zeros, 0.0).then_inc(s_zt, 1)
            nc.gpsimd.memset(xn[:], 0.0).then_inc(s_zt, 1)
            pool.wait_ge(s_zt, 2)
            pool.dma_start(whole(window_sums), zeros[:, 0:NT // P * M1]).then_inc(s_wadd, 16)
            for c in range(GT):
                pool.dma_start(whole(lap_sums[c]), zeros[:, 0:NT // P * M1]).then_inc(s_put[0][c], 16)
                pool.dma_start(whole(nei_sums[c]), zeros[:, 0:NT // P * F]).then_inc(s_put[1][c], 16)
                pool.dma_start(whole(last_rows[c]), zeros[:, 0:NT // P * 2]).then_inc(s_lastput[c], 16)
            nc.gpsimd.memset(ident[:], 0.0).then_inc(s_const, 1)
            nc.gpsimd.memset(tri[:], 1.0).then_inc(s_const, 1)
            nc.gpsimd.iota(part[:], pattern=[[0, 1]], base=0, channel_multiplier=1,
                           allow_small_or_imprecise_dtypes=True).then_inc(s_const, 1)
            nc.gpsimd.iota(trash[:], pattern=[[0, 1]], base=NP, channel_multiplier=1,
                           allow_small_or_imprecise_dtypes=True).then_inc(s_const, 1)
            nc.gpsimd.iota(iota_row[:], pattern=[[1, P]], base=0, channel_multiplier=0,
                           allow_small_or_imprecise_dtypes=True).then_inc(s_const, 1)
            nc.gpsimd.iota(eno[:], pattern=[[P, TS]], base=1, channel_multiplier=1,
                           allow_small_or_imprecise_dtypes=True).then_inc(s_const, 1)
            pool.wait_ge(s_const, 6)
            nc.gpsimd.affine_select(out=ident[:], in_=ident[:], compare_op=ALU.not_equal, fill=1.0, base=0,
                                    pattern=[[-1, P]], channel_multiplier=1).then_inc(s_const, 1)
            nc.gpsimd.affine_select(out=tri[:], in_=tri[:], compare_op=ALU.is_ge, fill=0.0, base=0,
                                    pattern=[[1, P]], channel_multiplier=-1).then_inc(s_const, 1)

            pool.wait_ge(s_h0d, 16)
            pool.wait_ge(s_wadd, FIRST)
            for c in range(GT):
                pool.wait_ge(s_put[1][c], FIRST)
                pool.wait_ge(s_lastput[c], FIRST)
            pool.wait_ge(s_tst[0], FIRST)
            pool.wait_ge(s_tst[1], FIRST)
            pool.sem_inc(s_gate, 1)

            def gather(n, i, g):
                for t in range(g * GT, (g + 1) * GT):
                    if n == 0:
                        nc.gpsimd.indirect_dma_start(
                            rows_b[:, t, :], None, h0_dram,
                            bass.IndirectOffsetOnAxis(ap=idx_a[:, t:t + 1], axis=0)).then_inc(s_got[n][g], 16)
                    else:
                        nc.gpsimd.indirect_dma_start(
                            rows_a[:, t, :], None, table,
                            bass.IndirectOffsetOnAxis(ap=idx_a[:, t:t + 1], axis=0)).then_inc(s_got[n][g], 16)
                        nc.gpsimd.indirect_dma_start(
                            rows_b[:, t, :], None, yh_dram,
                            bass.IndirectOffsetOnAxis(ap=idx_b[:, t:t + 1], axis=0)).then_inc(s_got[n][g], 16)

            def scatter(n, i, g):
                pool.wait_ge(s_out[n], i * NG + (g + 1) + ONE)
                pool.wait_ge(s_sidx[n], i * NG + (g + 1))
                for c in range(GT):
                    pool.wait_ge(s_put[n][c], i * (16 * NG) + 16 * g + FIRST)
                    if n:
                        pool.wait_ge(s_lastput[c], i * (16 * NG) + 16 * g + FIRST)
                pool.sem_inc(s_gate, 1)
                for c in range(GT):
                    t = g * GT + c
                    to = bass.IndirectOffsetOnAxis(ap=idx_s[:, t:t + 1], axis=0)
                    if n == 0:
                        nc.gpsimd.indirect_dma_start(lap_sums[c], to, sums[:, t, :], None,
                                                     compute_op=ALU.add).then_inc(s_put[n][c], 16)
                    else:
                        nc.gpsimd.indirect_dma_start(nei_sums[c], to, sums[:, t, 0:F], None,
                                                     compute_op=ALU.add).then_inc(s_put[n][c], 16)
                        nc.gpsimd.indirect_dma_start(last_rows[c], to, lastrow[:, t, :],
                                                     None).then_inc(s_lastput[c], 16)

            def edge_turn(n, i):
                pool.wait_ge(s_stage[n], i + 1 + ONE)
                pool.sem_inc(s_gate, 1)
                gather(n, i, 0)
                for g in range(NG):
                    if g + 1 < NG:
                        gather(n, i, g + 1)
                    scatter(n, i, g)

            def window_scatter(i, g):
                pool.wait_ge(s_out[0], i * NG + (g + 1 + ONE))
                pool.wait_ge(s_sidx[0], i * NG + (g + 1))
                pool.sem_inc(s_gate, 1)
                for c in range(GT):
                    t = g * GT + c
                    pool.wait_ge(s_put[0][c], i * (16 * NG) + (16 * g + FIRST))
                    pool.sem_inc(s_landed if c == GT - 1 else s_gate, 1)
                    nc.gpsimd.indirect_dma_start(lap_sums[c], bass.IndirectOffsetOnAxis(ap=idx_s[:, t:t + 1], axis=0),
                                                 sums[:, t, :], None, compute_op=ALU.add).then_inc(s_put[0][c], 16)

            def table_gather(i, g):
                pool.wait_ge(s_idx, i * NG + (g + 1))
                pool.sem_inc(s_gate, 1)
                for t in range(g * GT, (g + 1) * GT):
                    nc.gpsimd.indirect_dma_start(
                        rows_a[:, t, :], None, table,
                        bass.IndirectOffsetOnAxis(ap=idx_a[:, t:t + 1], axis=0)).then_inc(s_got[1][g], 16)

            def window_add(k):
                pool.wait_ge(s_wout, k + (1 + ONE))
                pool.sem_inc(s_gate, 1)
                pool.wait_ge(s_wadd, k * 16 + FIRST)
                pool.sem_inc(s_gate, 1)
                d0 = pool.value_load(first_dst[0:1, bass.ds(k, 1)], min_val=0, max_val=NP - 1)
                pool.dma_start(window_sums[bass.ds(d0, P), :], win_sb[:], accum_op=ALU.add).then_inc(s_wadd, 16)

            def gather_turn(i, first=False):
                for g in range(NG):
                    table_gather(i, g)
                    if g == 2 and not first:
                        window_add(i - 2)

            pool.wait_ge(s_flag, 1)
            unfit = pool.value_load(flag[0:1, 0:1], min_val=0, max_val=2 * P)
            with pool.If(unfit == 0):
                pool.sem_inc(s_landed, NG - 1)
                with pool.Fori(0, S) as i:
                    for g in range(NG):
                        window_scatter(i, g)
            with pool.Else():
                with pool.Fori(0, S) as i:
                    edge_turn(0, i)
            for b in range(2):
                pool.wait_ge(s_tst[b], 16 * (J // 2) + FIRST)
            pool.wait_ge(s_nst, 32)
            pool.sem_inc(s_gate, 1)
            with pool.If(unfit == 0):
                gather_turn(0, first=True)
                gather_turn(1, first=True)
                with pool.Fori(2, S) as i:
                    gather_turn(i)
                window_add(S - 2)
                window_add(S - 1)
            with pool.Else():
                with pool.Fori(0, S) as i:
                    edge_turn(1, i)

            with pool.Fori(0, J // 7) as i:
                pool.wait_ge(s_ci, i + 1)
                pool.sem_inc(s_gate, 1)
                for t in range(7):
                    nc.gpsimd.indirect_dma_start(
                        cg[:, t, :], None, self_dram,
                        bass.IndirectOffsetOnAxis(ap=cidx_s[:, t:t + 1], axis=0)).then_inc(s_cg, 16)

        @block.scalar
        def _(act):
            count_from_one(act, *s_rowb, *s_cast, *s_out, s_hT, s_npc, s_wout)

            def deviation(n):
                act.wait_ge(s_var, n + 1)
                nc.scalar.activation(stat[:, 2, :], stat[:, 1, :], ACT.Sqrt).then_inc(s_std, 1)

            def edge_turn(n, i):
                act.wait_ge(s_rawld[n], i * 48 + 48)
                act.sem_inc(s_agate, 1)
                rows = 64 if n == 0 else 96
                nc.scalar.copy(rawf[0:rows, :], raw[0:rows, :]).then_inc(s_cast[n], 1)
                for g in range(NG):
                    a, b = g * GT, (g + 1) * GT
                    if n == 1:
                        act.wait_ge(s_score, i * NG + (g + 1))
                        act.sem_inc(s_agate, 1)
                        nc.scalar.activation(score[:, 2, a:b], score[:, 1, a:b], ACT.Tanh,
                                             scale=float(F) ** -0.5).then_inc(s_att, 1)
                    act.wait_ge(s_sum[n], i * TS + (g + 1) * GT)
                    act.sem_inc(s_agate, 1)
                    o = (g // 2) * GT * M1
                    width = M1 if n == 0 else F
                    nc.scalar.copy(sums[:, a:b, 0:width], sum_ps[g % 2][:, o:o + GT * M1].rearrange(
                        "p (t f) -> p t f", f=M1)[:, :, 0:width]).then_inc(s_out[n], 1)

            act.wait_ge(s_zt, 2)
            nc.scalar.copy(raw[:], zeros[:, 0:P]).then_inc(s_agate, 1)
            nc.scalar.copy(rawf[:], zeros[:, 0:P]).then_inc(s_agate, 1)
            nc.scalar.copy(rowi[:], zeros[:, 0:P]).then_inc(s_agate, 1)
            deviation(0)
            act.wait_ge(s_agate, 3)
            def cast_rows(n, i):
                act.wait_ge(s_rowm[n], i + (1 + ONE))
                act.wait_ge(s_row[n], i * TS + ONE)
                act.sem_inc(s_agate, 1)
                nc.scalar.copy(rowb[:], rowm[:]).then_inc(s_rowb[n], 1)

            def split_window(n, i):
                act.wait_ge(s_winld[n], i * 16 + 16)
                act.wait_ge(s_sel[n], i * TS + (SEL_START if n else ONE))
                act.sem_inc(s_agate, 1)
                nc.scalar.copy(window3[:, 0, :], window[:]).then_inc(s_whi[n], 1)
                act.wait_ge(s_wrest[n], i + 1)
                act.sem_inc(s_agate, 1)
                nc.scalar.copy(window3[:, 1, :], wide_window[:]).then_inc(s_wmid[n], 1)

            def first_part(n, i, g):
                act.wait_ge(s_val[n], i * NG + (g + 1 + (VAL_START if n else ONE)))
                act.sem_inc(s_agate, 1)
                nc.scalar.copy(parts3[0][:, g * GT:(g + 1) * GT, :], val2[:, g * GT:(g + 1) * GT, 0, :]).then_inc(s_hi[n], 1)

            def second_part(n, i, g):
                act.wait_ge(s_rest[n], i * NG + (g + 1))
                act.sem_inc(s_agate, 1)
                nc.scalar.copy(parts3[1][:, g * GT:(g + 1) * GT, :], wide[:]).then_inc(s_mid[n], 1)

            def window_turn0(i):
                act.wait_ge(s_rawld[0], i * 48 + 48)
                act.wait_ge(s_cols[0], i + ONE)
                act.sem_inc(s_agate, 1)
                nc.scalar.copy(rawf[0:64, :], raw[0:64, :]).then_inc(s_agate, 1)
                nc.scalar.copy(rawf[64:64 + TS, :], wraw[0:TS, :]).then_inc(s_cast[0], 1)
                cast_rows(0, i)
                split_window(0, i)
                for g in range(NG):
                    first_part(0, i, g)
                    second_part(0, i, g)
                    act.wait_ge(s_landed, i * NG + (g + 1))
                    act.wait_ge(s_sum[0], i * NG + (g + 1 + NG))
                    act.sem_inc(s_agate, 1)
                    nc.scalar.copy(sums[:, g * GT:(g + 1) * GT, :], sum_ps[g % 2][:, 0:GT * M1].rearrange(
                        "p (t f) -> p t f", f=M1)).then_inc(s_out[0], 1)

            def cast1(k):
                act.wait_ge(s_rawld[1], k * 64 + 64)
                act.sem_inc(s_agate, 1)
                nc.scalar.copy(rawf[:], raw[:]).then_inc(s_cast[1], 1)

            def window_out(k):
                act.wait_ge(s_sum[1], k * NG + 2 * NG)
                act.wait_ge(s_wadd, k * 16 + FIRST)
                act.sem_inc(s_agate, 1)
                nc.scalar.copy(win_sb[:], banks[1][:, 0:M1]).then_inc(s_wout, 1)

            def group1(i, g, last=True):
                act.wait_ge(s_score, i * NG + (g + 1))
                act.sem_inc(s_agate, 1)
                nc.scalar.activation(score[:, 2, g * GT:(g + 1) * GT], score[:, 1, g * GT:(g + 1) * GT], ACT.Tanh,
                                     scale=float(F) ** -0.5).then_inc(s_att, 1)
                first_part(1, i, g)
                if g == NG - 2 and not last:
                    cast_rows(1, i + 1)
                second_part(1, i, g)

            def window_turn1(i, first=False, last=False):
                split_window(1, i)
                if not last:
                    act.wait_ge(s_cols[1], i + (1 + ONE))
                    act.sem_inc(s_agate, 1)
                    cast1(i + 1)
                if not first:
                    group1(i - 1, NG - 1)
                for g in range(NG - 1):
                    group1(i, g, last)
                    if g == 0 and not first:
                        window_out(i - 1)

            act.wait_ge(s_flag, 1)
            unfit = act.value_load(flag[0:1, 0:1], min_val=0, max_val=2 * P)
            with act.If(unfit == 0):
                with act.Fori(0, S) as i:
                    window_turn0(i)
            with act.Else():
                with act.Fori(0, S) as i:
                    edge_turn(0, i)
            deviation(1)
            act.sem_inc(s_ca, chunks_of_act)
            act.sem_inc(s_npc, 1)

            def turned_rows(j, b):
                act.wait_ge(s_hst, j + (1 + ONE))
                act.sem_inc(s_agate, 1)
                nc.scalar.copy(hT[:, b, :], turn_ps[0:PR, 0:P]).then_inc(s_hT, 1)

            def node_pair(i, last=False):
                for b in range(2):
                    j = i * 2 + b
                    if not (last and b):
                        turned_rows(j + 1, 1 - b)
                    act.wait_ge(s_tst[b], i * 16 + FIRST)
                    for q, (r, n) in list(enumerate(full_chunks))[0::2]:
                        act.wait_ge(s_tp, i * (2 * len(full_chunks)) + (b * len(full_chunks) + q + 1))
                        act.sem_inc(s_agate, 1)
                        nc.scalar.copy(tb[b][:, r // 2:(r + n) // 2, 0:2 * M1],
                                       chunk_ps[q][:, 0:n * M1].rearrange("p (h c) -> p h c", c=2 * M1)).then_inc(s_ca, 1)
                    act.wait_ge(s_xh, j + (1 + ONE))
                    act.sem_inc(s_agate, 1)
                    nc.scalar.copy(yhn[:, bass.ds(j, 1), :].rearrange("p j f -> p (j f)"),
                                   nrow[:, b, F:2 * F]).then_inc(s_agate, 1)
                    nc.scalar.copy(sfn[:, bass.ds(j, 1), :].rearrange("p j f -> p (j f)"),
                                   nrow[:, b, 2 * F:3 * F]).then_inc(s_npc, 1)

            turned_rows(0, 0)
            with act.Fori(0, J // 2 - 1) as i:
                node_pair(i)
            node_pair(J // 2 - 1, last=True)
            with act.If(unfit == 0):
                cast1(0)
                cast_rows(1, 0)
                window_turn1(0, first=True)
                with act.Fori(1, S - 1) as i:
                    window_turn1(i)
                window_turn1(S - 1, last=True)
                group1(S - 1, NG - 1)
                window_out(S - 1)
            with act.Else():
                with act.Fori(0, S) as i:
                    edge_turn(1, i)

        @block.tensor
        def _(pe):
            count_from_one(pe, *s_row, s_hst, *s_sel, *s_cols)
            pe.sem_inc(s_sel[1], SEL_START - ONE)
            pe.wait_ge(s_const, 8)
            pe.wait_ge(s_w, 16 * NW_DMAS)
            nc.tensor.transpose(banks[0][0:F, 0:R], rel_sb[:], ident[0:R, 0:R])
            nc.tensor.transpose(banks[1][0:B, 0:R], wc_sb[:], ident[0:R, 0:R])
            nc.tensor.matmul(banks[2][0:F + 1, 0:F], a1[:], ident[0:F, 0:F], start=True, stop=True)
            nc.tensor.matmul(banks[3][0:F + 1, 0:F], a2[:], ident[0:F, 0:F], start=True, stop=True).then_inc(s_wt, 1)
            pe.wait_ge(s_wtc, 1)
            for q in range(7):
                k = 5 if q < 6 else 2
                if q >= 1:
                    pe.wait_ge(s_wtc, q + 1)
                for m in range(k):
                    o = q * 5 + m
                    ins = nc.tensor.matmul(banks[q % 2][0:F, m * R:(m + 1) * R], w_sb[:, :, o], wcT[:],
                                           start=True, stop=True)
                ins.then_inc(s_wp, 1)
            nc.tensor.matmul(banks[2][0:F + 1, 0:R], a1[:], relT[:], start=True, stop=True).then_inc(s_wp, 1)

            def edge_turn(n, i):
                pe.wait_ge(s_cast[n], i + 1 + ONE)
                pe.wait_ge(s_rawld[n], i * 48 + 48)
                pe.wait_ge(s_stage[n], i + ONE)
                nc.tensor.transpose(cols_ps[:, 0:P], rawf[:], ident[:]).then_inc(s_cols[n], 1)
                for t in range(TS):
                    pe.wait_ge(s_eq[n], i * TS + max(t - 1, 0) + ONE)
                    nc.tensor.matmul(row_ps[t % 2], (row_of_dst if n else row_of_src)[:, t, :], rawf[:],
                                     start=True, stop=True).then_inc(s_row[n], 1)
                    if t >= GT - 1 and t % GT == GT - 1:
                        g = t // GT
                        pe.wait_ge(s_eq[n], i * TS + (t + 1) + ONE)
                        pe.wait_ge(s_val[n], i * NG + (g + 1))
                        pe.wait_ge(s_out[n], i * NG + max(g - 1, 0) + ONE)
                        for c in range(GT):
                            o = (g // 2) * GT * M1 + c * M1
                            k = g * GT + c
                            if n == 0:
                                ins = nc.tensor.matmul(sum_ps[g % 2][:, o:o + M1], eq[:, k, :], val[:, k, :],
                                                       start=True, stop=True)
                            else:
                                for h in range(2):
                                    ins = nc.tensor.matmul(sum_ps[g % 2][:, o:o + F], eq[:, k, :], val2[:, k, h, 0:F],
                                                           start=h == 0, stop=h == 1)
                            ins.then_inc(s_sum[n], 1)

            def spread(n, i, t):
                pe.wait_ge(s_cmp[n], i * TS + (max(t - 1, 0) + ONE))
                if n == 0:
                    nc.tensor.matmul(row_ps[t % 2], src_bits[:, t, :], rowb[:], start=True, stop=True)
                    nc.tensor.matmul(banks[3 + t % 2][:, P:2 * P], dst_bits[:, t, :], rowb[:],
                                     start=True, stop=True).then_inc(s_row[n], 1)
                else:
                    nc.tensor.matmul(row_ps[t % 2], dst_bits[:, t, :], rowb[:],
                                     start=True, stop=True).then_inc(s_row[n], 1)

            def select(n, i, t):
                g = t // GT
                pe.wait_ge(s_cmp[n], i * TS + (t + 1 + ONE))
                if t == 0:
                    pe.wait_ge(s_wpart[n], i + (1 + ONE))
                if t % GT == 0:
                    pe.wait_ge(s_val[n], i * NG + (BANK_FREE[g] + VAL_START if n else max(g - 1, 0) + ONE))
                for q in range(3):
                    ins = nc.tensor.matmul(banks[GROUP_BANK[g] if n else 5 + g % 2][:, (t % GT) * F:(t % GT + 1) * F], at_window[:, t % GT, :],
                                           window3[:, q, :], start=q == 0, stop=q == 2)
                ins.then_inc(s_sel[n], 1)

            def turn_columns(n, k):
                pe.wait_ge(s_cast[n], k + (1 + ONE))
                pe.wait_ge(s_stage[n], k + ONE)
                nc.tensor.transpose(cols_ps[:, 0:P], rawf[:], ident[:]).then_inc(s_cols[n], 1)

            def group_sums(i, g):
                pe.wait_ge(s_parts[0], i * NG + (g + 1))
                pe.wait_ge(s_out[0], i * NG + (max(g - 1, 0) + ONE))
                for c in range(GT):
                    k = g * GT + c
                    for q in range(3):
                        ins = nc.tensor.matmul(sum_ps[g % 2][:, c * M1:(c + 1) * M1], same[:, k, :], parts3[q][:, k, :],
                                               start=q == 0, stop=q == 2)
                ins.then_inc(s_sum[0], 1)

            def window_sum(i, k):
                g = k // GT
                if k % GT == 0:
                    pe.wait_ge(s_parts[1], i * NG + (g + 1))
                if k == 0:
                    pe.wait_ge(s_wout, i + ONE)
                for q in range(3):
                    ins = nc.tensor.matmul(banks[1][:, 0:M1], same[:, k, :], parts3[q][:, k, :],
                                           start=k == 0 and q == 0, stop=k == TS - 1 and q == 2)
                if k % GT == GT - 1:
                    ins.then_inc(s_sum[1], 1)

            def window_turn0(i):
                turn_columns(0, i)
                pe.wait_ge(s_rowb[0], i + (1 + ONE))
                for t in range(TS + 1):
                    if t < TS:
                        spread(0, i, t)
                    if t >= 1:
                        select(0, i, t - 1)
                    if t >= GT + DELAY and (t - DELAY) % GT == 0:
                        group_sums(i, (t - DELAY) // GT - 1)
                group_sums(i, NG - 1)

            def window_turn1(i, first=False, last=False):
                pe.wait_ge(s_rowb[1], i + (1 + ONE))
                for t in range(TS):
                    spread(1, i, t)
                    if t >= 1:
                        select(1, i, t - 1)
                    elif not first:
                        select(1, i - 1, TS - 1)
                    if t == 1 and not last:
                        turn_columns(1, i + 1)
                    if t >= SUM_LAG:
                        window_sum(i, t - SUM_LAG)
                    elif not first:
                        window_sum(i - 1, t - SUM_LAG + TS)

            pe.wait_ge(s_bad, 1)
            nc.tensor.matmul(banks[5][0:1, 0:1], odds[:, 2:3], tri[:, P - 1:P], start=True, stop=True).then_inc(s_badsum, 1)
            pe.wait_ge(s_const, 9)
            pe.wait_ge(s_flag, 1)
            unfit = pe.value_load(flag[0:1, 0:1], min_val=0, max_val=2 * P)
            with pe.If(unfit == 0):
                pe.sem_inc(s_sum[0], NG)
                pe.wait_ge(s_selectors, 6)
                with pe.Fori(0, S) as i:
                    window_turn0(i)
            with pe.Else():
                with pe.Fori(0, S) as i:
                    edge_turn(0, i)

            pe.wait_ge(s_wready, 1)
            pe.wait_ge(s_copies, 16 * 6)

            def turn_node(j, b):
                pe.wait_ge(s_hs, j + 1)
                pe.wait_ge(s_hT, j + ONE)
                nc.tensor.matmul(turn_ps[0:PR, 0:P], hs[:, b, 0:PR], ident16[:], start=True, stop=True).then_inc(s_hst, 1)

            def product(place, b, weights):
                for q in range(3):
                    ins = nc.tensor.matmul(place, hT[:, b, :], weights(q), start=q == 0, stop=q == 2)
                return ins

            def relations(r, n):
                return lambda q: TW3[:, q, r:r + n, :].rearrange("p r c -> p (r c)")

            def node_pair(i, last=False):
                for b in range(2):
                    j = i * 2 + b
                    if not (last and b):
                        turn_node(j + 1, 1 - b)
                    pe.wait_ge(s_hT, j + (1 + ONE))
                    pe.wait_ge(s_xh, j + ONE)
                    product(node_ps[:, 0:3 * F], b, lambda q: NW3[:, q, :])
                    r, n = last_chunk
                    product(node_ps[:, 3 * F:3 * F + n * M1], b, relations(r, n)).then_inc(s_np, 1)
                    for q, (r, n) in enumerate(full_chunks):
                        if q % 2 == 0:
                            pe.wait_ge(s_ca, i * (2 * chunks_of_act) + (b * chunks_of_act + q // 2 + 1))
                        else:
                            pe.wait_ge(s_cv, i * (2 * chunks_of_dve) + (b * chunks_of_dve + q // 2 + 1))
                        product(chunk_ps[q][:, 0:n * M1], b, relations(r, n)).then_inc(s_tp, 1)

            turn_node(0, 0)
            with pe.Fori(0, J // 2 - 1) as i:
                node_pair(i)
            node_pair(J // 2 - 1, last=True)
            with pe.If(unfit == 0):
                pe.sem_inc(s_sum[1], NG)
                turn_columns(1, 0)
                window_turn1(0, first=True)
                with pe.Fori(1, S - 1) as i:
                    window_turn1(i)
                window_turn1(S - 1, last=True)
                select(1, S - 1, TS - 1)
                for k in range(TS - SUM_LAG, TS):
                    window_sum(S - 1, k)
            with pe.Else():
                with pe.Fori(0, S) as i:
                    edge_turn(1, i)

        @block.vector
        def _(dve):
            count_from_one(dve, *s_stage, *s_eq, s_xh, *s_cmp, *s_rowm, *s_wpart)
            steps = Steps(dve, s_v)

            def bc(a):
                return a.unsqueeze(2).broadcast_to([P, J, F])

            def layer_norm(n):
                steps.done(nc.vector.tensor_reduce(stat[:, 0, :], xn[:], AX_X, ALU.add))
                steps.done(nc.vector.tensor_scalar(stat[:, 1, :], stat[:, 0, :], 1.0 / F, None, ALU.mult))
                steps.done(nc.vector.tensor_tensor(hn[:], xn[:], bc(stat[:, 1, :]), ALU.subtract))
                steps.done(nc.vector.tensor_tensor(sq[:], hn[:], hn[:], ALU.mult))
                steps.done(nc.vector.tensor_reduce(stat[:, 0, :], sq[:], AX_X, ALU.add))
                nc.vector.tensor_scalar(stat[:, 1, :], stat[:, 0, :], 1.0 / F, EPS, ALU.mult, ALU.add).then_inc(s_var, 1)
                dve.wait_ge(s_std, n + 1)
                steps.done(nc.vector.reciprocal(stat[:, 3, :], stat[:, 2, :]))
                steps.done(nc.vector.tensor_tensor(hn[:], hn[:], bc(stat[:, 3, :]), ALU.mult))
                nc.vector.tensor_scalar(hn[:], hn[:], 0.0, None, ALU.max).then_inc(s_h1 if n else s_h0, 1)

            nc.vector.memset(chk[:, CE:CE + 1], 1 << 20).then_inc(s_chk0, 1)
            nc.vector.memset(ends[:], 0).then_inc(s_chk0, 1)
            dve.wait_ge(s_x, 48)
            layer_norm(0)

            dve.wait_ge(s_chk, 16 * 5)
            steps.done(nc.vector.tensor_tensor(rises, chk[:, 1:CE + 1], chk[:, 0:CE], ALU.subtract))
            steps.done(nc.vector.tensor_reduce(odds[:, 0:1], rises, AX_X, ALU.min))
            steps.done(nc.vector.tensor_tensor(odds[:, 1:2], ends[:, 1:2], ends[:, 0:1], ALU.subtract))
            steps.done(nc.vector.tensor_scalar(odds[:, 0:1], odds[:, 0:1], 0.0, None, ALU.is_lt))
            steps.done(nc.vector.tensor_scalar(odds[:, 1:2], odds[:, 1:2], float(P - 1), None, ALU.is_gt))
            nc.vector.tensor_tensor(odds[:, 2:3], odds[:, 0:1], odds[:, 1:2], ALU.add).then_inc(s_bad, 1)

            dve.wait_ge(s_wt, 1)
            nc.vector.tensor_copy(NW[:, 0:F], banks[2][0:F + 1, 0:F]).then_inc(s_v, 1)
            nc.vector.tensor_copy(NW[:, F:2 * F], banks[3][0:F + 1, 0:F]).then_inc(s_v, 1)
            nc.vector.tensor_copy(relT[:], banks[0][0:F, 0:R]).then_inc(s_v, 1)
            steps.n += 3
            nc.vector.tensor_copy(wcT[:], banks[1][0:B, 0:R]).then_inc(s_v, 1)
            steps.n += 1
            nc.vector.memset(TW[F:F + 1, :, 0:F], 0.0).then_inc(s_v, 1)
            steps.n += 1
            dve.wait_ge(s_v, steps.value())
            dve.sem_inc(s_wtc, 1)
            for q in range(7):
                k = 5 if q < 6 else 2
                dve.wait_ge(s_wp, q + 1)
                nc.vector.tensor_copy(TW[0:F, :, q * 5:q * 5 + k],
                                      banks[q % 2][0:F, 0:k * R].rearrange("p (o r) -> p r o", o=k)).then_inc(s_wtc, 1)
            dve.wait_ge(s_wp, 8)
            dve.wait_ge(s_wtc, 8)
            steps.done(nc.vector.tensor_copy(TW[:, :, F:F + 1], banks[2][0:F + 1, 0:R].unsqueeze(2)))
            for whole_weights, parts in ((TW, TW3), (NW[:], NW3)):
                steps.done(nc.vector.tensor_copy(parts[0:F + 1, 0], whole_weights))
                steps.done(nc.vector.tensor_tensor(whole_weights, whole_weights, parts[0:F + 1, 0], ALU.subtract))
                steps.done(nc.vector.tensor_copy(parts[0:F + 1, 1], whole_weights))
                steps.done(nc.vector.tensor_tensor(parts[0:F + 1, 2], whole_weights, parts[0:F + 1, 1], ALU.subtract))
            dve.sem_inc(s_wready, 1)
            dve.wait_ge(s_const, 8)
            steps.done(nc.vector.tensor_copy(ident16[:], ident[:]))
            nc.vector.tensor_copy(row_of_src[:], ident[:, 0:TS].unsqueeze(2).broadcast_to([P, TS, P])).then_inc(s_v, 1)
            nc.vector.tensor_copy(row_of_dst[:], ident[:, 32:32 + TS].unsqueeze(2).broadcast_to([P, TS, P])).then_inc(s_const, 1)
            steps.n += 1

            def edge_turn(n, i, per_turn):
                steps = Steps(dve, s_dve[n], i, per_turn)
                key = 0 if n == 0 else 32
                for c in range(GT):
                    dve.wait_ge(s_put[n][c], i * (16 * NG) + FIRST)
                    if n:
                        dve.wait_ge(s_lastput[c], i * (16 * NG) + FIRST)
                dve.wait_ge(s_cols[n], i + (1 + ONE))
                steps.done(nc.vector.tensor_copy(cols[:], cols_ps[:, 0:P]))
                kcols = cols[:, key:key + TS]
                if n == 0:
                    steps.done(nc.vector.tensor_copy(idx_a[:], cols[:, 32:32 + TS]))
                else:
                    steps.done(nc.vector.tensor_copy(et_i[:], cols[:, 64:64 + TS]))
                    steps.done(nc.vector.tensor_scalar(et_i[:], et_i[:], 1, None, ALU.bitwise_and))
                    steps.done(nc.vector.tensor_copy(odd[:, :, 1:2], et_i[:].unsqueeze(2)))
                    steps.done(nc.vector.tensor_scalar(odd[:, :, 0:1], odd[:, :, 1:2], -1.0, 1.0, ALU.mult, ALU.add))
                    steps.done(nc.vector.scalar_tensor_tensor(out=picked[:], in0=cols[:, 0:TS], scalar=float(R),
                                                              in1=cols[:, 64:64 + TS], op0=ALU.mult, op1=ALU.add))
                    steps.done(nc.vector.tensor_tensor(picked[:].unsqueeze(2), picked[:].unsqueeze(2), odd[:, :, 1:2], ALU.subtract))
                    steps.done(nc.vector.tensor_scalar(idx_a[:], picked[:], 0.5, None, ALU.mult))
                    steps.done(nc.vector.tensor_copy(idx_b[:], cols[:, 32:32 + TS]))
                    steps.done(nc.vector.tensor_copy(lastrow[:, :, 0:1], eno[:].unsqueeze(2)))
                    steps.done(nc.vector.tensor_scalar(lastrow[:, :, 1:2], cols[:, 0:TS].unsqueeze(2), 1.0, None, ALU.add))
                    steps.done(nc.vector.tensor_scalar(eno[:], eno[:], float(SE), None, ALU.add))
                nc.vector.tensor_scalar(shifted[:], kcols, trash[:, 0:1], None, ALU.subtract).then_inc(s_stage[n], 1)
                for g in range(NG):
                    a, b = g * GT, (g + 1) * GT
                    for t in range(a, b):
                        dve.wait_ge(s_row[n], i * TS + (t + 1) + ONE)
                        nc.vector.scalar_tensor_tensor(out=eq[:, t, :], in0=row_ps[t % 2],
                                                       scalar=cols[:, key + t:key + t + 1], in1=tri[:],
                                                       op0=ALU.is_equal, op1=ALU.mult,
                                                       accum_out=cnt[:, t:t + 1]).then_inc(s_eq[n], 1)
                    dve.wait_ge(s_eq[n], i * TS + b + ONE)
                    dve.wait_ge(s_stage[n], i + 1 + ONE)
                    steps.done(nc.vector.scalar_tensor_tensor(out=picked[:, a:b], in0=cnt[:, a:b], scalar=1.0,
                                                              in1=shifted[:, a:b], op0=ALU.is_equal, op1=ALU.mult))
                    nc.vector.tensor_scalar(idx_s[:, a:b], picked[:, a:b], trash[:, 0:1], None,
                                            ALU.add).then_inc(s_sidx[n], 1)
                    dve.wait_ge(s_got[n][g], i * (16 * GT * (n + 1)) + 16 * GT * (n + 1))
                    if n == 0:
                        w = cols[:, 64 + a:64 + b].unsqueeze(2)
                        steps.done(nc.vector.tensor_copy(val[:, a:b, F:F + 1], w))
                        nc.vector.tensor_tensor(val[:, a:b, 0:F], rows_b[:, a:b, :], w.broadcast_to([P, GT, F]),
                                                ALU.mult).then_inc(s_val[n], 1)
                    else:
                        pair = rows_a[:, a:b, 0:2 * M1].rearrange("p t (h c) -> p t h c", h=2)
                        steps.done(nc.vector.tensor_tensor(prod[:, a:b, 0:F], rows_a[:, a:b, 2 * M1:TR], rows_b[:, a:b, :], ALU.mult))
                        steps.done(nc.vector.tensor_tensor(prod[:, a:b, F:F + 2].unsqueeze(3), pair[:, :, :, F:M1],
                                                           odd[:, a:b, :].unsqueeze(3), ALU.mult))
                        steps.done(nc.vector.tensor_reduce(score[:, 0, a:b], prod[:, a:b, :], AX_X, ALU.add))
                        nc.vector.tensor_scalar(score[:, 1, a:b], score[:, 0, a:b], 0.0, None, ALU.max).then_inc(s_score, 1)
                        dve.wait_ge(s_att, i * NG + (g + 1))
                        steps.done(nc.vector.scalar_tensor_tensor(out=weight2[:, a:b, :], in0=score[:, 2, a:b].unsqueeze(2).broadcast_to([P, GT, 2]),
                                                                  scalar=0.0, in1=odd[:, a:b, :], op0=ALU.max, op1=ALU.mult))
                        nc.vector.tensor_tensor(val2[:, a:b, :, 0:F], pair[:, :, :, 0:F],
                                                weight2[:, a:b, :].unsqueeze(3).broadcast_to([P, GT, 2, F]),
                                                ALU.mult).then_inc(s_val[n], 1)
                assert steps.n == per_turn, steps.n

            def compare(n, i, t, chain):
                dve.wait_ge(s_row[n], i * TS + (t + 1 + ONE))
                dst_ps = banks[3 + t % 2][:, P:2 * P] if n == 0 else row_ps[t % 2]
                if t == 0:
                    nc.vector.tensor_copy(base[:, 0:1], dst_ps[:, 0:1]).then_inc(chain.sem, 1)
                    chain.n += 1
                    chain.done(nc.vector.tensor_scalar(base[:, 1:2], dst_ps[:, 0:1], part[:, 0:1], None, ALU.add))
                dve.wait_ge(s_sel[n], i * TS + (t - GT + 1 + SEL_START if n else max(t - GT + 1, 0) + ONE))
                if t % GT == 0:
                    dve.wait_ge(s_sum[n], i * NG + (t // GT + 1))
                ins = nc.vector.tensor_scalar(at_window[:, t % GT, :], dst_ps, base[:, 1:2], None, ALU.is_equal)
                if n == 0:
                    nc.vector.scalar_tensor_tensor(out=same[:, t, :], in0=row_ps[t % 2], scalar=cols[:, t:t + 1], in1=tri[:],
                                                   op0=ALU.is_equal, op1=ALU.mult,
                                                   accum_out=cnt[:, t:t + 1]).then_inc(s_cmp[n], 1)
                else:
                    ins.then_inc(s_cmp[n], 1)
                    if t == 0:
                        chain.done(nc.vector.tensor_scalar(in_window[:], cols_next[:, 32:32 + TS], base[:, 0:1], None, ALU.subtract))
                    nc.vector.tensor_scalar(same[:, t, :], iota_row[:], in_window[:, t:t + 1], None, ALU.is_equal)

            def start_turn(n, i):
                dve.wait_ge(s_rowld[n], i * (64 // (1 + n)) + 64 // (1 + n))
                dve.wait_ge(s_rowb[n], i + ONE)
                nc.vector.tensor_scalar(rowm[:], rowi[:], row_mask[:, 0:1], None, ALU.bitwise_and).then_inc(s_rowm[n], 1)

            def window_parts(n, i):
                dve.wait_ge(s_whi[n], i + 1)
                nc.vector.tensor_tensor(wide_window[:], window[:], window3[:, 0, :], ALU.subtract).then_inc(s_wrest[n], 1)
                dve.wait_ge(s_wmid[n], i + 1)
                dve.wait_ge(s_wrest[n], i + 1)
                nc.vector.tensor_tensor(window3[:, 2, :], wide_window[:], window3[:, 1, :], ALU.subtract).then_inc(s_wpart[n], 1)

            def rest(n, i, g):
                dve.wait_ge(s_hi[n], i * NG + (g + 1))
                nc.vector.tensor_tensor(wide[:], val2[:, g * GT:(g + 1) * GT, 0, :],
                                        parts3[0][:, g * GT:(g + 1) * GT, :], ALU.subtract).then_inc(s_rest[n], 1)

            def third_part(n, i, g):
                dve.wait_ge(s_mid[n], i * NG + (g + 1))
                dve.wait_ge(s_rest[n], i * NG + (g + 1))
                nc.vector.tensor_tensor(parts3[2][:, g * GT:(g + 1) * GT, :], wide[:],
                                        parts3[1][:, g * GT:(g + 1) * GT, :], ALU.subtract).then_inc(s_parts[n], 1)

            def values0(i, g, chain):
                a, b = g * GT, (g + 1) * GT
                w = cols[:, 64 + a:64 + b].unsqueeze(2)
                dve.wait_ge(s_cmp[0], i * TS + (b + ONE))
                chain.done(nc.vector.scalar_tensor_tensor(out=picked[:, a:b], in0=cnt[:, a:b], scalar=1.0,
                                                          in1=shifted[:, a:b], op0=ALU.is_equal, op1=ALU.mult))
                dve.wait_ge(s_landed, i * NG + (g + 1))
                nc.vector.tensor_scalar(idx_s[:, a:b], picked[:, a:b], trash[:, 0:1], None, ALU.add).then_inc(s_sidx[0], 1)
                dve.wait_ge(s_sel[0], i * TS + (b + ONE))
                nc.vector.tensor_copy(val2[:, a:b, 0, F:M1], w)
                nc.vector.tensor_tensor(val2[:, a:b, 0, 0:F], banks[5 + g % 2][:, 0:GT * F].rearrange("p (t f) -> p t f", f=F),
                                        w.broadcast_to([P, GT, F]), ALU.mult).then_inc(s_val[0], 1)

            def window_turn0(i):
                chain = Steps(dve, s_edge[0], i, 9)
                start_turn(0, i)
                dve.wait_ge(s_cols[0], i + (1 + ONE))
                chain.done(nc.vector.tensor_copy(cols[:], cols_ps[:, 0:P]))
                chain.done(nc.vector.tensor_scalar(shifted[:], cols[:, 0:TS], trash[:, 0:1], None, ALU.subtract))
                dve.sem_inc(s_stage[0], 1)
                for t in range(TS):
                    compare(0, i, t, chain)
                    if t == 0:
                        window_parts(0, i)
                    if t > GT and t % GT == 1:
                        values0(i, t // GT - 1, chain)
                    if t > GT and t % GT == 2:
                        rest(0, i, t // GT - 1)
                    if t > GT and t % GT == 3:
                        third_part(0, i, t // GT - 1)
                values0(i, NG - 1, chain)
                rest(0, i, NG - 1)
                third_part(0, i, NG - 1)
                assert chain.n == chain.per_turn, chain.n

            def stage1(chain):
                chain.done(nc.vector.tensor_copy(cols_next[:], cols_ps[:, 0:P]))
                dve.sem_inc(s_stage[1], 1)
                chain.done(nc.vector.tensor_copy(et_i[:], cols_next[:, 64:64 + TS]))
                chain.done(nc.vector.tensor_scalar(et_i[:], et_i[:], 1, None, ALU.bitwise_and))
                chain.done(nc.vector.tensor_copy(odd_next[:, :, 1:2], et_i[:].unsqueeze(2)))
                chain.done(nc.vector.tensor_scalar(odd_next[:, :, 0:1], odd_next[:, :, 1:2], -1.0, 1.0, ALU.mult, ALU.add))
                chain.done(nc.vector.scalar_tensor_tensor(out=double_idx[:], in0=cols_next[:, 0:TS], scalar=float(R),
                                                          in1=cols_next[:, 64:64 + TS], op0=ALU.mult, op1=ALU.add))
                chain.done(nc.vector.tensor_tensor(double_idx[:].unsqueeze(2), double_idx[:].unsqueeze(2),
                                                   odd_next[:, :, 1:2], ALU.subtract))

            def index1(g):
                a, b = g * GT, (g + 1) * GT
                nc.vector.tensor_scalar(idx_a[:, a:b], double_idx[:, a:b], 0.5, None, ALU.mult).then_inc(s_idx, 1)

            def scores1(i, g, chain):
                a, b = g * GT, (g + 1) * GT
                pair = rows_a[:, a:b, 0:2 * M1].rearrange("p t (h c) -> p t h c", h=2)
                dve.wait_ge(s_got[1][g], i * (16 * GT) + 16 * GT)
                dve.wait_ge(s_sel[1], i * TS + (b + SEL_START))
                nc.vector.tensor_tensor(prod[:, a:b, F:F + 2].unsqueeze(3), pair[:, :, :, F:M1],
                                        odd[:, a:b, :].unsqueeze(3), ALU.mult)
                chain.done(nc.vector.tensor_tensor(prod[:, a:b, 0:F], rows_a[:, a:b, 2 * M1:TR],
                                                   banks[GROUP_BANK[g]][:, 0:GT * F].rearrange("p (t f) -> p t f", f=F), ALU.mult))
                chain.done(nc.vector.tensor_reduce(score[:, 0, a:b], prod[:, a:b, :], AX_X, ALU.add))
                nc.vector.tensor_scalar(score[:, 1, a:b], score[:, 0, a:b], 0.0, None, ALU.max).then_inc(s_score, 1)

            def values1(i, g, chain, last):
                a, b = g * GT, (g + 1) * GT
                pair = rows_a[:, a:b, 0:2 * M1].rearrange("p t (h c) -> p t h c", h=2)
                dve.wait_ge(s_att, i * NG + (g + 1))
                chain.done(nc.vector.scalar_tensor_tensor(out=weight2[:, a:b, :], in0=score[:, 2, a:b].unsqueeze(2).broadcast_to([P, GT, 2]),
                                                          scalar=0.0, in1=odd[:, a:b, :], op0=ALU.max, op1=ALU.mult))
                nc.vector.tensor_copy(val2[:, a:b, 0, F:M1], last_val[:, a:b].unsqueeze(2))
                chain.done(nc.vector.tensor_tensor(val2[:, a:b, :, 0:F], pair[:, :, :, 0:F],
                                                   weight2[:, a:b, :].unsqueeze(3).broadcast_to([P, GT, 2, F]), ALU.mult))
                nc.vector.tensor_tensor(val2[:, a:b, 0, 0:F], val2[:, a:b, 0, 0:F], val2[:, a:b, 1, 0:F],
                                        ALU.add).then_inc(s_val[1], 1)
                if not last:
                    index1(g)

            GROUP_STEPS, REST_STEPS = 4, 6 + STAGE_STEPS

            def kept1(chain):
                chain.done(nc.vector.tensor_copy(odd[:], odd_next[:]))
                chain.done(nc.vector.tensor_tensor(picked[:], cols_next[:, 32:32 + TS], cols_next[:, 96:96 + TS], ALU.not_equal))
                chain.done(nc.vector.scalar_tensor_tensor(out=last_val[:], in0=cols_next[:, 0:TS], scalar=1.0, in1=picked[:],
                                                          op0=ALU.add, op1=ALU.mult))

            def window_turn1(i, first=False, last=False):
                chain = Steps(dve, s_edge[1], i, NG * GROUP_STEPS + REST_STEPS, start=STAGE_STEPS - (0 if first else GROUP_STEPS))
                for t in range(TS):
                    compare(1, i, t, chain)
                    k, g = (i, t // GT - 1) if t >= GT else (i - 1, NG - 1)
                    before, h = (i, t // GT - 2) if t >= 2 * GT else (i - 1, t // GT - 2 + NG)
                    if t >= GT or not first:
                        if t % GT == 1:
                            scores1(k, g, chain)
                        if t % GT == 2:
                            values1(k, g, chain, last and t >= GT)
                        if t % GT == 4:
                            rest(1, k, g)
                    if t % GT == 0 and (t >= 2 * GT or not first):
                        third_part(1, before, h)
                    if t == 0:
                        window_parts(1, i)
                    if t == 3:
                        kept1(chain)
                    if t == GT and not last:
                        dve.wait_ge(s_cols[1], i + (2 + ONE))
                        stage1(chain)
                    if t == TS - 4 and not last:
                        start_turn(1, i + 1)
                return chain

            dve.wait_ge(s_badsum, 1)
            nc.vector.tensor_copy(flag[:], banks[5][0:1, 0:1]).then_inc(s_flag, 1)
            dve.wait_ge(s_flag, 1)
            unfit = dve.value_load(flag[0:1, 0:1], min_val=0, max_val=2 * P)
            dve.wait_ge(s_const, 9)
            with dve.If(unfit == 0):
                dve.sem_inc(s_val[0], ONE)
                for bits, q in ((src_bits, 0), (dst_bits, 64)):
                    nc.vector.tensor_tensor(bits, ident[:, q:q + TS].unsqueeze(2).broadcast_to([P, TS, P]),
                                            ident[:, q + 32:q + 32 + TS].unsqueeze(2).broadcast_to([P, TS, P]),
                                            ALU.add).then_inc(s_selectors, 1)
                for q in range(4):
                    nc.vector.memset(row_mask[q * 32:(q + 1) * 32, :], (P * 127, P - 1)[q % 2]).then_inc(s_selectors, 1)
                dve.wait_ge(s_selectors, 6)
                with dve.Fori(0, S) as i:
                    window_turn0(i)
            with dve.Else():
                with dve.Fori(0, S) as i:
                    edge_turn(0, i, 12)

            for c in range(GT):
                dve.wait_ge(s_part, 16 * (c + 1))
                if c == 0:
                    ins = nc.vector.tensor_copy(acc_flat, part_flat)
                else:
                    dve.wait_ge(s_partused, c)
                    ins = nc.vector.tensor_tensor(acc_flat, acc_flat, part_flat, ALU.add)
                ins.then_inc(s_partused, 1)
            dve.wait_ge(s_partused, GT)
            dve.wait_ge(s_h0, 1)
            dve.wait_ge(s_h0d, 16)
            steps.done(nc.vector.tensor_tensor(hn[:], hn[:], acc[:, :, F:F + 1].broadcast_to([P, J, F]), ALU.mult))
            steps.done(nc.vector.tensor_tensor(sq[:], acc[:, :, 0:F], hn[:], ALU.subtract))
            steps.done(nc.vector.tensor_tensor(xn[:], xn[:], sq[:], ALU.add))
            layer_norm(1)

            dve.wait_ge(s_h1, 1)
            steps.done(nc.vector.tensor_copy(h3[:, :, 0:F], hn[:]))
            steps.done(nc.vector.tensor_tensor(sq[:], hn[:], h3[:, :, 0:F], ALU.subtract))
            steps.done(nc.vector.tensor_copy(h3[:, :, F:2 * F], sq[:]))
            steps.done(nc.vector.tensor_tensor(h3[:, :, 2 * F:3 * F], sq[:], h3[:, :, F:2 * F], ALU.subtract))
            steps.done(nc.vector.memset(h3[:, :, 3 * F:PR + 1], 1.0))
            dve.sem_inc(s_cv, chunks_of_dve)

            def stage_node(j, b):
                nc.vector.tensor_copy(hs[:, b, :], h3[:, bass.ds(j, 1), :].rearrange("p j c -> p (j c)")).then_inc(s_hs, 1)

            def node_pair(i, last=False):
                for b in range(2):
                    j = i * 2 + b
                    if not (last and b):
                        dve.wait_ge(s_hst, j + ONE)
                        stage_node(j + 1, 1 - b)
                    dve.wait_ge(s_np, j + 1)
                    dve.wait_ge(s_npc, j + ONE)
                    nc.vector.tensor_copy(nrow[:, b, :], node_ps[:, 0:3 * F])
                    dve.wait_ge(s_tst[b], i * 16 + FIRST)
                    r, n = last_chunk
                    nc.vector.tensor_copy(tb[b][:, r // 2:(r + n) // 2, 0:2 * M1],
                                          node_ps[:, 3 * F:3 * F + n * M1].rearrange("p (h c) -> p h c", c=2 * M1)).then_inc(s_xh, 1)
                    dve.wait_ge(s_xh, j + (1 + ONE))
                    nc.vector.tensor_copy(tb[b][:, :, 2 * M1:TR], nrow[:, b, 0:F].unsqueeze(1).broadcast_to([P, H, F]))
                    for q, (r, n) in list(enumerate(full_chunks))[1::2]:
                        dve.wait_ge(s_tp, i * (2 * len(full_chunks)) + (b * len(full_chunks) + q + 1))
                        nc.vector.tensor_copy(tb[b][:, r // 2:(r + n) // 2, 0:2 * M1],
                                              chunk_ps[q][:, 0:n * M1].rearrange("p (h c) -> p h c", c=2 * M1)).then_inc(s_cv, 1)

            stage_node(0, 0)
            with dve.Fori(0, J // 2 - 1) as i:
                node_pair(i)
            node_pair(J // 2 - 1, last=True)

            tail_steps = Steps(dve, s_tail)
            latest, hit, found, source = (stat[:, q, :] for q in range(4))

            def last_sums():
                sq_flat = sq[:].rearrange("p j f -> p (j f)")
                for c in range(GT):
                    dve.wait_ge(s_part, 16 * (2 * GT + c + 1))
                    if c == 0:
                        ins = nc.vector.tensor_copy(sq_flat, part_flat[:, 0:J * F])
                    else:
                        dve.wait_ge(s_partused, GT + c)
                        ins = nc.vector.tensor_tensor(sq_flat, sq_flat, part_flat[:, 0:J * F], ALU.add)
                    ins.then_inc(s_partused, 1)
                tail_steps.done(nc.vector.tensor_copy(latest, last_in[:, 0, :, 0]))
                for c in range(1, GT):
                    tail_steps.done(nc.vector.tensor_tensor(latest, latest, last_in[:, c, :, 0], ALU.max))
                for c in range(GT):
                    tail_steps.done(nc.vector.tensor_tensor(hit, latest, last_in[:, c, :, 0], ALU.is_equal))
                    if c == 0:
                        tail_steps.done(nc.vector.tensor_tensor(source, hit, last_in[:, c, :, 1], ALU.mult))
                    else:
                        tail_steps.done(nc.vector.tensor_tensor(found, hit, last_in[:, c, :, 1], ALU.mult))
                        tail_steps.done(nc.vector.tensor_tensor(source, source, found, ALU.add))

            with dve.If(unfit == 0):
                dve.sem_inc(s_val[1], VAL_START)
                chain = Steps(dve, s_edge[1])
                dve.wait_ge(s_cols[1], 1 + ONE)
                stage1(chain)
                assert chain.n == STAGE_STEPS
                for g in range(NG):
                    index1(g)
                start_turn(1, 0)
                window_turn1(0, first=True)
                with dve.Fori(1, S - 1) as i:
                    window_turn1(i)
                chain = window_turn1(S - 1, last=True)
                third_part(1, S - 1, NG - 2)
                scores1(S - 1, NG - 1, chain)
                values1(S - 1, NG - 1, chain, True)
                rest(1, S - 1, NG - 1)
                third_part(1, S - 1, NG - 1)
                dve.wait_ge(s_part, 16 * (GT + 1))
                nc.vector.tensor_copy(sq[:], part_rows[:, :, 0:F]).then_inc(s_done, 1)
                nc.vector.tensor_copy(source.unsqueeze(2), part_rows[:, :, F:M1]).then_inc(s_done, 1)
            with dve.Else():
                with dve.Fori(0, S) as i:
                    edge_turn(1, i, 37)
                last_sums()
                dve.sem_inc(s_done, 2)
            dve.wait_ge(s_done, 2)
            tail_steps = Steps(dve, s_tail2)

            tail_steps.done(nc.vector.tensor_scalar(cidx[:], source, -1.0, 0.0, ALU.add, ALU.max))
            tail_steps.done(nc.vector.tensor_scalar(hit, source, 1.0, None, ALU.min))
            dve.wait_ge(s_nst, 32)
            with dve.Fori(0, J // 7) as i:
                nc.vector.tensor_copy(cidx_s[:], cidx[:, bass.ds(i * 7, 7)]).then_inc(s_ci, 1)
                dve.wait_ge(s_cg, i * (16 * 7) + 16 * 7)
                nc.vector.tensor_copy(yhn[:, bass.ds(i * 7, 7), :], cg[:]).then_inc(s_cgc, 1)
            dve.wait_ge(s_cgc, J // 7)
            tail_steps.done(nc.vector.tensor_tensor(sq[:], sq[:], yhn, ALU.add))
            tail_steps.done(nc.vector.tensor_tensor(sq[:], sq[:], bc(hit), ALU.mult))
            tail_steps.done(nc.vector.tensor_scalar(sq[:], sq[:], 0.0, None, ALU.max))
            nc.vector.tensor_tensor(xn[:], xn[:], sq[:], ALU.add).then_inc(s_res, 1)


_INS = ['x', 'src', 'dst', 'edge_type_86', 'edge_weight', 'L1_gnn_weight', 'L1_gnn_w_comp',
        'L1_gnn_self_loop_weight', 'L1_gnn_A1_w', 'L1_gnn_A1_b', 'L1_gnn_A2_w', 'L1_gnn_A2_b',
        'L1_gnn_rel_emb']


def kernel(**inputs):
    import numpy as _np
    import concourse.bacc as _bacc
    from concourse import mybir as _mybir
    from concourse.bass_utils import run_bass_kernel_spmd as _run

    nc = _bacc.Bacc("TRN2", target_bir_lowering=False, num_devices=1)
    arrays, args = {}, []
    for name in _INS:
        a = _np.ascontiguousarray(inputs[name])
        arrays[f"in_{name}_dram"] = a
        args.append(nc.dram_tensor(f"in_{name}_dram", a.shape, _mybir.dt.from_np(a.dtype), kind="ExternalInput").ap())
    out = nc.dram_tensor("out_0_dram", inputs["x"].shape, _mybir.dt.float32, kind="ExternalOutput").ap()
    gnn_kernel(nc, *args, out)
    r = _run(nc, [arrays], core_ids=[0])
    return r.results[0]["out_0_dram"]
```
